# Optimizing a Trainium2 kernel written in Bass

```python
import numpy as np
import jax
import jax.numpy as jnp

def _softmax(x, axis=-1):
    return jax.nn.softmax(x, axis=axis)

def _gelu(x):
    return jax.nn.gelu(x, approximate=True)

def _silu(x):
    return jax.nn.silu(x)

def _sigmoid(x):
    return jax.nn.sigmoid(x)

def _layernorm(x, axis=-1, eps=1e-05):
    m = jnp.mean(x, axis=axis, keepdims=True)
    v = jnp.var(x, axis=axis, keepdims=True)
    return (x - m) / jnp.sqrt(v + eps)

def _scatter_add(tgt, idx, src, axis=0):
    return tgt.at[idx].add(src)

def _segment_sum(src, seg, n):
    return jax.ops.segment_sum(src, seg, n)
kernel_name = 'mk_vit_tower_cls_d2_tok_img768_r4_1add90'

def setup_inputs(seed: int=0):
    np.random.seed(seed)
    _w = jnp.asarray

    def _rec_inputs():
        import jax
        import jax.numpy as jnp
        _rk = jax.random.key(seed)
        x = -0.00040386 + 0.999972 * jax.random.normal(jax.random.fold_in(_rk, 1), (32, 64, 64, 3), jnp.float32)
        cls_tok = 0.02 * jax.random.normal(jax.random.fold_in(_rk, 5), (1, 1, 192), jnp.float32)
        return (x, cls_tok)
    x, cls_tok = _rec_inputs()

    def _L0_tok_setup():
        import jax, jax.numpy as jnp
        import numpy as np
        IMG = 64
        PATCH = 16
        C = 3
        D = 192
        NP_ = (IMG // PATCH) ** 2
        B = 64

        def _patchify(x):
            Bn, H, Wd, Cn = x.shape
            hp, wp = (H // PATCH, Wd // PATCH)
            x = x.reshape(Bn, hp, PATCH, wp, PATCH, Cn)
            x = x.transpose(0, 1, 3, 2, 4, 5)
            return x.reshape(Bn, hp * wp, PATCH * PATCH * Cn)
        key = jax.random.key(seed)
        k1, k2, k3 = jax.random.split(key, 3)
        x = jax.random.normal(k1, (B, IMG, IMG, C), dtype=jnp.float32)
        patch_dim = C * PATCH * PATCH
        W = jax.random.normal(k2, (patch_dim, D), dtype=jnp.float32) / np.sqrt(patch_dim)
        b = jnp.zeros((D,), dtype=jnp.float32)
        pos_emb = jax.random.normal(k3, (NP_, D), dtype=jnp.float32) * 0.02
        return {'x': x, 'W': W, 'b': b, 'pos_emb': pos_emb}
    _L0_tok_all = _L0_tok_setup()
    _L0_tok_in = {k: v for k, v in _L0_tok_all.items() if k in ('W', 'b', 'pos_emb')}
    del _L0_tok_all

    def _L0_attn_setup():
        import jax, jax.numpy as jnp
        import numpy as np
        EPS = 0.0001
        LN_EPS = 1e-05

        def _layernorm(x, g, b):
            m = jnp.mean(x, axis=-1, keepdims=True)
            v = jnp.mean(jnp.square(x - m), axis=-1, keepdims=True)
            return (x - m) * jax.lax.rsqrt(v + LN_EPS) * g + b

        def _softmax_features(x, proj, is_query):
            d = x.shape[-1]
            xn = x * d ** (-0.25)
            u = jnp.einsum('bhnd,md->bhnm', xn, proj)
            diag = 0.5 * jnp.sum(jnp.square(xn), axis=-1, keepdims=True)
            if is_query:
                stab = jnp.max(u, axis=-1, keepdims=True)
            else:
                stab = jnp.max(u, axis=(-2, -1), keepdims=True)
            ratio = proj.shape[0] ** (-0.5)
            return ratio * (jnp.exp(u - diag - stab) + EPS)
        B, N, E, H, M, F = (4, 512, 192, 12, 64, 768)
        Dh = E // H
        key = jax.random.key(seed)
        ks = jax.random.split(key, 4)
        return {'x': jax.random.normal(ks[0], (B, N, E), jnp.float32), 'proj': jax.random.normal(ks[1], (M, Dh), jnp.float32), 'ln1_g': jnp.ones((E,), jnp.float32), 'ln1_b': jnp.zeros((E,), jnp.float32), 'ln2_g': jnp.ones((E,), jnp.float32), 'ln2_b': jnp.zeros((E,), jnp.float32), 'W1': jax.random.normal(ks[2], (E, F), jnp.float32) * 0.02, 'b1': jnp.zeros((F,), jnp.float32), 'W2': jax.random.normal(ks[3], (F, E), jnp.float32) * 0.02, 'b2': jnp.zeros((E,), jnp.float32)}
    _L0_attn_all = _L0_attn_setup()
    _L0_attn_in = {k: v for k, v in _L0_attn_all.items() if k in ('proj', 'ln1_g', 'ln1_b', 'ln2_g', 'ln2_b', 'W1', 'b1', 'W2', 'b2')}
    del _L0_attn_all

    def _L0_ffn_setup():
        import jax, jax.numpy as jnp
        import numpy as np
        TOP_K = 2
        ROUTED_SCALE = 1.0

        def _swiglu_all(x, gw, uw, dw):
            g = jnp.einsum('th,eih->tei', x, gw)
            u = jnp.einsum('th,eih->tei', x, uw)
            h = jax.nn.silu(g) * u
            return jnp.einsum('tei,ehi->teh', h, dw)
        key = jax.random.key(seed)
        ks = jax.random.split(key, 8)
        B, S, H, I, E, NS = (2, 256, 192, 768, 8, 2)
        w = lambda k, shape: jax.random.normal(k, shape, jnp.float32) * 0.02
        return {'hidden_states': jax.random.normal(ks[0], (B, S, H), jnp.float32), 'gate_w': w(ks[1], (E, H)), 'shared_gate': w(ks[2], (NS, I, H)), 'shared_up': w(ks[3], (NS, I, H)), 'shared_down': w(ks[4], (NS, H, I)), 'routed_gate': w(ks[5], (E, I, H)), 'routed_up': w(ks[6], (E, I, H)), 'routed_down': w(ks[7], (E, H, I))}
    _L0_ffn_all = _L0_ffn_setup()
    _L0_ffn_in = {k: v for k, v in _L0_ffn_all.items() if k in ('gate_w', 'shared_gate', 'shared_up', 'shared_down', 'routed_gate', 'routed_up', 'routed_down')}
    del _L0_ffn_all

    def _L1_attn_setup():
        import jax, jax.numpy as jnp
        import numpy as np
        TAU = 2.0
        BN_EPS = 1e-05
        SG_ALPHA = 2.0

        @jax.custom_vjp
        def spike(u):
            return (u >= 0).astype(u.dtype)

        def _spike_fwd(u):
            return (spike(u), u)

        def _spike_bwd(u, g):
            sg = SG_ALPHA / 2.0 / (1.0 + (jnp.pi / 2.0 * SG_ALPHA * u) ** 2)
            return (g * sg,)
        spike.defvjp(_spike_fwd, _spike_bwd)

        def lif(x, v_th):
            return spike(x / TAU - v_th)

        def bn_eval(x, gamma, beta, mean, var):
            inv = gamma / jnp.sqrt(var + BN_EPS)
            return x * inv + (beta - mean * inv)
        key = jax.random.key(seed)
        ks = jax.random.split(key, 7)
        B, N, D = (2, 512, 192)
        x = jax.random.normal(ks[0], (B, N, D), dtype=jnp.float32)
        W = jax.random.normal(ks[1], (4, D, D), dtype=jnp.float32) * 0.02
        b = jnp.zeros((4, D), dtype=jnp.float32)
        bn_gamma = jax.random.uniform(ks[2], (4, D), dtype=jnp.float32, minval=0.5, maxval=1.5)
        bn_beta = jax.random.normal(ks[3], (4, D), dtype=jnp.float32) * 0.1
        bn_mean = jax.random.normal(ks[4], (4, D), dtype=jnp.float32) * 0.1
        bn_var = jax.random.uniform(ks[5], (4, D), dtype=jnp.float32, minval=0.5, maxval=1.5)
        return {'x': x, 'W': W, 'b': b, 'bn_gamma': bn_gamma, 'bn_beta': bn_beta, 'bn_mean': bn_mean, 'bn_var': bn_var}
    _L1_attn_all = _L1_attn_setup()
    _L1_attn_in = {k: v for k, v in _L1_attn_all.items() if k in ('W', 'b', 'bn_gamma', 'bn_beta', 'bn_mean', 'bn_var')}
    del _L1_attn_all

    def _L1_ffn_setup():
        import jax, jax.numpy as jnp
        import numpy as np
        D_MODEL = 192
        D_FF = 768
        N_EXPERTS = 9
        key = jax.random.key(seed)
        ks = jax.random.split(key, 7)
        scale = 0.02
        return {'x': jax.random.normal(ks[0], (2, 256, D_MODEL), jnp.float32), 'Ws': jax.random.normal(ks[1], (D_MODEL, N_EXPERTS), jnp.float32) * scale, 'bs': jnp.zeros((N_EXPERTS,), jnp.float32), 'W1': jax.random.normal(ks[2], (N_EXPERTS, D_MODEL, D_FF), jnp.float32) * scale, 'b1': jnp.zeros((N_EXPERTS, D_FF), jnp.float32), 'W2': jax.random.normal(ks[3], (N_EXPERTS, D_FF, D_MODEL), jnp.float32) * scale, 'b2': jnp.zeros((N_EXPERTS, D_MODEL), jnp.float32)}
    _L1_ffn_all = _L1_ffn_setup()
    _L1_ffn_in = {k: v for k, v in _L1_ffn_all.items() if k in ('Ws', 'bs', 'W1', 'b1', 'W2', 'b2')}
    del _L1_ffn_all
    return {'x': x, 'cls_tok': cls_tok, 'L0_tok_W': _L0_tok_in['W'], 'L0_tok_b': _L0_tok_in['b'], 'L0_tok_pos_emb': _L0_tok_in['pos_emb'], 'L0_attn_proj': _L0_attn_in['proj'], 'L0_attn_ln1_g': _L0_attn_in['ln1_g'], 'L0_attn_ln1_b': _L0_attn_in['ln1_b'], 'L0_attn_ln2_g': _L0_attn_in['ln2_g'], 'L0_attn_ln2_b': _L0_attn_in['ln2_b'], 'L0_attn_W1': _L0_attn_in['W1'], 'L0_attn_b1': _L0_attn_in['b1'], 'L0_attn_W2': _L0_attn_in['W2'], 'L0_attn_b2': _L0_attn_in['b2'], 'L0_ffn_gate_w': _L0_ffn_in['gate_w'], 'L0_ffn_shared_gate': _L0_ffn_in['shared_gate'], 'L0_ffn_shared_up': _L0_ffn_in['shared_up'], 'L0_ffn_shared_down': _L0_ffn_in['shared_down'], 'L0_ffn_routed_gate': _L0_ffn_in['routed_gate'], 'L0_ffn_routed_up': _L0_ffn_in['routed_up'], 'L0_ffn_routed_down': _L0_ffn_in['routed_down'], 'L1_attn_W': _L1_attn_in['W'], 'L1_attn_b': _L1_attn_in['b'], 'L1_attn_bn_gamma': _L1_attn_in['bn_gamma'], 'L1_attn_bn_beta': _L1_attn_in['bn_beta'], 'L1_attn_bn_mean': _L1_attn_in['bn_mean'], 'L1_attn_bn_var': _L1_attn_in['bn_var'], 'L1_ffn_Ws': _L1_ffn_in['Ws'], 'L1_ffn_bs': _L1_ffn_in['bs'], 'L1_ffn_W1': _L1_ffn_in['W1'], 'L1_ffn_b1': _L1_ffn_in['b1'], 'L1_ffn_W2': _L1_ffn_in['W2'], 'L1_ffn_b2': _L1_ffn_in['b2']}

def reference(x, cls_tok, L0_tok_W, L0_tok_b, L0_tok_pos_emb, L0_attn_proj, L0_attn_ln1_g, L0_attn_ln1_b, L0_attn_ln2_g, L0_attn_ln2_b, L0_attn_W1, L0_attn_b1, L0_attn_W2, L0_attn_b2, L0_ffn_gate_w, L0_ffn_shared_gate, L0_ffn_shared_up, L0_ffn_shared_down, L0_ffn_routed_gate, L0_ffn_routed_up, L0_ffn_routed_down, L1_attn_W, L1_attn_b, L1_attn_bn_gamma, L1_attn_bn_beta, L1_attn_bn_mean, L1_attn_bn_var, L1_ffn_Ws, L1_ffn_bs, L1_ffn_W1, L1_ffn_b1, L1_ffn_W2, L1_ffn_b2):
    import jax
    import jax.numpy as jnp

    def _L0_tok_ref(x, W, b, pos_emb):
        import jax, jax.numpy as jnp
        import numpy as np
        IMG = 64
        PATCH = 16
        C = 3
        D = 192
        NP_ = (IMG // PATCH) ** 2
        B = 64

        def _patchify(x):
            Bn, H, Wd, Cn = x.shape
            hp, wp = (H // PATCH, Wd // PATCH)
            x = x.reshape(Bn, hp, PATCH, wp, PATCH, Cn)
            x = x.transpose(0, 1, 3, 2, 4, 5)
            return x.reshape(Bn, hp * wp, PATCH * PATCH * Cn)
        patches = _patchify(x)
        proj = jnp.einsum('bnd,de->bne', patches, W) + b
        return proj + pos_emb[None, :, :]

    def _L0_attn_ref(x, proj, ln1_g, ln1_b, ln2_g, ln2_b, W1, b1, W2, b2):
        import jax, jax.numpy as jnp
        import numpy as np
        EPS = 0.0001
        LN_EPS = 1e-05

        def _layernorm(x, g, b):
            m = jnp.mean(x, axis=-1, keepdims=True)
            v = jnp.mean(jnp.square(x - m), axis=-1, keepdims=True)
            return (x - m) * jax.lax.rsqrt(v + LN_EPS) * g + b

        def _softmax_features(x, proj, is_query):
            d = x.shape[-1]
            xn = x * d ** (-0.25)
            u = jnp.einsum('bhnd,md->bhnm', xn, proj)
            diag = 0.5 * jnp.sum(jnp.square(xn), axis=-1, keepdims=True)
            if is_query:
                stab = jnp.max(u, axis=-1, keepdims=True)
            else:
                stab = jnp.max(u, axis=(-2, -1), keepdims=True)
            ratio = proj.shape[0] ** (-0.5)
            return ratio * (jnp.exp(u - diag - stab) + EPS)
        B, N, E = x.shape
        M, Dh = proj.shape
        H = E // Dh
        h = _layernorm(x, ln1_g, ln1_b)
        qkv = h.reshape(B, N, H, Dh).transpose(0, 2, 1, 3)
        q_p = _softmax_features(qkv, proj, is_query=True)
        k_p = _softmax_features(qkv, proj, is_query=False)
        k_sum = jnp.sum(k_p, axis=-2)
        d_inv = 1.0 / jnp.einsum('bhnm,bhm->bhn', q_p, k_sum)
        ctx = jnp.einsum('bhnm,bhnd->bhmd', k_p, qkv)
        attn = jnp.einsum('bhnm,bhmd,bhn->bhnd', q_p, ctx, d_inv)
        attn = attn.transpose(0, 2, 1, 3).reshape(B, N, E)
        x = x + attn
        h2 = _layernorm(x, ln2_g, ln2_b)
        h2 = jax.nn.gelu(h2 @ W1 + b1, approximate=False) @ W2 + b2
        return x + h2

    def _L0_ffn_ref(hidden_states, gate_w, shared_gate, shared_up, shared_down, routed_gate, routed_up, routed_down):
        import jax, jax.numpy as jnp
        import numpy as np
        TOP_K = 2
        ROUTED_SCALE = 1.0

        def _swiglu_all(x, gw, uw, dw):
            g = jnp.einsum('th,eih->tei', x, gw)
            u = jnp.einsum('th,eih->tei', x, uw)
            h = jax.nn.silu(g) * u
            return jnp.einsum('tei,ehi->teh', h, dw)
        B, S, H = hidden_states.shape
        T = B * S
        x = hidden_states.reshape(T, H)
        router_logits = x @ gate_w.T
        scores = jax.nn.softmax(router_logits, axis=-1)
        _, topk_idx = jax.lax.top_k(scores, TOP_K)
        topk_w = jnp.take_along_axis(scores, topk_idx, axis=-1)
        topk_w = topk_w / (topk_w.sum(axis=-1, keepdims=True) + 1e-08)
        topk_w = topk_w * ROUTED_SCALE
        E = gate_w.shape[0]
        combine = jnp.zeros((T, E), scores.dtype).at[jnp.arange(T)[:, None], topk_idx].add(topk_w)
        routed_all = _swiglu_all(x, routed_gate, routed_up, routed_down)
        routed_out = jnp.einsum('teh,te->th', routed_all, combine)
        NS = shared_gate.shape[0]
        shared_all = _swiglu_all(x, shared_gate, shared_up, shared_down)
        shared_out = shared_all.sum(axis=1) / NS
        out = (shared_out + routed_out).reshape(B, S, H)
        return out

    def _L1_attn_ref(x, W, b, bn_gamma, bn_beta, bn_mean, bn_var):
        import jax, jax.numpy as jnp
        import numpy as np
        TAU = 2.0
        BN_EPS = 1e-05
        SG_ALPHA = 2.0

        @jax.custom_vjp
        def spike(u):
            return (u >= 0).astype(u.dtype)

        def _spike_fwd(u):
            return (spike(u), u)

        def _spike_bwd(u, g):
            sg = SG_ALPHA / 2.0 / (1.0 + (jnp.pi / 2.0 * SG_ALPHA * u) ** 2)
            return (g * sg,)
        spike.defvjp(_spike_fwd, _spike_bwd)

        def lif(x, v_th):
            return spike(x / TAU - v_th)

        def bn_eval(x, gamma, beta, mean, var):
            inv = gamma / jnp.sqrt(var + BN_EPS)
            return x * inv + (beta - mean * inv)
        B, N, D = x.shape
        H = 12
        Hd = D // H
        scale = Hd ** (-0.125)

        def branch(inp, i, v_th=1.0):
            y = jnp.einsum('bnd,od->bno', inp, W[i]) + b[i]
            y = bn_eval(y, bn_gamma[i], bn_beta[i], bn_mean[i], bn_var[i])
            return lif(y, v_th)
        q = branch(x, 0)
        k = branch(x, 1)
        v = branch(x, 2)
        q = q.reshape(B, N, H, Hd).transpose(0, 2, 1, 3)
        k = k.reshape(B, N, H, Hd).transpose(0, 2, 1, 3)
        v = v.reshape(B, N, H, Hd).transpose(0, 2, 1, 3)
        attn = jnp.einsum('bhnd,bhmd->bhnm', q, k) * scale
        xa = jnp.einsum('bhnm,bhmd->bhnd', attn, v)
        xa = xa.transpose(0, 2, 1, 3).reshape(B, N, D)
        xa = lif(xa, 0.5)
        xa = branch(xa, 3)
        return xa

    def _L1_ffn_ref(x, Ws, bs, W1, b1, W2, b2):
        import jax, jax.numpy as jnp
        import numpy as np
        D_MODEL = 192
        D_FF = 768
        N_EXPERTS = 9
        B, S, d = x.shape
        xt = x.reshape(-1, d)
        route_prob = jax.nn.softmax(xt @ Ws + bs, axis=-1)
        p = jnp.max(route_prob, axis=-1)
        routes = jnp.argmax(route_prob, axis=-1)
        h = jax.nn.gelu(jnp.einsum('td,edf->tef', xt, W1) + b1, approximate=False)
        out = jnp.einsum('tef,efd->ted', h, W2) + b2
        common = out[:, 0, :]
        sel = jnp.take_along_axis(out, routes[:, None, None], axis=1)[:, 0, :]
        scaling = (p / jax.lax.stop_gradient(p))[:, None]
        pe = p[:, None]
        final = jnp.where((routes == 0)[:, None], common * scaling, pe * sel + (1.0 - pe) * common)
        return final.reshape(B, S, d)
    h = _L0_tok_ref(x, L0_tok_W, L0_tok_b, L0_tok_pos_emb)
    h = jnp.concatenate([jnp.broadcast_to(cls_tok, (h.shape[0], 1, h.shape[2])), h], axis=1)
    h = h + _L0_attn_ref(_layernorm(h, axis=-1), L0_attn_proj, L0_attn_ln1_g, L0_attn_ln1_b, L0_attn_ln2_g, L0_attn_ln2_b, L0_attn_W1, L0_attn_b1, L0_attn_W2, L0_attn_b2)
    h = h + _L0_ffn_ref(_layernorm(h, axis=-1), L0_ffn_gate_w, L0_ffn_shared_gate, L0_ffn_shared_up, L0_ffn_shared_down, L0_ffn_routed_gate, L0_ffn_routed_up, L0_ffn_routed_down)
    h = h + _L1_attn_ref(_layernorm(h, axis=-1), L1_attn_W, L1_attn_b, L1_attn_bn_gamma, L1_attn_bn_beta, L1_attn_bn_mean, L1_attn_bn_var)
    h = h + _L1_ffn_ref(_layernorm(h, axis=-1), L1_ffn_Ws, L1_ffn_bs, L1_ffn_W1, L1_ffn_b1, L1_ffn_W2, L1_ffn_b2)
    return h

_drawn_inputs = setup_inputs


def setup_inputs(seed=0):
    import zlib

    import numpy as np

    out = dict(_drawn_inputs(seed))
    spreads = {'L0_tok_b': (0.0, 0.1),
     'L0_attn_ln1_g': (1.0, 0.2),
     'L0_attn_ln1_b': (0.0, 0.1),
     'L0_attn_ln2_g': (1.0, 0.6),
     'L0_attn_ln2_b': (0.0, 0.8),
     'L0_attn_b1': (0.0, 0.619),
     'L0_attn_b2': (0.0, 0.1),
     'L1_attn_b': (0.0, 0.1),
     'L1_ffn_bs': (0.0, 2.0),
     'L1_ffn_b1': (0.0, 2.0),
     'L1_ffn_b2': (0.0, 0.8)}
    factors = {'L0_tok_pos_emb': 2.761,
     'L0_ffn_gate_w': 8.0,
     'L0_ffn_shared_gate': 8.0,
     'L0_ffn_shared_up': 8.0,
     'L0_ffn_shared_down': 8.0,
     'L0_ffn_routed_gate': 8.0,
     'L0_ffn_routed_up': 8.0,
     'L0_ffn_routed_down': 8.0,
     'L1_ffn_Ws': 35.983,
     'L1_ffn_W1': 8.0,
     'L1_ffn_W2': 3.909}
    for name, (base, spread) in spreads.items():
        noise = np.random.default_rng([zlib.crc32(name.encode()), seed]).standard_normal(out[name].shape)
        drawn = base * np.exp(spread * noise) if base else spread * noise
        out[name] = jnp.asarray(drawn.astype(out[name].dtype))
    for name, factor in factors.items():
        out[name] = (out[name] * factor).astype(out[name].dtype)
    return out
```

```python
import numpy as np
import concourse.bass as bass
from concourse import mybir
from contextlib import ExitStack

F32 = mybir.dt.float32
F32R = mybir.dt.float32r
BF16 = mybir.dt.bfloat16
I32 = mybir.dt.int32
U32 = mybir.dt.uint32
ALU = mybir.AluOpType
ACT = mybir.ActivationFunctionType
AXX = mybir.AxisListType.X

IMAGES, GRID, PATCH, CHANNELS = 32, 4, 16, 3
TOKENS = GRID * GRID + 1
D, FF, HEADS, FEATURES = 192, 768, 12, 64
HD = D // HEADS
PATCH_DIM = PATCH * PATCH * CHANNELS
EXPERTS = 8
GROUP = 7
TT = GROUP * TOKENS
NT = -(-IMAGES // GROUP)
TP = NT * TT
TX = TP + 1
HX = TX // 2
T = IMAGES * TOKENS
D0, D1 = 128, D - 128
KT = PATCH_DIM // 128
FC = FF // 128
STEPS = FC // 2
BLK = 2 * TT
BLOCKS = [(0, BLK), (BLK, BLK), (2 * BLK, T - 2 * BLK)]
NB = len(BLOCKS)
LN_EPS = 1e-5
FEATURE_EPS = 1e-4
UP, GW = 2 * FF, FC * D
MAIN_S, MAIN_G = UP + GW, FF + GW + FC
QK_CHUNKS = 3
A1 = 2 * QK_CHUNKS * 128 + 2 * D
V_COL = 2 * QK_CHUNKS * 128
SCALE1 = float(HD) ** -0.125
M_ROUTED0 = 3 * NB
M_COMMON = M_ROUTED0 + EXPERTS
M_ROUTED1 = M_COMMON + NB
M_END = M_ROUTED1 + EXPERTS
SW0 = NB * STEPS


def tiles_of(start, width):
    return [(start // TT + i, i * TT, min(TT, width - i * TT)) for i in range(-(-width // TT))]


def tower_kernel(nc, patches, tok_w, tok_b, cls_pos, proj_t, rows, router_w, router_b, sw_main, sw_rem,
                 ge_main, ge_rem, a1_main, a1_rem, a1_col, a1_row, moe_b2, out, caps=(192, 128)):
    CAP = caps
    STILES = [-(-c // 128) for c in CAP]
    ST = [c // n for c, n in zip(CAP, STILES)]
    ctx = ExitStack()
    with ctx:
        def sem(name):
            return ctx.enter_context(nc.semaphore(name))

        SIZE = {F32: 4, F32R: 4, I32: 4, U32: 4, BF16: 2}
        place = [-(-nc.sbuf_base // 64) * 64]

        def sb(name, shape, dt=F32):
            offset = place[0]
            width = int(np.prod(shape[1:])) * SIZE[dt]
            place[0] = offset + -(-width // 32) * 32
            return nc.alloc_sbuf_tensor_at(name, shape, dt, offset=offset)

        h = sb("h", [TT, NT, D])
        x0 = sb("x0", [TT, NT, D])
        xn = sb("xn", [TT, NT, D])
        xtok = sb("xtok", [TT, NT, 4, 128], F32R)
        xt = sb("xt", [128, 4, TX], F32R)
        raw_main = sb("raw_main", [128, 2, MAIN_S])
        raw_rem = sb("raw_rem", [D1, 2, UP])
        w_high = sb("w_high", [128, 2, UP], F32R)
        w_low = sb("w_low", [128, 2, UP], F32R)
        w_rest = sb("w_rest", [128, 2, UP], F32R)
        d_high = sb("d_high", [128, 2, GW], F32R)
        d_low = sb("d_low", [128, 2, GW], F32R)
        bias1 = sb("bias1", [128, 2, FC])
        row_sb = sb("row_sb", [TT, 5, D])
        ident = sb("ident", [128, 128])
        ident_b = sb("ident_b", [128, 128], BF16)
        bmask = sb("bmask", [TT, TT])
        valid = sb("valid", [TT, NT])
        tri = sb("tri", [TT, TT], BF16)
        ones_b = sb("ones_b", [TT, TT], BF16)
        zeros_b = sb("zeros_b", [1, 512], BF16)
        slot_row = sb("slot_row", [TT, max(CAP)])
        slot_col = sb("slot_col", [128, 2, 2])
        expert_id = sb("expert_id", [TT, 10])
        stats = sb("stats", [TT, NT, 6])
        mv = sb("mv", [TT, NT, 2])
        veps = sb("veps", [TT, NT])
        std = sb("std", [TT, NT])
        rstd = sb("rstd", [TT, NT])
        rw_raw = sb("rw_raw", [128, 2, 10])
        rw_rraw = sb("rw_rraw", [D1, 2, 10])
        rw = sb("rw", [128, 2, 3, 10], F32R)
        rb = sb("rb", [TT, 10])
        logit = sb("logit", [TT, NT, 10])
        lmax = sb("lmax", [TT, NT])
        shifted = sb("shifted", [TT, NT, 10])
        lexp = sb("lexp", [TT, NT, 10])
        lsum = sb("lsum", [TT, NT])
        linv = sb("linv", [TT, NT])
        prob = sb("prob", [TT, NT, 10])
        top8 = sb("top8", [TT, NT, 8])
        idx8 = sb("idx8", [TT, NT, 8], U32)
        idxf = sb("idxf", [TT, NT, 8])
        pick1 = sb("pick1", [TT, NT, 10])
        pick2 = sb("pick2", [TT, NT, 10])
        topw = sb("topw", [TT, NT, 2])
        comb = sb("comb", [TT, NT, 10])
        maskf = sb("maskf", [TT, NT, EXPERTS])
        maskb = sb("maskb", [TT, NT, EXPERTS], BF16)
        farb = sb("farb", [TT, NT, EXPERTS], BF16)
        rank = sb("rank", [TT, NT, EXPERTS])
        wtab = sb("wtab", [TT, NT, EXPERTS, 2], F32R)
        wcur = sb("wcur", [TT, 2, NT, 2], F32R)
        slot_w = sb("slot_w", [128, 2])
        slot_row_x = sb("slot_row_x", [TT, max(CAP)])
        slot_col_x = sb("slot_col_x", [128, 2])
        most = sb("most", [TT, 1])
        over = sb("over", [TT, 8])
        rounds_f = sb("rounds_f", [TT, 2])
        rounds = sb("rounds", [TT, 2], I32)
        c0 = sb("c0", [TT, NT])
        c0p = sb("c0p", [TT, NT, 2])
        b2_sb = sb("b2_sb", [EXPERTS + 1, D])
        shared_base = place[0]

        patch_sb = sb("patch_sb", [128, KT, TP])
        tokw_sb = sb("tokw_sb", [128, KT, D])
        tokb_sb = sb("tokb_sb", [1, D])
        prow = sb("prow", [1, GROUP, TOKENS])
        clspos_sb = sb("clspos_sb", [TT, D])
        bdiag = sb("bdiag", [128, 8 * FEATURES])
        bdiag2 = sb("bdiag2", [D1, 4 * FEATURES])
        negsel = sb("negsel", [HEADS, HEADS, FEATURES])
        vaug = sb("vaug", [TT, NT, HEADS, HD + 1])
        sq = sb("sq", [TT, NT, D])
        y_t0 = sb("y_t0", [128, TP])
        y_t1 = sb("y_t1", [D1, TP])
        md = sb("md", [TT, 2, NT, HEADS])
        mx_t = sb("mx_t", [HEADS, TP])
        dg_t = sb("dg_t", [HEADS, TP])
        stab = sb("stab", [HEADS, NT * GROUP])
        bq = sb("bq", [HEADS, TP])
        bk = sb("bk", [HEADS, TP])
        qkf = sb("qkf", [128, 2, 2, TP])
        am = sb("am", [TT, 2, 2, NT, TT])
        ctx_sb = sb("ctx_sb", [TT, NT, HEADS, HD + 1])
        rden = sb("rden", [TT, NT, HEADS])
        top_a = place[0]

        place[0] = shared_base
        xg = sb("xg", [128, 4, max(CAP)], F32R)
        act_out = sb("act_out", [128, 2, 2 * BLK])
        prod = sb("prod", [128, 2 * BLK])
        h_high = sb("h_high", [128, 2, FC, BLK], F32R)
        h_lowp = sb("h_lowp", [128, 2, FC, BLK], F32R)
        rank_all = sb("rank_all", [128, EXPERTS, TX])
        gat = sb("gat", [TT, 2, NT, max(CAP)], F32R)
        sca = sb("sca", [128, 2, TX], F32R)
        y_s = sb("y_s", [128, 2, D])
        y_h = sb("y_h", [128, 2, D], F32R)
        y_l = sb("y_l", [128, 2, D], F32R)
        rank_t = sb("rank_t", [EXPERTS, TX], F32R)
        comb_t = sb("comb_t", [EXPERTS + 1, TP])
        pick_row = sb("pick_row", [EXPERTS, EXPERTS, 128], F32R)
        top_b = place[0]

        place[0] = shared_base
        a_raw = sb("a_raw", [128, A1])
        a_rraw = sb("a_rraw", [D1, A1])
        a_high = sb("a_high", [128, A1], F32R)
        a_low = sb("a_low", [128, A1], F32R)
        a_rest = sb("a_rest", [128, A1], F32R)
        col_raw = sb("col_raw", [128, 5, 2 * QK_CHUNKS])
        col_ve = sb("col_ve", [128, 2 * QK_CHUNKS])
        col_std = sb("col_std", [128, 2 * QK_CHUNKS])
        col_is = sb("col_is", [128, 2 * QK_CHUNKS])
        col_inv = sb("col_inv", [128, 2 * QK_CHUNKS])
        col_mi = sb("col_mi", [128, 2 * QK_CHUNKS])
        col_shift = sb("col_shift", [128, 2 * QK_CHUNKS])
        row_raw = sb("row_raw", [TT, 2, 5, D])
        row_ve = sb("row_ve", [TT, 2, D])
        row_std = sb("row_std", [TT, 2, D])
        row_is = sb("row_is", [TT, 2, D])
        row_inv = sb("row_inv", [TT, 2, D])
        row_mi = sb("row_mi", [TT, 2, D])
        row_shift = sb("row_shift", [TT, 2, D])
        ymid = sb("ymid", [128, 2, HX])
        qk_spk = sb("qk_spk", [128, 2, QK_CHUNKS, TX], BF16)
        bt1 = sb("bt1", [TT, NT, D])
        bt2 = sb("bt2", [TT, NT, D])
        v_spk = sb("v_spk", [TT, NT, D], BF16)
        am1 = sb("am1", [TT, 4, QK_CHUNKS, TT], BF16)
        xs = sb("xs", [TT, NT, 2, 128])
        top_c = place[0]
        assert max(top_a, top_b, top_c) <= nc.sbuf_usable_end, (top_a, top_b, top_c, nc.sbuf_usable_end)

        PS = ctx.enter_context(nc.psum_tensor("PS", [128, 8, 512], F32))
        YB = 7
        GATE, UPB = (3, 5), (4, 6)

        def acc(t):
            return PS[0:TT, t // 2, (t % 2) * D:(t % 2 + 1) * D]

        def cols(t):
            return slice(t * TT, (t + 1) * TT)

        def buf_of(n):
            return n % 2

        def blocks_done(n):
            return 3 * (n + 1) if n < 3 else n + 7 if n < 11 else 20 if n == 11 else n + 9

        def chunk2(ap, n):
            return ap.rearrange("p (c n) -> p c n", n=n)

        patch_in = [sem(f"patch_in{i}") for i in range(KT)]
        tok_in = sem("tok_in"); clspos_in = sem("clspos_in"); rows_in = sem("rows_in")
        proj_in = sem("proj_in"); router_in = sem("router_in"); b2_in = sem("b2_in")
        raw_in = [sem("raw_in0"), sem("raw_in1")]; a1_in = sem("a1_in"); a1bn_in = sem("a1bn_in")
        const = sem("const")
        vec = sem("vec"); pool_step = sem("pool_step")
        embedded = sem("embedded"); var_ready = sem("var_ready"); std_ready = sem("std_ready")
        y_ready = sem("y_ready"); vaug_ready = sem("vaug_ready"); yt_done = sem("yt_done"); yt_ready = sem("yt_ready")
        u_done = sem("u_done"); u_max = sem("u_max"); diag_ready = sem("diag_ready"); mdt_done = sem("mdt_done")
        bias_ready = sem("bias_ready"); feat_done = sem("feat_done"); exp_done = sem("exp_done")
        eps_done = sem("eps_done"); a_done = sem("a_done"); mask_done = sem("mask_done"); av_done = sem("av_done")
        ctx_ready = sem("ctx_ready")
        tok_split = sem("tok_split"); xt_done = sem("xt_done"); xt_act = sem("xt_act"); xt_vec = sem("xt_vec")
        hi_up = sem("hi_up"); hi_dn = sem("hi_dn"); lo_up = sem("lo_up"); lo_dn = sem("lo_dn"); rem_lo = sem("rem_lo")
        gu_done = sem("gu_done"); act_done = sem("act_done"); up_read = sem("up_read"); high_done = sem("high_done")
        low_done = sem("low_done"); down_done = sem("down_done"); acc_read = sem("acc_read")
        rw_high = sem("rw_high"); rw_ready = sem("rw_ready")
        logit_done = sem("logit_done"); shift_ready = sem("shift_ready"); lexp_ready = sem("lexp_ready")
        mask_ready = sem("mask_ready"); rank_done = sem("rank_done"); rank_read = sem("rank_read")
        all_done = sem("all_done"); all_read = sem("all_read"); comb_done = sem("comb_done"); comb_read = sem("comb_read")
        gat_ready = sem("gat_ready"); pick_ready = sem("pick_ready"); wt_ready = sem("wt_ready"); gathered = sem("gathered"); xg_ready = sem("xg_ready")
        y_read = sem("y_read"); slotw = sem("slotw"); y_scaled = sem("y_scaled"); y_high = sem("y_high")
        y_split = sem("y_split"); sca_ready = sem("sca_ready"); scattered = sem("scattered")
        a_hi = sem("a_hi"); a_lo = sem("a_lo"); a_lor = sem("a_lor"); bn_var = sem("bn_var"); bn_std = sem("bn_std")
        qk_done = sem("qk_done"); qk_mid = sem("qk_mid"); qk_spiked = sem("qk_spiked")
        v_done = sem("v_done"); v_ready = sem("v_ready"); s_done = sem("s_done"); s_masked = sem("s_masked")
        xa_done = sem("xa_done"); xs_ready = sem("xs_ready"); xst_done = sem("xst_done"); xst_ready = sem("xst_ready")
        rounds_ready = sem("rounds_ready"); mixed = sem("mixed")
        further = [{n: sem(f"further{r}_{n}") for n in (
            "loaded", "high", "low", "rest", "slots", "table", "gathered", "tokens", "products", "activated",
            "gated", "hidden_high", "hidden", "down", "weights", "outputs", "outputs_high", "outputs_split",
            "scattered")} for r in range(2)]
        o_done = sem("o_done"); y_out = sem("y_out"); stored = sem("stored")

        class Chain:
            def __init__(self, eng, steps):
                self.eng, self.steps, self.n = eng, steps, 0

            def mark(self, ins):
                ins.then_inc(self.steps, 1)
                self.n += 1

            def link(self, ins):
                self.mark(ins)
                self.eng.wait_ge(self.steps, self.n)

            def settle(self):
                self.eng.wait_ge(self.steps, self.n)

        def further_rounds(eng, r, unit, begin=None):
            eng.wait_ge(rounds_ready, r + 1)
            n = eng.value_load(rounds[0:1, r:r + 1], min_val=0, max_val=-(-T // CAP[r]) - 1)
            with eng.If(n):
                with eng.Fori(0, n) as q:
                    if begin is not None:
                        begin(q)
                    with eng.Fori(0, EXPERTS) as k:
                        unit(r, q, k)

        block = ctx.enter_context(nc.Block())

        @block.sync
        def _(sp):
            sp.dma_start(tokw_sb[:, :, :], tok_w).then_inc(tok_in, 16)
            for kt in range(KT):
                sp.dma_start(patch_sb[:, kt, :], patches[:, kt, :]).then_inc(patch_in[kt], 16)

            def load(n, b, main, rem, width, rem_width):
                sp.dma_start(raw_main[:, b, 0:width], main).then_inc(raw_in[b], 16)
                sp.dma_start(raw_rem[:, b, 0:rem_width], rem).then_inc(raw_in[b], 16)

            def release(n):
                sp.wait_ge(lo_dn, n + 1)
                sp.wait_ge(rem_lo, n + 1)

            def one(a, i):
                return a[bass.ds(i, 1), :, :].rearrange("e p n -> p (e n)")

            load(0, 0, one(ge_main, 0), one(ge_rem, 0), MAIN_G, FF)
            load(1, 1, one(sw_main, 0), one(sw_rem, 0), MAIN_S, UP)
            release(0)
            load(2, 0, one(sw_main, 1), one(sw_rem, 1), MAIN_S, UP)
            with sp.Fori(0, EXPERTS // 2) as p:
                for b in range(2):
                    k = 2 * p + b
                    release(1 + k)
                    load(3 + k, 1 - b, one(sw_main, 2 + k), one(sw_rem, 2 + k), MAIN_S, UP)
            release(9)
            load(11, 1, one(ge_main, 1), one(ge_rem, 1), MAIN_G, FF)

            def further_load(r, q, k):
                i = q * EXPERTS + k
                x = further[r]
                main, rem, first, width = ((sw_main, sw_rem, 2, UP), (ge_main, ge_rem, 2, FF))[r]
                sp.wait_ge(x["scattered"], i + 1)
                cols_ = MAIN_S if r == 0 else MAIN_G
                sp.dma_start(raw_main[:, 0, 0:cols_], one(main, first + k)).then_inc(x["loaded"], 16)
                sp.dma_start(raw_rem[:, 0, 0:width], one(rem, first + k)).then_inc(x["loaded"], 16)

            sp.wait_ge(scattered, EXPERTS)
            further_rounds(sp, 0, further_load)
            sp.wait_ge(mixed, 1)
            sp.wait_ge(acc_read, 2)
            sp.dma_start(a_raw[:, :], a1_main).then_inc(a1_in, 16)
            sp.dma_start(a_rraw[:, :], a1_rem).then_inc(a1_in, 16)
            sp.dma_start(col_raw[:, :, :], a1_col).then_inc(a1bn_in, 16)
            sp.dma_start(row_raw[:, :, :, :].rearrange("p a b d -> p (a b d)"),
                         a1_row.rearrange("a b d -> (a b d)").partition_broadcast(TT)).then_inc(a1bn_in, 16)
            with sp.Fori(0, EXPERTS // 2) as p:
                for b in range(2):
                    k = 2 * p + b
                    release(10 + k)
                    load(12 + k, b, one(ge_main, 2 + k), one(ge_rem, 2 + k), MAIN_G, FF)
            sp.wait_ge(scattered, 2 * EXPERTS)
            further_rounds(sp, 1, further_load)
            sp.wait_ge(y_out, 1)
            sp.dma_start(out[0:4 * TT, :].rearrange("(t p) d -> p t d", p=TT), h[:, 0:4, :]).then_inc(stored, 16)
            sp.dma_start(out[4 * TT:T, :], h[0:T - 4 * TT, 4, :]).then_inc(stored, 16)
            sp.wait_ge(stored, 32)

        @block.gpsimd
        def _(pool):
            c = Chain(pool, pool_step)
            g = nc.gpsimd
            g.memset(bdiag[:, :], 0.0)
            c.mark(g.memset(bdiag2[:, :], 0.0))
            g.memset(ident[:, :], 0.0)
            g.memset(bmask[:, :], 1.0)
            g.memset(valid[:, :], 1.0)
            g.memset(ones_b[:, :], 1.0)
            g.memset(zeros_b[:, :], 0.0)
            g.memset(prow[:, :, :], 1.0)
            g.memset(negsel[:, :, :], 0.0)
            g.memset(xt[:, :, TP:TX].bitcast(F32), 0.0)
            c.link(g.memset(vaug[:, :, :, :], 1.0))
            g.memset(prow[:, :, 0:1], 0.0)
            g.affine_select(out=ident[:, :], in_=ident[:, :], compare_op=ALU.not_equal, fill=1.0, base=0,
                            pattern=[[-1, 128]], channel_multiplier=1)
            same = bmask[:, :].rearrange("p (i n) -> p i n", n=TOKENS)
            g.affine_select(out=negsel[:, :, :], in_=negsel[:, :, :], compare_op=ALU.not_equal, fill=-1.0, base=0,
                            pattern=[[-1, HEADS], [0, FEATURES]], channel_multiplier=1)
            g.affine_select(out=tri[:, :], in_=ones_b[:, :], compare_op=ALU.is_ge, fill=0.0, base=-1,
                            pattern=[[1, TT]], channel_multiplier=-1)
            g.affine_select(out=valid[:, :], in_=valid[:, :], compare_op=ALU.is_ge, fill=0.0, base=T - 1,
                            pattern=[[-TT, NT]], channel_multiplier=-1)
            c.link(g.affine_select(out=same, in_=same, compare_op=ALU.is_ge, fill=0.0, base=0,
                                   pattern=[[-TOKENS, GROUP], [0, TOKENS]], channel_multiplier=1))
            g.affine_select(out=same, in_=same, compare_op=ALU.is_ge, fill=0.0, base=TOKENS - 1,
                            pattern=[[TOKENS, GROUP], [0, TOKENS]], channel_multiplier=-1)
            g.iota(slot_row[:, :], pattern=[[1, max(CAP)]], base=0, channel_multiplier=0,
                   allow_small_or_imprecise_dtypes=True)
            g.iota(expert_id[:, :], pattern=[[1, 10]], base=0, channel_multiplier=0,
                   allow_small_or_imprecise_dtypes=True)
            for r in range(2):
                g.iota(slot_col[:, r, :], pattern=[[ST[r], 2]], base=0, channel_multiplier=1,
                       allow_small_or_imprecise_dtypes=True)
            g.tensor_copy(ident_b[:, :], ident[:, :]).then_inc(const, 1)

            def low_parts(n, b, up_width):
                pool.wait_ge(hi_up, n + 1)
                g.tensor_tensor(w_low[:, b, 0:up_width], raw_main[:, b, 0:up_width],
                                w_high[:, b, 0:up_width].bitcast(F32), ALU.subtract).then_inc(lo_up, 1)
                pool.wait_ge(hi_dn, n + 1)
                g.tensor_tensor(d_low[:, b, :], raw_main[:, b, up_width:up_width + GW],
                                d_high[:, b, :].bitcast(F32), ALU.subtract).then_inc(lo_dn, 1)

            def make_selector(stage):
                pool.wait_ge(tok_split, stage)
                c.link(g.memset(pick_row[:, :, :].bitcast(F32), 0.0))
                g.affine_select(out=pick_row[:, :, :], in_=pick_row[:, :, :].bitcast(F32),
                                compare_op=ALU.not_equal, fill=1.0, base=0,
                                pattern=[[-1, EXPERTS], [0, 128]], channel_multiplier=1).then_inc(pick_ready, 1)

            def further_low(r, q, k):
                i = q * EXPERTS + k
                x, width = further[r], (UP, FF)[r]
                pool.wait_ge(x["high"], i + 1)
                g.tensor_tensor(w_low[:, 0, 0:width], raw_main[:, 0, 0:width], w_high[:, 0, 0:width].bitcast(F32),
                                ALU.subtract)
                g.tensor_tensor(d_low[:, 0, :], raw_main[:, 0, width:width + GW], d_high[:, 0, :].bitcast(F32),
                                ALU.subtract).then_inc(x["low"], 1)

            low_parts(0, 0, FF)
            make_selector(1)
            low_parts(1, 1, UP)
            low_parts(2, 0, UP)
            with pool.Fori(0, EXPERTS // 2) as p:
                for b in range(2):
                    low_parts(3 + 2 * p + b, 1 - b, UP)
            low_parts(11, 1, FF)
            further_rounds(pool, 0, further_low)
            pool.wait_ge(a_hi, 1)
            g.tensor_tensor(a_low[:, :], a_raw[:, :], a_high[:, :].bitcast(F32), ALU.subtract).then_inc(a_lo, 1)
            make_selector(4)
            with pool.Fori(0, EXPERTS // 2) as p:
                for b in range(2):
                    low_parts(12 + 2 * p + b, b, FF)
            further_rounds(pool, 1, further_low)

        @block.tensor
        def _(pe):
            mm = nc.tensor.matmul

            def five(out_ap, w3, x4, start, stop):
                wh, wl, wr = w3
                xh, xhr, xl, xlr = x4
                pairs = [(wh, xh), (wh, xl), (wl, xh), (wr, xhr), (wr, xlr)]
                for i, (w, x) in enumerate(pairs):
                    last = mm(out_ap, w, x, start=start and i == 0, stop=stop and i == 4, skip_group_check=True)
                return last

            def transpose(out_ap, in_ap, parts=TT):
                return mm(out_ap, in_ap, ident[0:parts, 0:parts], start=True, stop=True, is_transpose=True,
                          skip_group_check=True)

            pe.wait_ge(const, 1)
            pe.wait_ge(tok_in, 32)
            for kt in range(KT):
                pe.wait_ge(patch_in[kt], 16)
                for t in range(NT):
                    mm(PS[0:TT, 3 + t, 0:D], patch_sb[:, kt, cols(t)], tokw_sb[:, kt, :], start=kt == 0, stop=False)
            for t in range(NT):
                mm(PS[0:TT, 3 + t, 0:D], prow[0:1, :, :].rearrange("p a b -> p (a b)"), tokb_sb[0:1, :],
                   start=False, stop=True).then_inc(embedded, 1)
            pe.wait_ge(y_ready, 1)
            for t in range(NT):
                transpose(PS[:, 3 + t, 0:TT], xn[:, t, 0:D0])
                transpose(PS[0:D1, 3 + t, 128:128 + TT], xn[:, t, D0:D]).then_inc(yt_done, 1)
            pe.wait_ge(yt_ready, NT)
            pe.wait_ge(proj_in, 16 * HEADS)
            for t in range(NT):
                a, b = ((3, 4), (5, 6))[t % 2]
                if t >= 2:
                    pe.wait_ge(u_max, t - 1)
                mm(PS[0:TT, a, :], y_t0[:, cols(t)], bdiag[:, :], start=True, stop=True)
                mm(PS[0:TT, b, 0:256], y_t1[:, cols(t)], bdiag2[:, :], start=True, stop=True).then_inc(u_done, 1)
            pe.wait_ge(u_max, NT)
            pe.wait_ge(diag_ready, 1)
            for t in range(NT):
                for w in range(2):
                    bank, at = ((7, 0)[w], t * TT) if t < 4 else (1, w * 128)
                    last = transpose(PS[0:HEADS, bank, at:at + TT], md[:, w, t, :])
            last.then_inc(mdt_done, 1)
            pe.wait_ge(bias_ready, 1)
            pe.wait_ge(vaug_ready, 1)

            def features(c):
                for w, bias in ((0, bq), (1, bk)):
                    for half, (lo, hi) in enumerate(((0, HX), (HX, TP))):
                        i = 2 * w + half
                        if c:
                            pe.wait_ge(exp_done, 4 * (c - 1) + i + 1)
                        o = PS[:, 3 + i, 0:hi - lo]
                        if c < 4:
                            mm(o, bdiag[:, c * 128:(c + 1) * 128], y_t0[:, lo:hi], start=True, stop=False)
                        else:
                            mm(o, bdiag2[:, (c - 4) * 128:(c - 3) * 128], y_t1[:, lo:hi], start=True, stop=False)
                        mm(o, negsel[:, 2 * c:2 * c + 2, :].rearrange("h a f -> h (a f)"), bias[:, lo:hi],
                           start=False, stop=True).then_inc(feat_done, 1)

            def products(c, tiles):
                for j in range(2):
                    rows_ = slice(64 * j, 64 * j + 64)
                    for i, t in enumerate(tiles):
                        last = mm(PS[0:TT, j, i * TT:(i + 1) * TT], qkf[rows_, c % 2, 1, cols(t)],
                                  qkf[rows_, c % 2, 0, cols(t)], start=True, stop=True)
                last.then_inc(a_done, 1)

            features(0)
            for c in range(HEADS // 2):
                pe.wait_ge(eps_done, 2 * c + 2)
                if c:
                    pe.wait_ge(mask_done, 4 * c)
                products(c, range(4))
                if c < HEADS // 2 - 1:
                    features(c + 1)
                pe.wait_ge(mask_done, 4 * c + 2)
                products(c, [4])
                pe.wait_ge(mask_done, 4 * c + 4)
                if c >= 2:
                    pe.wait_ge(ctx_ready, c - 1)
                bank = (2, 7)[c % 2]
                for t in range(NT):
                    for j in range(2):
                        at = (2 * t + j) * (HD + 1)
                        last = mm(PS[0:TT, bank, at:at + HD + 1], am[:, c % 2, j, t, :], vaug[:, t, 2 * c + j, :],
                                  start=True, stop=True)
                last.then_inc(av_done, 1)

            def to_features(stage):
                pe.wait_ge(tok_split, stage + 1)
                for t in range(NT):
                    for j in range(4):
                        last = transpose(PS[:, 3 + t, j * TT:(j + 1) * TT], xtok[:, t, j, :].bitcast(F32))
                    last.then_inc(xt_done, 1)

            def await_xt(stage):
                pe.wait_ge(xt_act, 3 * (stage + 1))
                pe.wait_ge(xt_vec, 2 * (stage + 1))

            def clear_acc():
                for i in range(3):
                    mm(PS[0:TT, i, :], zeros_b[:, 0:TT], zeros_b[:, :], start=True, stop=True, skip_group_check=True)

            def w_slices(b, at):
                return [w[:, b, at:at + 128] for w in (w_high, w_low, w_rest)]

            def step(b, s, pair, x4, width, gated, done=gu_done):
                for bank, base in ((GATE[pair], 0), (UPB[pair], FF)) if gated else ((GATE[pair], 0),):
                    for i in range(2):
                        last = five(PS[:, bank, i * width:(i + 1) * width], w_slices(b, base + (2 * s + i) * 128),
                                    x4, True, True)
                last.then_inc(done, 1)

            def down(out_ap, b, hb, at, n, start):
                for i in range(FC):
                    for j, (hp, dp) in enumerate(((h_high, d_high), (h_high, d_low), (h_lowp, d_high))):
                        last = mm(out_ap, hp[:, hb, i, at:at + n], dp[:, b, i * D:(i + 1) * D],
                                  start=start and i == 0 and j == 0, stop=i == FC - 1 and j == 2,
                                  skip_group_check=True)
                return last

            def dense_down(m, n):
                pe.wait_ge(hi_dn, n + 1)
                pe.wait_ge(lo_dn, n + 1)
                pe.wait_ge(low_done, 3 * (m + 1))
                start, width = BLOCKS[m % NB if m < M_ROUTED0 else m - M_COMMON]
                for t, at, k in tiles_of(start, width):
                    last = down(acc(t)[0:k], buf_of(n), m % 2, at, k, False)
                last.then_inc(down_done, 1)

            def dense(m, n, gated, before, extra):
                start, width = BLOCKS[m % NB if m < M_ROUTED0 else m - M_COMMON]
                x4 = [xt[:, j, start:start + width] for j in range(4)]
                for s in range(STEPS):
                    g = 3 * m + s
                    if s == 0:
                        pe.wait_ge(hi_up, n + 1)
                        pe.wait_ge(lo_up, n + 1)
                        pe.wait_ge(rem_lo, n + 1)
                    if g >= 2:
                        pe.wait_ge(act_done, g - 1)
                        if g - 1 > SW0:
                            pe.wait_ge(up_read, min(g - 1, 3 * M_COMMON) - SW0)
                    step(buf_of(n), s, g % 2, x4, width, gated)
                    if s == 0 and before is not None:
                        dense_down(*before)
                    extra(m, s)

            def nothing(m, s):
                pass

            to_features(0)
            clear_acc()
            await_xt(0)
            for m in range(NB):
                dense(m, 0, False, (m - 1, 0) if m else None, nothing)
            dense_down(NB - 1, 0)

            def router(r):
                pe.wait_ge(rw_ready, 1)
                for t in range(NT):
                    last = router_tile(r, t)
                last.then_inc(logit_done, 1)

            def router_tile(r, t):
                o = PS[0:TT, YB, t * 10:(t + 1) * 10]
                xh, xhr, xl, xlr = [xt[:, j, cols(t)] for j in range(4)]
                pairs = [(xh, 0), (xl, 0), (xh, 1), (xhr, 2), (xlr, 2)]
                for i, (x, w) in enumerate(pairs):
                    last = mm(o, x, rw[:, r, w, :], start=i == 0, stop=i == 4, skip_group_check=True)
                return last

            def ranks(r):
                def by_expert(t, at):
                    o = PS[0:EXPERTS, YB, at:at + TT]
                    mm(o, farb[:, t, :], ident_b[0:TT, 0:TT], start=True, stop=False, skip_group_check=True)
                    for i in range(t):
                        mm(o, maskb[:, i, :], ones_b[:, :], start=False, stop=False, skip_group_check=True)
                    return mm(o, maskb[:, t, :], tri[:, :], start=False, stop=True, skip_group_check=True)

                pe.wait_ge(mask_ready, r + 1)
                for t in range(4):
                    last = by_expert(t, t * TT)
                last.then_inc(rank_done, 1)
                pe.wait_ge(rank_read, 2 * r + 1)
                by_expert(4, 0)
                for t in range(NT):
                    o = PS[0:TT, YB, 128 + t * EXPERTS:128 + (t + 1) * EXPERTS]
                    mm(o, ident_b[0:TT, 0:TT], farb[:, t, :], start=True, stop=False, skip_group_check=True)
                    for i in range(t):
                        mm(o, ones_b[:, :], maskb[:, i, :], start=False, stop=False, skip_group_check=True)
                    mm(o, tri[:, :], maskb[:, t, :], start=False, stop=True, skip_group_check=True)
                for t in range(NT):
                    last = mm(PS[0:TT, YB, 192:192 + EXPERTS], ones_b[:, :], maskb[:, t, :], start=t == 0,
                              stop=t == NT - 1, skip_group_check=True)
                last.then_inc(rank_done, 1)

            def spread(r, i):
                if i == 0:
                    pe.wait_ge(pick_ready, r + 1)
                    pe.wait_ge(rank_read, 2 * r + 2)
                else:
                    pe.wait_ge(all_read, 2 * EXPERTS * r + i)
                e, half = i // 2, i % 2
                mm(PS[:, YB, 0:HX], pick_row[:, e, :], rank_t[:, half * HX:(half + 1) * HX],
                   start=True, stop=True).then_inc(all_done, 1)

            def extras0(m, s):
                g = 3 * m + s - SW0
                if g == 1:
                    ranks(0)
                if 5 <= g < 13:
                    spread(0, 2 * (g - 5))
                    spread(0, 2 * (g - 5) + 1)

            def weights_by_expert():
                for t in range(4):
                    last = transpose(PS[0:EXPERTS + 1, YB, cols(t)], comb[:, t, 0:EXPERTS + 1])
                last.then_inc(comb_done, 1)
                pe.wait_ge(comb_read, 1)
                transpose(PS[0:EXPERTS + 1, YB, 0:TT], comb[:, 4, 0:EXPERTS + 1]).then_inc(comb_done, 1)
                pe.wait_ge(comb_read, 2)

            def extras1(m, s):
                g = 3 * (m - M_COMMON) + s
                if g == 1:
                    ranks(1)
                    pe.wait_ge(rank_read, 4)
                    weights_by_expert()
                if g >= 1:
                    spread(1, 2 * (g - 1))
                    spread(1, 2 * (g - 1) + 1)

            def gather(r, k, b, g):
                cap = CAP[r]
                pe.wait_ge(gat_ready, EXPERTS * r + k + 1)
                pe.wait_ge(act_done, g)
                if r == 0:
                    pe.wait_ge(up_read, g - SW0)
                for j in range(4):
                    bank, at = (GATE[1], UPB[1])[j // 2], (j % 2) * cap
                    for t in range(NT):
                        last = mm(PS[:, bank, at:at + cap], xtok[:, t, j, :], gat[:, b, t, 0:cap],
                                  start=t == 0, stop=t == NT - 1, skip_group_check=True)
                last.then_inc(gathered, 1)

            def scatter(r, k, last_one=False):
                pe.wait_ge(y_split, EXPERTS * r + k + 1)
                pe.wait_ge(sca_ready, EXPERTS * r + k + 1)
                st = ST[r]
                for t in range(NT):
                    for i in range(STILES[r]):
                        for y in (y_h, y_l):
                            last = mm(acc(t), sca[0:st, i, cols(t)], y[0:st, i, :], start=False, stop=False,
                                      skip_group_check=True)
                last.then_inc(scattered, 1)

            def expert(r, k, b, first, final):
                n0, m0 = ((3, M_ROUTED0), (12, M_ROUTED1))[r]
                n, m = n0 + k, m0 + k
                g = 3 * m
                wb = (n0 + b) % 2
                cap, st, gated = CAP[r], ST[r], r == 0
                x4 = [xg[:, j, 0:cap] for j in range(4)]
                pe.wait_ge(hi_up, n + 1)
                pe.wait_ge(lo_up, n + 1)
                pe.wait_ge(rem_lo, n + 1)
                pe.wait_ge(xg_ready, EXPERTS * r + k + 1)
                pe.wait_ge(act_done, g)
                if gated:
                    pe.wait_ge(up_read, g - SW0)
                step(wb, 0, 0, x4, cap, gated)
                if not first:
                    scatter(r, k - 1)
                step(wb, 1, 1, x4, cap, gated)
                pe.wait_ge(act_done, g + 1)
                if gated:
                    pe.wait_ge(up_read, g + 1 - SW0)
                step(wb, 2, 0, x4, cap, gated)
                if not final:
                    gather(r, k + 1, 1 - b, g + 2)
                pe.wait_ge(hi_dn, n + 1)
                pe.wait_ge(lo_dn, n + 1)
                pe.wait_ge(low_done, g + 3)
                if not first:
                    pe.wait_ge(y_read, EXPERTS * r + k)
                elif r == 1:
                    pe.wait_ge(y_read, EXPERTS)
                for i in range(STILES[r]):
                    for t in range(NT):
                        mm(PS[0:st, YB, 2 * D + 2 * i:2 * D + 2 * i + 2], gat[:, b, t, i * st:(i + 1) * st],
                           wcur[:, b, t, :], start=t == 0, stop=t == NT - 1, skip_group_check=True)
                for i in range(STILES[r]):
                    last = down(PS[0:st, YB, i * D:(i + 1) * D], wb, m % 2 if isinstance(m, int) else (m0 + b) % 2,
                                i * st, st, True)
                last.then_inc(down_done, 1)

            def experts(r):
                for b in range(2):
                    expert(r, b, b, b == 0, False)
                with pe.Fori(1, EXPERTS // 2 - 1) as p:
                    for b in range(2):
                        expert(r, 2 * p + b, b, False, False)
                for b in range(2):
                    expert(r, EXPERTS - 2 + b, b, False, b == 1)
                scatter(r, EXPERTS - 1)
                mm(acc(0), zeros_b[:, 0:TT], zeros_b[:, 0:D], start=False, stop=False,
                   skip_group_check=True).then_inc(further[r]["scattered"], 1)
                further_rounds(pe, r, further_unit)
                mm(acc(0), zeros_b[:, 0:TT], zeros_b[:, 0:D], start=False, stop=True,
                   skip_group_check=True).then_inc(mixed, 1)

            def further_unit(r, q, k):
                i = q * EXPERTS + k
                x, cap, st = further[r], CAP[r], ST[r]
                pe.wait_ge(x["table"], i + 1)
                for j in range(4):
                    bank, at = (GATE[1], UPB[1])[j // 2], (j % 2) * cap
                    for t in range(NT):
                        last = mm(PS[:, bank, at:at + cap], xtok[:, t, j, :], gat[:, 0, t, 0:cap],
                                  start=t == 0, stop=t == NT - 1, skip_group_check=True)
                last.then_inc(x["gathered"], 1)
                pe.wait_ge(x["tokens"], i + 1)
                pe.wait_ge(x["low"], i + 1)
                pe.wait_ge(x["rest"], i + 1)
                x4 = [xg[:, j, 0:cap] for j in range(4)]
                for s in range(STEPS):
                    step(0, s, 0, x4, cap, r == 0, x["products"])
                    pe.wait_ge(x["hidden"], STEPS * i + s + 1)
                for n in range(STILES[r]):
                    for t in range(NT):
                        mm(PS[0:st, YB, 2 * D + 2 * n:2 * D + 2 * n + 2], gat[:, 0, t, n * st:(n + 1) * st],
                           wcur[:, 0, t, :], start=t == 0, stop=t == NT - 1, skip_group_check=True)
                for n in range(STILES[r]):
                    last = down(PS[0:st, YB, n * D:(n + 1) * D], 0, 0, n * st, st, True)
                last.then_inc(x["down"], 1)
                pe.wait_ge(x["outputs_split"], i + 1)
                for t in range(NT):
                    for n in range(STILES[r]):
                        for y in (y_h, y_l):
                            last = mm(acc(t), sca[0:st, n, cols(t)], y[0:st, n, :], start=False, stop=False,
                                      skip_group_check=True)
                last.then_inc(x["scattered"], 1)

            to_features(1)
            pe.wait_ge(acc_read, 1)
            clear_acc()
            await_xt(1)
            router(0)
            for m in range(NB, M_ROUTED0):
                n = m // NB
                dense(m, n, True, (m - 1, (m - 1) // NB) if m > NB else None, extras0)
            gather(0, 0, 0, 3 * M_ROUTED0 - 1)
            dense_down(M_ROUTED0 - 1, 2)
            pe.wait_ge(all_read, 16)
            experts(0)

            to_features(2)
            await_xt(2)
            pe.wait_ge(a_lo, 1)
            pe.wait_ge(a_lor, 1)

            def a_slices(at, n):
                return [w[:, at:at + n] for w in (a_high, a_low, a_rest)]

            i = 0
            for w in range(2):
                for c in range(QK_CHUNKS):
                    for half in range(2):
                        if i >= 4:
                            pe.wait_ge(qk_mid, i - 3)
                        five(PS[:, 3 + i % 4, 0:HX], a_slices((w * QK_CHUNKS + c) * 128, 128),
                             [xt[:, j, half * HX:(half + 1) * HX] for j in range(4)], True, True).then_inc(qk_done, 1)
                        i += 1
            pe.wait_ge(acc_read, 2)
            for t in range(NT):
                xh, xhr, xl, xlr = [xt[:, j, cols(t)] for j in range(4)]
                wh, wl, wr = a_slices(V_COL, D)
                for i, (x, w) in enumerate([(xh, wh), (xl, wh), (xh, wl), (xhr, wr), (xlr, wr)]):
                    last = mm(acc(t), x, w, start=i == 0, stop=i == 4, skip_group_check=True)
            last.then_inc(v_done, 1)
            pe.wait_ge(qk_spiked, 12)
            pe.wait_ge(v_ready, 1)
            for t in range(NT):
                if t:
                    pe.wait_ge(s_masked, 4 * t)
                for c in range(QK_CHUNKS):
                    for j in range(4):
                        last = mm(PS[0:TT, 3 + j, c * TT:(c + 1) * TT], qk_spk[32 * j:32 * j + 32, 1, c, cols(t)],
                                  qk_spk[32 * j:32 * j + 32, 0, c, cols(t)], start=True, stop=True,
                                  skip_group_check=True)
                last.then_inc(s_done, 1)
                pe.wait_ge(s_masked, 4 * t + 4)
                for head in range(HEADS):
                    last = mm(acc(t)[:, head * HD:(head + 1) * HD], am1[:, head % 4, head // 4, :],
                              v_spk[:, t, head * HD:(head + 1) * HD], start=True, stop=True, skip_group_check=True)
                last.then_inc(xa_done, 1)
            pe.wait_ge(xs_ready, 1)
            for t in range(NT):
                for j in range(2):
                    last = transpose(PS[:, 3 + t, j * TT:(j + 1) * TT], xs[:, t, j, :])
                last.then_inc(xst_done, 1)
            pe.wait_ge(xst_ready, NT)
            for t in range(NT):
                wh, wl, wr = a_slices(V_COL + D, D)
                for i, (j, w) in enumerate([(0, wh), (0, wl), (1, wr)]):
                    last = mm(acc(t), xt[:, j, cols(t)], w, start=i == 0, stop=i == 2, skip_group_check=True)
            last.then_inc(o_done, 1)

            to_features(3)
            clear_acc()
            await_xt(3)
            router(1)
            for m in range(M_COMMON, M_ROUTED1):
                dense(m, 11, False, (m - 1, 11) if m > M_COMMON else None, extras1)
            gather(1, 0, 0, 3 * M_ROUTED1)
            dense_down(M_ROUTED1 - 1, 11)
            pe.wait_ge(all_read, 32)
            pe.wait_ge(acc_read, 3)
            pe.wait_ge(b2_in, 16)
            clear_acc()
            for t in range(NT):
                mm(acc(t), comb_t[:, cols(t)], b2_sb[:, :], start=False, stop=False, skip_group_check=True)
            experts(1)

        @block.scalar
        def _(act):
            s = nc.scalar
            act.dma_start(tokb_sb[:, :], tok_b).then_inc(tok_in, 16)
            for i in range(GROUP):
                act.dma_start(clspos_sb[i * TOKENS:(i + 1) * TOKENS, :], cls_pos).then_inc(clspos_in, 16)
            act.dma_start(row_sb[:, :, :].rearrange("p a d -> p (a d)"),
                          rows.rearrange("a d -> (a d)").partition_broadcast(TT)).then_inc(rows_in, 16)
            act.wait_ge(pool_step, 1)
            for head in range(HEADS):
                tile_, i = (bdiag, head) if head < 8 else (bdiag2, head - 8)
                act.dma_start(tile_[i * HD:(i + 1) * HD, i * FEATURES:(i + 1) * FEATURES],
                              proj_t).then_inc(proj_in, 16)
            act.dma_start(rw_raw[:, :, :], router_w[0:D0]).then_inc(router_in, 16)
            act.dma_start(rw_rraw[:, :, :], router_w[D0:D]).then_inc(router_in, 16)
            act.dma_start(rb[:, :], router_b.partition_broadcast(TT)).then_inc(router_in, 16)
            act.dma_start(b2_sb[:, :], moe_b2).then_inc(b2_in, 16)

            def deviation(i):
                act.wait_ge(var_ready, i + 1)
                s.activation(std[:, :], veps[:, :], ACT.Sqrt).then_inc(std_ready, 1)

            deviation(0)
            deviation(1)
            act.wait_ge(y_ready, 1)
            act.wait_ge(const, 1)
            s.activation(vaug[:, :, :, 0:HD], xn[:, :, :].rearrange("p t (h d) -> p t h d", d=HD),
                         ACT.Copy).then_inc(vaug_ready, 1)
            for t in range(NT):
                act.wait_ge(yt_done, t + 1)
                s.activation(y_t0[:, cols(t)], PS[:, 3 + t, 0:TT], ACT.Copy)
                s.activation(y_t1[:, cols(t)], PS[0:D1, 3 + t, 128:128 + TT], ACT.Copy).then_inc(yt_ready, 1)
            act.wait_ge(router_in, 48)
            s.activation(rw[:, :, 0, :], rw_raw[:, :, :], ACT.Copy)
            s.activation(rw[0:D1, :, 2, :], rw_rraw[:, :, :], ACT.Copy).then_inc(rw_high, 1)

            def high_up(n, b, fill, width, done):
                act.wait_ge(raw_in[b], 32 * (fill + 1))
                if done is not None:
                    act.wait_ge(down_done, done)
                s.activation(w_high[:, b, 0:width], raw_main[:, b, 0:width], ACT.Copy)
                if width == FF:
                    s.activation(bias1[:, b, :], raw_main[:, b, FF + GW:MAIN_G], ACT.Copy)

            def high_rest(b, width):
                s.activation(w_rest[0:D1, b, 0:width], raw_rem[:, b, 0:width], ACT.Copy).then_inc(hi_up, 1)

            def high_down(b, width):
                s.activation(d_high[:, b, :], raw_main[:, b, width:width + GW], ACT.Copy).then_inc(hi_dn, 1)

            def high_all(n, done):
                width = UP if 1 <= n <= 10 else FF
                high_up(n, n % 2, n // 2, width, done)
                high_rest(n % 2, width)
                high_down(n % 2, width)

            high_all(0, None)

            def exps(c):
                for w in range(2):
                    for half, (lo, hi) in enumerate(((0, HX), (HX, TP))):
                        i = 2 * w + half
                        act.wait_ge(feat_done, 4 * c + i + 1)
                        if c >= 2:
                            act.wait_ge(a_done, 2 * (c - 1))
                        s.activation(qkf[:, c % 2, w, lo:hi], PS[:, 3 + i, 0:hi - lo], ACT.Exp,
                                     scale=0.5).then_inc(exp_done, 1)

            exps(0)
            for c in range(HEADS // 2):
                if c < HEADS // 2 - 1:
                    exps(c + 1)
                act.wait_ge(av_done, c + 1)
                s.activation(ctx_sb[:, :, 2 * c:2 * c + 2, :],
                             PS[0:TT, (2, 7)[c % 2], 0:NT * 2 * (HD + 1)].rearrange("p (t h d) -> p t h d", t=NT, h=2),
                             ACT.Copy).then_inc(ctx_ready, 1)

            def xt_out(stage):
                for t in (0, 2, 4):
                    act.wait_ge(xt_done, NT * stage + t + 1)
                    s.activation(xt[:, :, cols(t)], chunk2(PS[:, 3 + t, 0:4 * TT], TT), ACT.Copy).then_inc(xt_act, 1)

            def hidden(m, n, b, s_, pair, ring, width, gated):
                g = 3 * m + s_
                act.wait_ge(gu_done, g + 1)
                if not (isinstance(g, int) and g < 2):
                    act.wait_ge(low_done, g - 1)
                if gated:
                    s.activation(act_out[:, ring, 0:2 * width], PS[:, GATE[pair], 0:2 * width],
                                 ACT.Silu).then_inc(act_done, 1)
                    return
                act.wait_ge(hi_up, n + 1)
                for i in range(2):
                    at = slice(i * width, (i + 1) * width)
                    last = s.activation(act_out[:, ring, at], PS[:, GATE[pair], at], ACT.Gelu,
                                        bias=bias1[:, b, 2 * s_ + i:2 * s_ + i + 1])
                last.then_inc(act_done, 1)

            def spread_out(r, i):
                act.wait_ge(all_done, 2 * EXPERTS * r + i + 1)
                e, half = i // 2, i % 2
                s.activation(rank_all[:, e, half * HX:(half + 1) * HX], PS[:, YB, 0:HX], ACT.Copy).then_inc(all_read, 1)

            def gathered_out(r, k):
                act.wait_ge(gathered, EXPERTS * r + k + 1)
                cap = CAP[r]
                s.activation(xg[:, 0:2, 0:cap], chunk2(PS[:, GATE[1], 0:2 * cap], cap), ACT.Copy)
                s.activation(xg[:, 2:4, 0:cap], chunk2(PS[:, UPB[1], 0:2 * cap], cap), ACT.Copy).then_inc(xg_ready, 1)

            def dense(m, n, gated, extra):
                width = BLOCKS[m % NB if m < M_ROUTED0 else m - M_COMMON][1]
                for i in range(STEPS):
                    g = 3 * m + i
                    hidden(m, n, n % 2, i, g % 2, g % 2, width, gated)
                    if i == 0 and m % NB == (0 if m < M_ROUTED0 else M_COMMON % NB):
                        high_all(n + 1, None if n == 0 else blocks_done(n - 1))
                    extra(m, i)

            def nothing(m, i):
                pass

            def extras0(m, i):
                g = 3 * m + i - SW0
                if 5 <= g < 13:
                    spread_out(0, 2 * (g - 5))
                    spread_out(0, 2 * (g - 5) + 1)

            def extras1(m, i):
                g = 3 * (m - M_COMMON) + i
                if g >= 1:
                    spread_out(1, 2 * (g - 1))
                    spread_out(1, 2 * (g - 1) + 1)

            def expert(r, k, p, b, final):
                n0, m0 = ((3, M_ROUTED0), (12, M_ROUTED1))[r]
                n, m = n0 + k, m0 + k
                wb, gated, cap = (n0 + b) % 2, r == 0, CAP[r]
                ring = (m0 + b) % 2
                more = not final or r == 0
                width = UP if r == 0 and not final else FF
                nb = 1 - wb
                hidden(m, n, wb, 0, 0, ring, cap, gated)
                if more:
                    high_up(n + 1, nb, (n0 + 1 + b) // 2 + p, width, m)
                hidden(m, n, wb, 1, 1, 1 - ring, cap, gated)
                if more:
                    high_rest(nb, width)
                hidden(m, n, wb, 2, 0, ring, cap, gated)
                if not final:
                    gathered_out(r, k + 1)
                if more:
                    high_down(nb, width)

            def experts(r):
                for b in range(2):
                    expert(r, b, 0, b, False)
                with act.Fori(1, EXPERTS // 2 - 1) as p:
                    for b in range(2):
                        expert(r, 2 * p + b, p, b, False)
                for b in range(2):
                    expert(r, EXPERTS - 2 + b, EXPERTS // 2 - 1, b, b == 1)
                further_rounds(act, r, further_unit)

            def further_unit(r, q, k):
                i = q * EXPERTS + k
                x, cap, width = further[r], CAP[r], (UP, FF)[r]
                act.wait_ge(x["loaded"], 32 * i + 32)
                s.activation(w_high[:, 0, 0:width], raw_main[:, 0, 0:width], ACT.Copy)
                if r:
                    s.activation(bias1[:, 0, :], raw_main[:, 0, FF + GW:MAIN_G], ACT.Copy)
                s.activation(w_rest[0:D1, 0, 0:width], raw_rem[:, 0, 0:width], ACT.Copy)
                s.activation(d_high[:, 0, :], raw_main[:, 0, width:width + GW], ACT.Copy).then_inc(x["high"], 1)
                act.wait_ge(x["high"], i + 1)
                act.wait_ge(x["gathered"], i + 1)
                s.activation(xg[:, 0:2, 0:cap], chunk2(PS[:, GATE[1], 0:2 * cap], cap), ACT.Copy)
                s.activation(xg[:, 2:4, 0:cap], chunk2(PS[:, UPB[1], 0:2 * cap], cap), ACT.Copy).then_inc(x["tokens"], 1)
                for n in range(STEPS):
                    act.wait_ge(x["products"], STEPS * i + n + 1)
                    for c in range(2):
                        at = slice(c * cap, (c + 1) * cap)
                        last = s.activation(act_out[:, 0, at], PS[:, GATE[0], at], ACT.Gelu,
                                            bias=bias1[:, 0, 2 * n + c:2 * n + c + 1]) if r else \
                            s.activation(act_out[:, 0, at], PS[:, GATE[0], at], ACT.Silu)
                    last.then_inc(x["activated"], 1)

            def router(r):
                act.wait_ge(shift_ready, r + 1)
                s.activation(lexp[:, :, :], shifted[:, :, :], ACT.Exp).then_inc(lexp_ready, 1)

            deviation(2)
            xt_out(0)
            for m in range(NB):
                dense(m, 0, False, nothing)
            deviation(3)
            xt_out(1)
            router(0)
            for m in range(NB, M_ROUTED0):
                dense(m, m // NB, True, extras0)
            gathered_out(0, 0)
            experts(0)
            deviation(4)
            act.wait_ge(bn_var, 1)
            s.activation(col_std[:, :], col_ve[:, :], ACT.Sqrt)
            s.activation(row_std[:, :, :], row_ve[:, :, :], ACT.Sqrt).then_inc(bn_std, 1)
            act.wait_ge(a1_in, 32)
            s.activation(a_high[:, :], a_raw[:, :], ACT.Copy)
            s.activation(a_rest[0:D1, :], a_rraw[:, :], ACT.Copy).then_inc(a_hi, 1)
            xt_out(2)
            for t in range(NT):
                act.wait_ge(xst_done, t + 1)
                s.activation(xt[:, 0:2, cols(t)], chunk2(PS[:, 3 + t, 0:2 * TT], TT), ACT.Copy).then_inc(xst_ready, 1)
            deviation(5)
            xt_out(3)
            router(1)
            for m in range(M_COMMON, M_ROUTED1):
                dense(m, 11, False, extras1)
            gathered_out(1, 0)
            experts(1)

        @block.vector
        def _(dve):
            v = nc.vector
            c = Chain(dve, vec)

            def over_tiles(row):
                return row.to_broadcast([TT, NT, D])

            def layernorm(src, dst, i):
                for t in range(NT):
                    c.mark(v.bn_stats(stats[:, t, :], src[:, t, :]))
                c.settle()
                for t in range(NT):
                    c.mark(v.bn_aggr(mv[:, t, :], stats[:, t, :]))
                c.settle()
                v.tensor_scalar(veps[:, :], mv[:, :, 1], LN_EPS, None, ALU.add).then_inc(var_ready, 1)
                dve.wait_ge(std_ready, i + 1)
                c.link(v.reciprocal(rstd[:, :], std[:, :]))
                for t in range(NT):
                    c.mark(v.tensor_scalar(dst[:, t, :], src[:, t, :], mv[:, t, 0:1], rstd[:, t:t + 1],
                                           ALU.subtract, ALU.mult))
                c.settle()

            def split_tokens():
                c.mark(v.tensor_copy(xtok[:, :, 0, :], xn[:, :, 0:D0]))
                for i in range(2):
                    c.mark(v.tensor_copy(xtok[:, :, 1, i * D1:(i + 1) * D1], xn[:, :, D0:D]))
                c.settle()
                v.tensor_tensor(xtok[:, :, 2, :], xn[:, :, 0:D0], xtok[:, :, 0, :].bitcast(F32), ALU.subtract)
                for i in range(2):
                    last = v.tensor_tensor(xtok[:, :, 3, i * D1:(i + 1) * D1], xn[:, :, D0:D],
                                           xtok[:, :, 1, i * D1:(i + 1) * D1].bitcast(F32), ALU.subtract)
                last.then_inc(tok_split, 1)

            def xt_out(stage):
                for t in (1, 3):
                    dve.wait_ge(xt_done, NT * stage + t + 1)
                    v.tensor_copy(xt[:, :, cols(t)], chunk2(PS[:, 3 + t, 0:4 * TT], TT)).then_inc(xt_vec, 1)

            def per_bank(f):
                for bank in range(3):
                    ts = slice(2 * bank, min(2 * bank + 2, NT))
                    last = f(ts, chunk2(PS[0:TT, bank, 0:(ts.stop - ts.start) * D], D))
                return last

            dve.wait_ge(clspos_in, 16 * GROUP)
            for t in range(NT):
                dve.wait_ge(embedded, t + 1)
                c.mark(v.tensor_tensor(h[:, t, :], PS[0:TT, 3 + t, 0:D], clspos_sb[:, :], ALU.add))
            c.settle()
            layernorm(h, x0, 0)
            layernorm(x0, xn, 1)
            dve.wait_ge(rows_in, 16)
            c.link(v.tensor_tensor(xn[:, :, :], xn[:, :, :], over_tiles(row_sb[:, 0:1, :]), ALU.mult))
            v.tensor_tensor(xn[:, :, :], xn[:, :, :], over_tiles(row_sb[:, 1:2, :]), ALU.add).then_inc(y_ready, 1)
            dve.wait_ge(y_ready, 1)
            c.link(v.tensor_tensor(sq[:, :, :], xn[:, :, :], xn[:, :, :], ALU.mult))
            c.link(v.tensor_reduce(md[:, 1, :, :], sq[:, :, :].rearrange("p t (h d) -> p t h d", d=HD), AXX, ALU.add))
            v.tensor_scalar(md[:, 1, :, :], md[:, 1, :, :], 0.25, None, ALU.mult).then_inc(diag_ready, 1)
            for t in range(NT):
                dve.wait_ge(u_done, t + 1)
                a, b = ((3, 4), (5, 6))[t % 2]
                v.tensor_reduce(md[:, 0, t, 0:8], chunk2(PS[0:TT, a, :], FEATURES), AXX, ALU.max)
                v.tensor_reduce(md[:, 0, t, 8:12], chunk2(PS[0:TT, b, 0:256], FEATURES), AXX, ALU.max).then_inc(u_max, 1)
            dve.wait_ge(mdt_done, 1)
            c.mark(v.tensor_copy(mx_t[:, 0:4 * TT], PS[0:HEADS, 7, 0:4 * TT]))
            c.mark(v.tensor_copy(mx_t[:, 4 * TT:TP], PS[0:HEADS, 1, 0:TT]))
            c.mark(v.tensor_copy(dg_t[:, 0:4 * TT], PS[0:HEADS, 0, 0:4 * TT]))
            c.mark(v.tensor_copy(dg_t[:, 4 * TT:TP], PS[0:HEADS, 1, 128:128 + TT]))
            c.settle()
            c.mark(v.tensor_tensor(bq[:, :], mx_t[:, :], dg_t[:, :], ALU.add))
            c.link(v.tensor_reduce(stab[:, :], chunk2(mx_t[:, :], TOKENS), AXX, ALU.max))
            v.tensor_tensor(chunk2(bk[:, :], TOKENS), chunk2(dg_t[:, :], TOKENS),
                            stab[:, :].unsqueeze(2).to_broadcast([HEADS, NT * GROUP, TOKENS]),
                            ALU.add).then_inc(bias_ready, 1)
            dve.wait_ge(rw_high, 1)
            v.tensor_tensor(rw[:, :, 1, :], rw_raw[:, :, :], rw[:, :, 0, :].bitcast(F32), ALU.subtract)
            v.tensor_tensor(rw[D1:D0, :, 2, :], rw_rraw[:, :, :], rw[0:D1, :, 2, :].bitcast(F32),
                            ALU.subtract).then_inc(rw_ready, 1)

            def rem_low(n, b, width):
                dve.wait_ge(hi_up, n + 1)
                v.tensor_tensor(w_rest[D1:D0, b, 0:width], raw_rem[:, b, 0:width],
                                w_rest[0:D1, b, 0:width].bitcast(F32), ALU.subtract).then_inc(rem_lo, 1)

            rem_low(0, 0, FF)

            def add_eps(c_):
                for w in range(2):
                    dve.wait_ge(exp_done, 4 * c_ + 2 * w + 2)
                    f = qkf[:, c_ % 2, w, :]
                    v.tensor_scalar(f, f, FEATURE_EPS, None, ALU.add).then_inc(eps_done, 1)

            def masks(c_, tiles):
                dve.wait_ge(a_done, 2 * c_ + (1 if tiles.start == 0 else 2))
                if c_ >= 2:
                    dve.wait_ge(av_done, c_ - 1)
                n = tiles.stop - tiles.start
                for j in range(2):
                    v.tensor_tensor(am[:, c_ % 2, j, tiles, :], chunk2(PS[0:TT, j, 0:n * TT], TT),
                                    bmask[:, :].unsqueeze(1).to_broadcast([TT, n, TT]),
                                    ALU.mult).then_inc(mask_done, 1)

            add_eps(0)
            for c_ in range(HEADS // 2):
                masks(c_, slice(0, 4))
                if c_ < HEADS // 2 - 1:
                    add_eps(c_ + 1)
                masks(c_, slice(4, 5))
            dve.wait_ge(ctx_ready, HEADS // 2)
            c.link(v.reciprocal(rden[:, :, :], ctx_sb[:, :, :, HD]))
            c.link(v.tensor_tensor(xn[:, :, :].rearrange("p t (h d) -> p t h d", d=HD), ctx_sb[:, :, :, 0:HD],
                                   rden[:, :, :].unsqueeze(3).to_broadcast([TT, NT, HEADS, HD]), ALU.mult))
            c.link(v.tensor_tensor(x0[:, :, :], x0[:, :, :], xn[:, :, :], ALU.add))
            layernorm(x0, xn, 2)
            c.link(v.tensor_tensor(xn[:, :, :], xn[:, :, :], over_tiles(row_sb[:, 2:3, :]), ALU.mult))
            c.link(v.tensor_tensor(xn[:, :, :], xn[:, :, :], over_tiles(row_sb[:, 3:4, :]), ALU.add))
            split_tokens()
            xt_out(0)
            c.link(v.tensor_tensor(x0[:, :, :], x0[:, :, :], over_tiles(row_sb[:, 4:5, :]), ALU.add))
            c.link(v.tensor_tensor(h[:, :, :], h[:, :, :], x0[:, :, :], ALU.add))

            def hidden(m, s_, hb, ring, pair, width, gated, factor):
                g = 3 * m + s_
                if s_ == 0 and not (isinstance(m, int) and m < 2):
                    dve.wait_ge(down_done, m - 1)
                dve.wait_ge(act_done, g + 1)
                src = act_out[:, ring, 0:2 * width]
                if gated:
                    dve.wait_ge(low_done, g)
                    v.scalar_tensor_tensor(out=prod[:, 0:2 * width], in0=PS[:, UPB[pair], 0:2 * width],
                                           scalar=factor, in1=src, op0=ALU.mult, op1=ALU.mult).then_inc(up_read, 1)
                    dve.wait_ge(up_read, g + 1 - SW0)
                    src = prod[:, 0:2 * width]
                hi_ = h_high[:, hb, 2 * s_:2 * s_ + 2, 0:width]
                v.tensor_copy(hi_, chunk2(src, width)).then_inc(high_done, 1)
                dve.wait_ge(high_done, g + 1)
                v.tensor_tensor(h_lowp[:, hb, 2 * s_:2 * s_ + 2, 0:width], chunk2(src, width), hi_.bitcast(F32),
                                ALU.subtract).then_inc(low_done, 1)

            def dense(m, n, gated, factor):
                width = BLOCKS[m % NB if m < M_ROUTED0 else m - M_COMMON][1]
                for i in range(STEPS):
                    g = 3 * m + i
                    hidden(m, i, m % 2, g % 2, g % 2, width, gated, factor)
                    if i == 0 and m % NB == (0 if m < M_ROUTED0 else M_COMMON % NB):
                        rem_low(n + 1, (n + 1) % 2, UP if 1 <= n + 1 <= 10 else FF)

            def add_acc(which):
                last = per_bank(lambda ts, a: v.tensor_tensor(h[:, ts, :], h[:, ts, :], a, ALU.add))
                last.then_inc(acc_read, 1)
                dve.wait_ge(acc_read, which)

            def router(r):
                ne = EXPERTS + r
                e_ = slice(0, ne)
                dve.wait_ge(logit_done, r + 1)
                psum = chunk2(PS[0:TT, YB, 0:NT * 10], 10)
                if r:
                    c.link(v.tensor_tensor(logit[:, :, :], psum,
                                           rb[:, :].unsqueeze(1).to_broadcast([TT, NT, 10]), ALU.add))
                else:
                    c.link(v.tensor_copy(logit[:, :, :], psum))
                c.link(v.tensor_reduce(lmax[:, :], logit[:, :, e_], AXX, ALU.max))
                v.tensor_tensor(shifted[:, :, :], logit[:, :, :],
                                lmax[:, :].unsqueeze(2).to_broadcast([TT, NT, 10]), ALU.subtract).then_inc(shift_ready, 1)
                dve.wait_ge(lexp_ready, r + 1)
                c.link(v.tensor_reduce(lsum[:, :], lexp[:, :, e_], AXX, ALU.add))
                c.link(v.reciprocal(linv[:, :], lsum[:, :]))
                c.link(v.tensor_tensor(prob[:, :, e_], lexp[:, :, e_],
                                       linv[:, :].unsqueeze(2).to_broadcast([TT, NT, ne]), ALU.mult))
                for t in range(NT):
                    c.mark(v.max(top8[:, t, :], prob[:, t, e_]))
                c.settle()
                for t in range(NT):
                    c.mark(v.max_index(idx8[:, t, :], top8[:, t, :], prob[:, t, e_]))
                c.settle()
                c.link(v.tensor_copy(idxf[:, :, :], idx8[:, :, :]))

                def chosen(out_, i):
                    c.mark(v.tensor_tensor(out_[:, :, e_], expert_id[:, e_].unsqueeze(1).to_broadcast([TT, NT, ne]),
                                           idxf[:, :, i:i + 1].to_broadcast([TT, NT, ne]), ALU.is_equal))

                def weighted(out_, pick, w):
                    c.link(v.tensor_tensor(out_, pick, w.to_broadcast([TT, NT, pick.shape[2]]), ALU.mult))

                chosen(pick1, 0)
                if r == 0:
                    chosen(pick2, 1)
                    c.settle()
                    c.link(v.tensor_tensor(maskf[:, :, :], pick1[:, :, e_], pick2[:, :, e_], ALU.add))
                    c.link(v.tensor_tensor(lsum[:, :], top8[:, :, 0], top8[:, :, 1], ALU.add))
                    c.link(v.tensor_scalar(lsum[:, :], lsum[:, :], 1e-8, None, ALU.add))
                    c.link(v.reciprocal(linv[:, :], lsum[:, :]))
                    c.link(v.tensor_tensor(topw[:, :, :], top8[:, :, 0:2],
                                           linv[:, :].unsqueeze(2).to_broadcast([TT, NT, 2]), ALU.mult))
                    weighted(comb[:, :, e_], pick1[:, :, e_], topw[:, :, 0:1])
                    weighted(pick1[:, :, e_], pick2[:, :, e_], topw[:, :, 1:2])
                    c.link(v.tensor_tensor(comb[:, :, e_], comb[:, :, e_], pick1[:, :, e_], ALU.add))
                else:
                    c.settle()
                    c.link(v.tensor_copy(maskf[:, :, :], pick1[:, :, 1:ne]))
                    c.link(v.tensor_scalar(c0p[:, :, 0], top8[:, :, 0], -1.0, 1.0, ALU.mult, ALU.add))
                    c.link(v.tensor_tensor(c0p[:, :, 1], top8[:, :, 0], pick1[:, :, 0], ALU.mult))
                    c.link(v.tensor_tensor(c0[:, :], c0p[:, :, 0], c0p[:, :, 1], ALU.add))
                    weighted(comb[:, :, 1:ne], pick1[:, :, 1:ne], top8[:, :, 0:1])
                    c.link(v.tensor_copy(comb[:, :, 0], c0[:, :]))
                c.link(v.tensor_tensor(maskf[:, :, :], maskf[:, :, :],
                                       valid[:, :].unsqueeze(2).to_broadcast([TT, NT, EXPERTS]), ALU.mult))
                v.tensor_copy(maskb[:, :, :], maskf[:, :, :])
                v.tensor_scalar(farb[:, :, :], maskf[:, :, :], -1024.0, 1024.0, ALU.mult, ALU.add).then_inc(mask_ready, 1)
                w = comb[:, :, ne - EXPERTS:ne]
                c.link(v.tensor_copy(wtab[:, :, :, 0], w))
                c.link(v.tensor_tensor(wtab[:, :, :, 1], w, wtab[:, :, :, 0].bitcast(F32), ALU.subtract))
                c.link(v.memset(rank_t[:, TP:TX].bitcast(F32), 0.0))
                dve.wait_ge(rank_done, 2 * r + 1)
                v.tensor_copy(rank_t[:, 0:4 * TT], PS[0:EXPERTS, YB, 0:4 * TT]).then_inc(rank_read, 1)
                dve.wait_ge(rank_done, 2 * r + 2)
                c.mark(v.tensor_copy(rank_t[:, 4 * TT:TP], PS[0:EXPERTS, YB, 0:TT]))
                c.mark(v.tensor_reduce(most[:, :], PS[0:TT, YB, 192:192 + EXPERTS], AXX, ALU.max))
                v.tensor_copy(rank[:, :, :], chunk2(PS[0:TT, YB, 128:128 + NT * EXPERTS], EXPERTS)).then_inc(rank_read, 1)
                dve.wait_ge(rank_read, 2 * r + 2)

            def gather_table(r, k, b):
                cap = CAP[r]
                e = slice(k, k + 1) if isinstance(k, int) else bass.ds(k, 1)
                for t in range(NT):
                    v.tensor_scalar(gat[:, b, t, 0:cap], slot_row[:, 0:cap], rank[:, t, e], None, ALU.is_equal)
                v.tensor_copy(wcur[:, b, :, :], wtab[:, :, e, :].rearrange("p t e w -> p t (e w)").bitcast(F32))\
                 .then_inc(gat_ready, 1)

            def expert(r, k, b, first, final):
                n0, m0 = ((3, M_ROUTED0), (12, M_ROUTED1))[r]
                n, m = n0 + k, m0 + k
                cap, st, gated, wb = CAP[r], ST[r], r == 0, (n0 + b) % 2
                ring = (m0 + b) % 2
                e = slice(k, k + 1) if isinstance(k, int) else bass.ds(k, 1)
                hidden(m, 0, ring, ring, 0, cap, gated, 1.0)
                if not final:
                    dve.wait_ge(down_done, m)
                    gather_table(r, k + 1, 1 - b)
                if not final or r == 0:
                    rem_low(n + 1, 1 - wb, UP if r == 0 and not final else FF)
                hidden(m, 1, ring, 1 - ring, 1, cap, gated, 1.0)
                if first:
                    dve.wait_ge(all_read, 2 * EXPERTS * (r + 1))
                if not first or r == 1:
                    dve.wait_ge(scattered, EXPERTS * r + k)
                for i in range(STILES[r]):
                    last = v.tensor_scalar(sca[0:st, i, :], rank_all[0:st, e, :].rearrange("p e t -> p (e t)"),
                                           slot_col[0:st, r, i:i + 1], None, ALU.is_equal)
                last.then_inc(sca_ready, 1)
                hidden(m, 2, ring, ring, 0, cap, gated, 1.0)
                dve.wait_ge(down_done, m + 1)
                ns = STILES[r]
                v.tensor_reduce(slot_w[0:st, 0:ns], chunk2(PS[0:st, YB, 2 * D:2 * D + 2 * ns], 2), AXX,
                                ALU.add).then_inc(slotw, 1)
                dve.wait_ge(slotw, EXPERTS * r + k + 1)
                for i in range(ns):
                    last = v.tensor_scalar(y_s[0:st, i, :], PS[0:st, YB, i * D:(i + 1) * D], slot_w[0:st, i:i + 1],
                                           None, ALU.mult)
                last.then_inc(y_read, 1)
                dve.wait_ge(y_read, EXPERTS * r + k + 1)
                v.tensor_copy(y_h[0:st, 0:ns, :], y_s[0:st, 0:ns, :]).then_inc(y_high, 1)
                dve.wait_ge(y_high, EXPERTS * r + k + 1)
                v.tensor_tensor(y_l[0:st, 0:ns, :], y_s[0:st, 0:ns, :], y_h[0:st, 0:ns, :].bitcast(F32),
                                ALU.subtract).then_inc(y_split, 1)

            def further_unit(r, q, k):
                i = q * EXPERTS + k
                x, cap, st, ns, width = further[r], CAP[r], ST[r], STILES[r], (UP, FF)[r]
                dve.wait_ge(x["scattered"], i + 1)
                dve.wait_ge(x["slots"], 2 * q + 4)
                e = bass.ds(k, 1)
                for t in range(NT):
                    v.tensor_scalar(gat[:, 0, t, 0:cap], slot_row_x[:, 0:cap], rank[:, t, e], None, ALU.is_equal)
                for n in range(ns):
                    v.tensor_scalar(sca[0:st, n, :], rank_all[0:st, e, :].rearrange("p e t -> p (e t)"),
                                    slot_col_x[0:st, n:n + 1], None, ALU.is_equal)
                v.tensor_copy(wcur[:, 0, :, :], wtab[:, :, e, :].rearrange("p t e w -> p t (e w)").bitcast(F32))\
                 .then_inc(x["table"], 1)
                dve.wait_ge(x["high"], i + 1)
                v.tensor_tensor(w_rest[D1:D0, 0, 0:width], raw_rem[:, 0, 0:width],
                                w_rest[0:D1, 0, 0:width].bitcast(F32), ALU.subtract).then_inc(x["rest"], 1)
                for n in range(STEPS):
                    dve.wait_ge(x["activated"], STEPS * i + n + 1)
                    src = act_out[:, 0, 0:2 * cap]
                    if r == 0:
                        v.tensor_tensor(prod[:, 0:2 * cap], PS[:, UPB[0], 0:2 * cap], src,
                                        ALU.mult).then_inc(x["gated"], 1)
                        dve.wait_ge(x["gated"], STEPS * i + n + 1)
                        src = prod[:, 0:2 * cap]
                    hi_ = h_high[:, 0, 2 * n:2 * n + 2, 0:cap]
                    v.tensor_copy(hi_, chunk2(src, cap)).then_inc(x["hidden_high"], 1)
                    dve.wait_ge(x["hidden_high"], STEPS * i + n + 1)
                    v.tensor_tensor(h_lowp[:, 0, 2 * n:2 * n + 2, 0:cap], chunk2(src, cap), hi_.bitcast(F32),
                                    ALU.subtract).then_inc(x["hidden"], 1)
                    dve.wait_ge(x["hidden"], STEPS * i + n + 1)
                dve.wait_ge(x["down"], i + 1)
                v.tensor_reduce(slot_w[0:st, 0:ns], chunk2(PS[0:st, YB, 2 * D:2 * D + 2 * ns], 2), AXX,
                                ALU.add).then_inc(x["weights"], 1)
                dve.wait_ge(x["weights"], i + 1)
                for n in range(ns):
                    last = v.tensor_scalar(y_s[0:st, n, :], PS[0:st, YB, n * D:(n + 1) * D], slot_w[0:st, n:n + 1],
                                           None, ALU.mult)
                last.then_inc(x["outputs"], 1)
                dve.wait_ge(x["outputs"], i + 1)
                v.tensor_copy(y_h[0:st, 0:ns, :], y_s[0:st, 0:ns, :]).then_inc(x["outputs_high"], 1)
                dve.wait_ge(x["outputs_high"], i + 1)
                v.tensor_tensor(y_l[0:st, 0:ns, :], y_s[0:st, 0:ns, :], y_h[0:st, 0:ns, :].bitcast(F32),
                                ALU.subtract).then_inc(x["outputs_split"], 1)

            def experts(r):
                for b in range(2):
                    expert(r, b, b, b == 0, False)
                with dve.Fori(1, EXPERTS // 2 - 1) as p:
                    for b in range(2):
                        expert(r, 2 * p + b, b, False, False)
                for b in range(2):
                    expert(r, EXPERTS - 2 + b, b, False, b == 1)
                dve.wait_ge(scattered, EXPERTS * (r + 1))

                def next_slots(q):
                    dve.wait_ge(further[r]["scattered"], q * EXPERTS + 1)
                    dve.wait_ge(further[r]["slots"], 2 * q + 2)
                    v.tensor_scalar(slot_row_x[:, :], slot_row_x[:, :], float(CAP[r]), None,
                                    ALU.add).then_inc(further[r]["slots"], 1)
                    v.tensor_scalar(slot_col_x[:, :], slot_col_x[:, :], float(CAP[r]), None,
                                    ALU.add).then_inc(further[r]["slots"], 1)

                v.tensor_copy(slot_row_x[:, :], slot_row[:, :]).then_inc(further[r]["slots"], 1)
                v.tensor_copy(slot_col_x[:, :], slot_col[:, r, :]).then_inc(further[r]["slots"], 1)
                further_rounds(dve, r, further_unit, next_slots)

            def count_rounds(r):
                further_n = -(-T // CAP[r]) - 1
                for q in range(further_n):
                    c.mark(v.tensor_scalar(over[:, q:q + 1], most[:, :], float(CAP[r] * (q + 1)), None, ALU.is_gt))
                c.settle()
                c.link(v.tensor_reduce(rounds_f[:, r:r + 1], over[:, 0:further_n], AXX, ALU.add))
                v.tensor_copy(rounds[:, r:r + 1], rounds_f[:, r:r + 1]).then_inc(rounds_ready, 1)

            for m in range(NB):
                dense(m, 0, False, 1.0)
            dve.wait_ge(down_done, NB)
            add_acc(1)
            layernorm(h, xn, 3)
            split_tokens()
            xt_out(1)
            router(0)
            for m in range(NB, M_ROUTED0):
                dense(m, m // NB, True, 0.5)
            gather_table(0, 0, 0)
            count_rounds(0)
            experts(0)
            dve.wait_ge(mixed, 1)
            add_acc(2)
            layernorm(h, xn, 4)
            split_tokens()
            dve.wait_ge(a1bn_in, 32)
            v.tensor_scalar(col_ve[:, :], col_raw[:, 4, :], LN_EPS, None, ALU.add)
            v.tensor_scalar(row_ve[:, :, :], row_raw[:, :, 4, :], LN_EPS, None, ALU.add).then_inc(bn_var, 1)
            xt_out(2)
            dve.wait_ge(a_hi, 1)
            v.tensor_tensor(a_rest[D1:D0, :], a_rraw[:, :], a_rest[0:D1, :].bitcast(F32),
                            ALU.subtract).then_inc(a_lor, 1)
            dve.wait_ge(bn_std, 1)
            for raw, sd, is_, inv, mi, shift in (
                    (lambda i: col_raw[:, i, :], col_std[:, :], col_is[:, :], col_inv[:, :], col_mi[:, :], col_shift[:, :]),
                    (lambda i: row_raw[:, :, i, :], row_std[:, :, :], row_is[:, :, :], row_inv[:, :, :],
                     row_mi[:, :, :], row_shift[:, :, :])):
                c.link(v.reciprocal(is_, sd))
                c.link(v.tensor_tensor(inv, raw(1), is_, ALU.mult))
                c.link(v.tensor_tensor(mi, raw(3), inv, ALU.mult))
                c.link(v.tensor_tensor(shift, raw(2), mi, ALU.subtract))
            for i in range(12):
                w, cc, half = i // 6, i // 2 % QK_CHUNKS, i % 2
                col = w * QK_CHUNKS + cc
                dve.wait_ge(qk_done, i + 1)
                if i >= 2:
                    dve.wait_ge(qk_spiked, i - 1)
                v.tensor_scalar(ymid[:, i % 2, :], PS[:, 3 + i % 4, 0:HX], col_raw[:, 0, col:col + 1],
                                col_inv[:, col:col + 1], ALU.add, ALU.mult).then_inc(qk_mid, 1)
                dve.wait_ge(qk_mid, i + 1)
                v.tensor_scalar(qk_spk[:, w, cc, half * HX:(half + 1) * HX], ymid[:, i % 2, :],
                                col_shift[:, col:col + 1], 2.0, ALU.add, ALU.is_ge).then_inc(qk_spiked, 1)

            def normalise(i):
                def row(a):
                    return a[:, i:i + 1, :]
                last = per_bank(lambda ts, a: v.tensor_tensor(
                    bt1[:, ts, :], a, row_raw[:, i, 0:1, :].to_broadcast([TT, ts.stop - ts.start, D]), ALU.add))
                c.link(last)
                c.link(v.tensor_tensor(bt2[:, :, :], bt1[:, :, :], over_tiles(row(row_inv)), ALU.mult))
                c.link(v.tensor_tensor(bt1[:, :, :], bt2[:, :, :], over_tiles(row(row_shift)), ALU.add))

            dve.wait_ge(v_done, 1)
            normalise(0)
            v.tensor_scalar(v_spk[:, :, :], bt1[:, :, :], 2.0, None, ALU.is_ge).then_inc(v_ready, 1)
            for t in range(NT):
                dve.wait_ge(s_done, t + 1)
                if t:
                    dve.wait_ge(xa_done, t)
                for j in range(4):
                    v.tensor_tensor(am1[:, j, :, :], chunk2(PS[0:TT, 3 + j, 0:QK_CHUNKS * TT], TT),
                                    bmask[:, :].unsqueeze(1).to_broadcast([TT, QK_CHUNKS, TT]),
                                    ALU.mult).then_inc(s_masked, 1)
            dve.wait_ge(xa_done, NT)
            for lo, hi, out_ in ((0, D0, lambda ts: xs[:, ts, 0, :]), (D0, D, lambda ts: xs[:, ts, 1, 0:D1]),
                                 (D0, D, lambda ts: xs[:, ts, 1, D1:D0])):
                last = per_bank(lambda ts, a: v.tensor_scalar(out_(ts), a[:, :, lo:hi], SCALE1, 1.0,
                                                              ALU.mult, ALU.is_ge))
            last.then_inc(xs_ready, 1)
            dve.wait_ge(o_done, 1)
            normalise(1)
            c.link(v.tensor_scalar(bt2[:, :, :], bt1[:, :, :], 2.0, None, ALU.is_ge))
            c.link(v.tensor_tensor(h[:, :, :], h[:, :, :], bt2[:, :, :], ALU.add))
            layernorm(h, xn, 5)
            split_tokens()
            xt_out(3)
            router(1)
            dve.wait_ge(comb_done, 1)
            v.tensor_copy(comb_t[:, 0:4 * TT], PS[0:EXPERTS + 1, YB, 0:4 * TT]).then_inc(comb_read, 1)
            dve.wait_ge(comb_done, 2)
            v.tensor_copy(comb_t[:, 4 * TT:TP], PS[0:EXPERTS + 1, YB, 0:TT]).then_inc(comb_read, 1)
            for m in range(M_COMMON, M_ROUTED1):
                dense(m, 11, False, 1.0)
            gather_table(1, 0, 0)
            count_rounds(1)
            dve.wait_ge(down_done, M_ROUTED1)
            for t in range(NT):
                last = v.scalar_tensor_tensor(out=h[:, t, :], in0=acc(t), scalar=c0[:, t:t + 1], in1=h[:, t, :],
                                              op0=ALU.mult, op1=ALU.add)
            last.then_inc(acc_read, 1)
            experts(1)
            dve.wait_ge(mixed, 2)
            last = per_bank(lambda ts, a: v.tensor_tensor(h[:, ts, :], h[:, ts, :], a, ALU.add))
            last.then_inc(y_out, 1)


_OUT = (T, D)


def _launch_arrays(i):
    f = {k: np.asarray(v) for k, v in i.items()}

    def split_rows(w):
        return w[..., :D0, :], w[..., D0:, :]

    def chunked(w):
        return w.reshape(-1, FC, 128, D).transpose(0, 2, 1, 3).reshape(-1, 128, GW)

    x = f["x"].reshape(IMAGES, GRID, PATCH, GRID, PATCH, CHANNELS).transpose(2, 4, 5, 0, 1, 3)
    patches = np.zeros((PATCH_DIM, NT * GROUP, TOKENS), np.float32)
    patches[:, :IMAGES, 1:] = x.reshape(PATCH_DIM, IMAGES, GRID * GRID)
    swi = np.concatenate([f["L0_ffn_shared_gate"], f["L0_ffn_routed_gate"]]), \
        np.concatenate([f["L0_ffn_shared_up"], f["L0_ffn_routed_up"]]), \
        np.concatenate([f["L0_ffn_shared_down"], f["L0_ffn_routed_down"]])
    up_main, up_rem = split_rows(np.concatenate([swi[0].transpose(0, 2, 1), swi[1].transpose(0, 2, 1)], axis=2))
    g1 = np.concatenate([f["L0_attn_W1"][None], f["L1_ffn_W1"]])
    g2 = np.concatenate([f["L0_attn_W2"][None], f["L1_ffn_W2"]])
    gb = np.concatenate([f["L0_attn_b1"][None], f["L1_ffn_b1"]]).reshape(-1, FC, 128).transpose(0, 2, 1)
    g_main, g_rem = split_rows(g1)
    wt = f["L1_attn_W"].transpose(0, 2, 1)
    qk = np.zeros((D, 2, HEADS, 32), np.float32)
    qk[..., :HD] = wt[:2].transpose(1, 0, 2).reshape(D, 2, HEADS, HD)
    a1 = np.concatenate([qk.reshape(D, -1), wt[2], wt[3]], axis=1)
    bn = np.stack([f["L1_attn_b"], f["L1_attn_bn_gamma"], f["L1_attn_bn_beta"], f["L1_attn_bn_mean"],
                   f["L1_attn_bn_var"]])
    col = np.zeros((5, 2, HEADS, 32), np.float32)
    col[..., :HD] = bn[:, :2].reshape(5, 2, HEADS, HD)
    router = np.zeros((D, 2, 10), np.float32)
    router[:, 0, :EXPERTS] = f["L0_ffn_gate_w"].T
    router[:, 1, :EXPERTS + 1] = f["L1_ffn_Ws"]
    router_b = np.zeros((10,), np.float32)
    router_b[:EXPERTS + 1] = f["L1_ffn_bs"]
    arrays = dict(
        patches=patches.reshape(KT, 128, TP).transpose(1, 0, 2),
        tok_w=f["L0_tok_W"].reshape(KT, 128, D).transpose(1, 0, 2),
        tok_b=f["L0_tok_b"].reshape(1, D),
        cls_pos=np.concatenate([f["cls_tok"].reshape(1, D), f["L0_tok_pos_emb"]]),
        proj_t=f["L0_attn_proj"].T,
        rows=np.stack([f["L0_attn_ln1_g"], f["L0_attn_ln1_b"], f["L0_attn_ln2_g"], f["L0_attn_ln2_b"],
                       f["L0_attn_b2"]]),
        router_w=router, router_b=router_b,
        sw_main=np.concatenate([up_main, chunked(swi[2].transpose(0, 2, 1))], axis=2), sw_rem=up_rem,
        ge_main=np.concatenate([g_main, chunked(g2), gb], axis=2), ge_rem=g_rem,
        a1_main=a1[:D0], a1_rem=a1[D0:],
        a1_col=col.reshape(5, 2 * QK_CHUNKS, 128).transpose(2, 0, 1),
        a1_row=bn[:, 2:].transpose(1, 0, 2),
        moe_b2=f["L1_ffn_b2"],
    )
    return {k: np.ascontiguousarray(a) for k, a in arrays.items()}


def kernel(**inputs):
    import concourse.bacc as bacc
    from concourse.bass_utils import run_bass_kernel_spmd

    nc = bacc.Bacc("TRN2", target_bir_lowering=False, num_devices=1)
    arrays = _launch_arrays(inputs)
    args = {k: nc.dram_tensor(f"in_{k}", a.shape, F32, kind="ExternalInput").ap() for k, a in arrays.items()}
    out = nc.dram_tensor("out", _OUT, F32, kind="ExternalOutput").ap()
    tower_kernel(nc, out=out, **args)
    r = run_bass_kernel_spmd(nc, [{f"in_{k}": a for k, a in arrays.items()}], core_ids=[0])
    return r.results[0]["out"].reshape(IMAGES, TOKENS, D)
```

```python
import numpy as np
import concourse.bass as bass
from concourse import mybir
from contextlib import ExitStack

F32 = mybir.dt.float32
F32R = mybir.dt.float32r
BF16 = mybir.dt.bfloat16
I32 = mybir.dt.int32
U32 = mybir.dt.uint32
ALU = mybir.AluOpType
ACT = mybir.ActivationFunctionType
AXX = mybir.AxisListType.X

IMAGES, GRID, PATCH, CHANNELS = 32, 4, 16, 3
TOKENS = GRID * GRID + 1
D, FF, HEADS, FEATURES = 192, 768, 12, 64
HD = D // HEADS
PATCH_DIM = PATCH * PATCH * CHANNELS
EXPERTS = 8
GROUP = 7
TT = GROUP * TOKENS
NT = -(-IMAGES // GROUP)
TP = NT * TT
TX = TP + 1
HX = TX // 2
T = IMAGES * TOKENS
D0, D1 = 128, D - 128
KT = PATCH_DIM // 128
FC = FF // 128
STEPS = FC // 2
BLK = 2 * TT
BLOCKS = [(0, BLK), (BLK, BLK), (2 * BLK, T - 2 * BLK)]
NB = len(BLOCKS)
WARM = (20, 2, 7, 16, 16, 14, 16, 4, 8)
LN_EPS = 1e-5
FEATURE_EPS = 1e-4
UP, GW = 2 * FF, FC * D
MAIN_S, MAIN_G = UP + GW, FF + GW + FC
QK_CHUNKS = 3
A1 = 2 * QK_CHUNKS * 128 + 2 * D
V_COL = 2 * QK_CHUNKS * 128
SCALE1 = float(HD) ** -0.125
M_ROUTED0 = 3 * NB
M_COMMON = M_ROUTED0 + EXPERTS
M_ROUTED1 = M_COMMON + NB
M_END = M_ROUTED1 + EXPERTS
SW0 = NB * STEPS


def tiles_of(start, width):
    return [(start // TT + i, i * TT, min(TT, width - i * TT)) for i in range(-(-width // TT))]


def tower_kernel(nc, patches, tok_w, tok_b, cls_pos, proj_t, rows, router_w, router_b, sw_main, sw_rem,
                 ge_main, ge_rem, a1_main, a1_rem, a1_col, a1_row, moe_b2, out, caps=(192, 128)):
    CAP = caps
    STILES = [-(-c // 128) for c in CAP]
    ST = [c // n for c, n in zip(CAP, STILES)]
    ctx = ExitStack()
    with ctx:
        def sem(name):
            return ctx.enter_context(nc.semaphore(name))

        SIZE = {F32: 4, F32R: 4, I32: 4, U32: 4, BF16: 2}
        place = [-(-nc.sbuf_base // 64) * 64]

        def sb(name, shape, dt=F32):
            offset = place[0]
            width = int(np.prod(shape[1:])) * SIZE[dt]
            place[0] = offset + -(-width // 32) * 32
            return nc.alloc_sbuf_tensor_at(name, shape, dt, offset=offset)

        h = sb("h", [TT, NT, D])
        x0 = sb("x0", [TT, NT, D])
        xn = sb("xn", [TT, NT, D])
        xtok = sb("xtok", [TT, NT, 4, 128], F32R)
        xt = sb("xt", [128, 4, TX], F32R)
        raw_main = sb("raw_main", [128, 2, MAIN_S])
        raw_rem = sb("raw_rem", [D1, 2, UP])
        w_high = sb("w_high", [128, 2, UP], F32R)
        w_low = sb("w_low", [128, 2, UP], F32R)
        w_rest = sb("w_rest", [128, 2, UP], F32R)
        d_high = sb("d_high", [128, 2, GW], F32R)
        d_low = sb("d_low", [128, 2, GW], F32R)
        bias1 = sb("bias1", [128, 2, FC])
        row_sb = sb("row_sb", [TT, 5, D])
        ident = sb("ident", [128, 128])
        ident_b = sb("ident_b", [128, 128], BF16)
        bmask = sb("bmask", [TT, TT])
        valid = sb("valid", [TT, NT])
        tri = sb("tri", [TT, TT], BF16)
        ones_b = sb("ones_b", [TT, TT], BF16)
        zeros_b = sb("zeros_b", [1, 512], BF16)
        slot_row = sb("slot_row", [TT, max(CAP)])
        slot_col = sb("slot_col", [128, 2, 2])
        expert_id = sb("expert_id", [TT, 10])
        stats = sb("stats", [TT, NT, 6])
        mv = sb("mv", [TT, NT, 2])
        veps = sb("veps", [TT, NT])
        std = sb("std", [TT, NT])
        rstd = sb("rstd", [TT, NT])
        rw_raw = sb("rw_raw", [128, 2, 10])
        rw_rraw = sb("rw_rraw", [D1, 2, 10])
        rw = sb("rw", [128, 2, 3, 10], F32R)
        rb = sb("rb", [TT, 10])
        logit = sb("logit", [TT, NT, 10])
        lmax = sb("lmax", [TT, NT])
        shifted = sb("shifted", [TT, NT, 10])
        lexp = sb("lexp", [TT, NT, 10])
        lsum = sb("lsum", [TT, NT])
        linv = sb("linv", [TT, NT])
        prob = sb("prob", [TT, NT, 10])
        top8 = sb("top8", [TT, NT, 8])
        idx8 = sb("idx8", [TT, NT, 8], U32)
        idxf = sb("idxf", [TT, NT, 8])
        pick1 = sb("pick1", [TT, NT, 10])
        pick2 = sb("pick2", [TT, NT, 10])
        topw = sb("topw", [TT, NT, 2])
        comb = sb("comb", [TT, NT, 10])
        maskf = sb("maskf", [TT, NT, EXPERTS])
        maskb = sb("maskb", [TT, NT, EXPERTS], BF16)
        farb = sb("farb", [TT, NT, EXPERTS], BF16)
        rank = sb("rank", [TT, NT, EXPERTS])
        wtab = sb("wtab", [TT, NT, EXPERTS, 2], F32R)
        wcur = sb("wcur", [TT, 2, NT, 32], F32R)
        w_row = sb("w_row", [32, max(CAP)], F32R)
        ones_f = sb("ones_f", [32, 2], F32R)
        slot_w = sb("slot_w", [128, 2])
        slot_row_x = sb("slot_row_x", [TT, max(CAP)])
        slot_col_x = sb("slot_col_x", [128, 2])
        most = sb("most", [TT, 1])
        over = sb("over", [TT, 8])
        rounds_f = sb("rounds_f", [TT, 2])
        rounds = sb("rounds", [TT, 2], I32)
        c0 = sb("c0", [TT, NT])
        c0p = sb("c0p", [TT, NT, 2])
        b2_sb = sb("b2_sb", [EXPERTS + 1, D])
        shared_base = place[0]

        bdiag = sb("bdiag", [128, 8 * FEATURES])
        patch_base = place[0]
        patch_sb = sb("patch_sb", [128, KT, TP])
        tokw_sb = sb("tokw_sb", [128, KT, D])
        patch_end = place[0]
        tokb_sb = sb("tokb_sb", [1, D])
        prow = sb("prow", [1, GROUP, TOKENS])
        clspos_sb = sb("clspos_sb", [TT, D])
        bdiag2 = sb("bdiag2", [128, 4 * FEATURES])
        bd_high = sb("bd_high", [128, 8 * FEATURES], F32R)
        bd_low = sb("bd_low", [128, 8 * FEATURES], F32R)
        bd2_high = sb("bd2_high", [128, 4 * FEATURES], F32R)
        bd2_low = sb("bd2_low", [128, 4 * FEATURES], F32R)
        negsel = sb("negsel", [128, HEADS, FEATURES], F32R)
        vaug = sb("vaug", [TT, NT, HEADS, 32])
        sq = sb("sq", [TT, NT, D])
        y_high = sb("y_high", [128, TX], F32R)
        y_low = sb("y_low", [128, TX], F32R)
        y_rest = sb("y_rest", [128, TX], F32R)
        md = sb("md", [TT, 2, NT, HEADS])
        mx_t = sb("mx_t", [HEADS, TP])
        dg_t = sb("dg_t", [HEADS, TP])
        stab = sb("stab", [HEADS, NT * GROUP])
        bsum = sb("bsum", [HEADS, 2, TP])
        bq = sb("bq", [128, TX], F32R)
        bk = sb("bk", [128, TX], F32R)
        qkf = sb("qkf", [128, 2, 2, TP])
        rden = sb("rden", [TT, NT, HEADS])
        top_a = place[0]
        place[0] = patch_base
        am = sb("am", [TT, 2, 2, NT, TT])
        ctx_t = sb("ctx_t", [128, HEADS // 4, TP])
        assert place[0] <= patch_end

        place[0] = shared_base
        xg = sb("xg", [128, 4, max(CAP)], F32R)
        act_out = sb("act_out", [128, 2, 2 * BLK])
        prod = sb("prod", [128, 2 * BLK])
        h_high = sb("h_high", [128, 2, FC, BLK], F32R)
        h_lowp = sb("h_lowp", [128, 2, FC, BLK], F32R)
        rank_all = sb("rank_all", [128, EXPERTS, TX])
        gat = sb("gat", [TT, 2, NT, max(CAP)], F32R)
        sca = sb("sca", [128, 2, TX], F32R)
        y_h = sb("y_h", [128, 2, D], F32R)
        y_l = sb("y_l", [128, 2, D], F32R)
        rank_t = sb("rank_t", [EXPERTS, TX], F32R)
        comb_t = sb("comb_t", [EXPERTS + 1, TP])
        pick_row = sb("pick_row", [EXPERTS, EXPERTS, 128], F32R)
        top_b = place[0]

        place[0] = shared_base
        a_raw = sb("a_raw", [128, A1])
        a_rraw = sb("a_rraw", [D1, A1])
        a_high = sb("a_high", [128, A1], F32R)
        a_low = sb("a_low", [128, A1], F32R)
        a_rest = sb("a_rest", [128, A1], F32R)
        col_raw = sb("col_raw", [128, 5, 2 * QK_CHUNKS])
        col_ve = sb("col_ve", [128, 2 * QK_CHUNKS])
        col_std = sb("col_std", [128, 2 * QK_CHUNKS])
        col_is = sb("col_is", [128, 2 * QK_CHUNKS])
        col_inv = sb("col_inv", [128, 2 * QK_CHUNKS])
        col_mi = sb("col_mi", [128, 2 * QK_CHUNKS])
        col_shift = sb("col_shift", [128, 2 * QK_CHUNKS])
        row_raw = sb("row_raw", [TT, 2, 5, D])
        row_ve = sb("row_ve", [TT, 2, D])
        row_std = sb("row_std", [TT, 2, D])
        row_is = sb("row_is", [TT, 2, D])
        row_inv = sb("row_inv", [TT, 2, D])
        row_mi = sb("row_mi", [TT, 2, D])
        row_shift = sb("row_shift", [TT, 2, D])
        ymid = sb("ymid", [128, 2, HX])
        qk_spk = sb("qk_spk", [128, 2, QK_CHUNKS, TX], BF16)
        bt1 = sb("bt1", [TT, NT, D])
        bt2 = sb("bt2", [TT, NT, D])
        v_spk = sb("v_spk", [TT, NT, D], BF16)
        am1 = sb("am1", [TT, 4, QK_CHUNKS, TT], BF16)
        xs = sb("xs", [TT, NT, 2, 128])
        top_c = place[0]
        assert max(top_a, top_b, top_c) <= nc.sbuf_usable_end, (top_a, top_b, top_c, nc.sbuf_usable_end)

        PS = ctx.enter_context(nc.psum_tensor("PS", [128, 8, 512], F32))
        YB = 7
        CTX_BANKS = (3, 4, 5, 0, 1)
        GATE, UPB = (3, 5), (4, 6)

        def acc(t):
            return PS[0:TT, t // 2, (t % 2) * D:(t % 2 + 1) * D]

        def cols(t):
            return slice(t * TT, (t + 1) * TT)

        def buf_of(n):
            return n % 2

        def blocks_done(n):
            return 3 * (n + 1) if n < 3 else n + 7 if n < 11 else 20 if n == 11 else n + 9

        def chunk2(ap, n):
            return ap.rearrange("p (c n) -> p c n", n=n)

        patch_in = [sem(f"patch_in{i}") for i in range(KT)]
        tok_in = sem("tok_in"); clspos_in = sem("clspos_in"); rows_in = sem("rows_in")
        proj_in = sem("proj_in"); proj_high = sem("proj_high"); proj_low = sem("proj_low"); router_in = sem("router_in"); b2_in = sem("b2_in")
        raw_in = [sem("raw_in0"), sem("raw_in1")]; a1_in = sem("a1_in"); a1bn_in = sem("a1bn_in")
        const = sem("const")
        vec = sem("vec"); pool_step = sem("pool_step")
        embedded = sem("embedded"); var_ready = sem("var_ready"); std_ready = sem("std_ready")
        y_ready = sem("y_ready"); vaug_ready = sem("vaug_ready"); yt_done = sem("yt_done"); yt_ready = sem("yt_ready")
        yt_high = sem("yt_high"); tail_done = sem("tail_done"); q_bias = sem("q_bias")
        u_done = sem("u_done"); u_max = sem("u_max"); diag_ready = sem("diag_ready"); mdt_done = sem("mdt_done")
        bias_ready = sem("bias_ready"); feat_done = sem("feat_done"); exp_done = sem("exp_done")
        eps_done = sem("eps_done"); a_done = sem("a_done"); mask_done = sem("mask_done"); av_done = sem("av_done")
        ctx_ready = sem("ctx_ready"); ctx_done = sem("ctx_done")
        tok_split = sem("tok_split"); xt_done = sem("xt_done"); xt_act = sem("xt_act"); xt_vec = sem("xt_vec")
        hi_up = sem("hi_up"); hi_rest = sem("hi_rest"); hi_dn = sem("hi_dn"); lo_up = sem("lo_up"); lo_dn = sem("lo_dn"); rem_lo = sem("rem_lo")
        gu_done = sem("gu_done"); act_done = sem("act_done"); up_read = sem("up_read"); high_done = sem("high_done")
        low_done = sem("low_done"); down_done = sem("down_done"); acc_read = sem("acc_read")
        rw_high = sem("rw_high"); rw_ready = sem("rw_ready")
        logit_done = sem("logit_done"); shift_ready = sem("shift_ready"); lexp_ready = sem("lexp_ready")
        mask_ready = sem("mask_ready"); rank_done = sem("rank_done"); rank_read = sem("rank_read")
        all_done = sem("all_done"); all_read = sem("all_read"); comb_done = sem("comb_done"); comb_read = sem("comb_read")
        gat_ready = sem("gat_ready"); pick_ready = sem("pick_ready"); wt_ready = sem("wt_ready"); gathered = sem("gathered"); xg_ready = sem("xg_ready")
        slotw = sem("slotw"); out_high = sem("out_high")
        y_split = sem("y_split"); sca_ready = sem("sca_ready"); scattered = sem("scattered")
        a_hi = sem("a_hi"); a_lo = sem("a_lo"); a_lor = sem("a_lor"); bn_var = sem("bn_var"); bn_std = sem("bn_std")
        qk_done = sem("qk_done"); qk_mid = sem("qk_mid"); qk_spiked = sem("qk_spiked")
        v_done = sem("v_done"); v_ready = sem("v_ready"); s_done = sem("s_done"); s_masked = sem("s_masked")
        xa_done = sem("xa_done"); xs_ready = sem("xs_ready"); xst_done = sem("xst_done"); xst_ready = sem("xst_ready")
        rounds_ready = sem("rounds_ready"); mixed = sem("mixed")
        further = [{n: sem(f"further{r}_{n}") for n in (
            "loaded", "high", "low", "rest", "slots", "table", "gathered", "tokens", "products", "activated",
            "gated", "hidden_high", "hidden", "down", "weights", "outputs_high", "outputs_split",
            "scattered")} for r in range(2)]
        o_done = sem("o_done"); y_out = sem("y_out"); stored = sem("stored")

        class Chain:
            def __init__(self, eng, steps):
                self.eng, self.steps, self.n = eng, steps, 0

            def mark(self, ins):
                ins.then_inc(self.steps, 1)
                self.n += 1

            def link(self, ins):
                self.mark(ins)
                self.eng.wait_ge(self.steps, self.n)

            def settle(self):
                self.eng.wait_ge(self.steps, self.n)

        def further_rounds(eng, r, unit, begin=None):
            eng.wait_ge(rounds_ready, r + 1)
            n = eng.value_load(rounds[0:1, r:r + 1], min_val=0, max_val=-(-T // CAP[r]) - 1)
            with eng.If(n):
                with eng.Fori(0, n) as q:
                    if begin is not None:
                        begin(q)
                    with eng.Fori(0, EXPERTS) as k:
                        unit(r, q, k)

        block = ctx.enter_context(nc.Block())

        @block.sync
        def _(sp):
            sp.dma_start(tokw_sb[:, :, :], tok_w).then_inc(tok_in, 16)
            for kt in range(KT):
                sp.dma_start(patch_sb[:, kt, :], patches[:, kt, :]).then_inc(patch_in[kt], 16)

            def load(n, b, main, rem, width, rem_width):
                sp.dma_start(raw_main[:, b, 0:width], main).then_inc(raw_in[b], 16)
                sp.dma_start(raw_rem[:, b, 0:rem_width], rem).then_inc(raw_in[b], 16)

            def release(n):
                sp.wait_ge(lo_dn, n + 1)
                sp.wait_ge(rem_lo, n + 1)

            def one(a, i):
                return a[bass.ds(i, 1), :, :].rearrange("e p n -> p (e n)")

            load(0, 0, one(ge_main, 0), one(ge_rem, 0), MAIN_G, FF)
            load(1, 1, one(sw_main, 0), one(sw_rem, 0), MAIN_S, UP)
            release(0)
            load(2, 0, one(sw_main, 1), one(sw_rem, 1), MAIN_S, UP)
            with sp.Fori(0, EXPERTS // 2) as p:
                for b in range(2):
                    k = 2 * p + b
                    release(1 + k)
                    load(3 + k, 1 - b, one(sw_main, 2 + k), one(sw_rem, 2 + k), MAIN_S, UP)
            release(9)
            load(11, 1, one(ge_main, 1), one(ge_rem, 1), MAIN_G, FF)

            def further_load(r, q, k):
                i = q * EXPERTS + k
                x = further[r]
                main, rem, first, width = ((sw_main, sw_rem, 2, UP), (ge_main, ge_rem, 2, FF))[r]
                sp.wait_ge(x["scattered"], i + 1)
                cols_ = MAIN_S if r == 0 else MAIN_G
                sp.dma_start(raw_main[:, 0, 0:cols_], one(main, first + k)).then_inc(x["loaded"], 16)
                sp.dma_start(raw_rem[:, 0, 0:width], one(rem, first + k)).then_inc(x["loaded"], 16)

            sp.wait_ge(scattered, EXPERTS)
            further_rounds(sp, 0, further_load)
            sp.wait_ge(mixed, 1)
            sp.wait_ge(acc_read, 2)
            sp.dma_start(a_raw[:, :], a1_main).then_inc(a1_in, 16)
            sp.dma_start(a_rraw[:, :], a1_rem).then_inc(a1_in, 16)
            sp.dma_start(col_raw[:, :, :], a1_col).then_inc(a1bn_in, 16)
            sp.dma_start(row_raw[:, :, :, :].rearrange("p a b d -> p (a b d)"),
                         a1_row.rearrange("a b d -> (a b d)").partition_broadcast(TT)).then_inc(a1bn_in, 16)
            with sp.Fori(0, EXPERTS // 2) as p:
                for b in range(2):
                    k = 2 * p + b
                    release(10 + k)
                    load(12 + k, b, one(ge_main, 2 + k), one(ge_rem, 2 + k), MAIN_G, FF)
            sp.wait_ge(scattered, 2 * EXPERTS)
            further_rounds(sp, 1, further_load)
            sp.wait_ge(y_out, 1)
            sp.dma_start(out[0:4 * TT, :].rearrange("(t p) d -> p t d", p=TT), h[:, 0:4, :]).then_inc(stored, 16)
            sp.dma_start(out[4 * TT:T, :], h[0:T - 4 * TT, 4, :]).then_inc(stored, 16)
            sp.wait_ge(stored, 32)

        @block.gpsimd
        def _(pool):
            c = Chain(pool, pool_step)
            g = nc.gpsimd
            g.memset(bdiag[:, :], 0.0)
            c.mark(g.memset(bdiag2[:, :], 0.0))
            g.memset(ident[:, :], 0.0)
            g.memset(bmask[:, :], 1.0)
            g.memset(valid[:, :], 1.0)
            g.memset(ones_b[:, :], 1.0)
            g.memset(zeros_b[:, :], 0.0)
            g.memset(ones_f[:, :].bitcast(F32), 1.0)
            g.memset(wcur[:, :, :, :].bitcast(F32), 0.0)
            g.memset(prow[:, :, :], 1.0)
            g.memset(negsel[:, :, :].bitcast(F32), 0.0)
            g.memset(bq[:, :].bitcast(F32), 0.0)
            g.memset(bk[:, :].bitcast(F32), 0.0)
            for y in (y_high, y_low, y_rest):
                g.memset(y[:, TP:TX].bitcast(F32), 0.0)
            g.memset(xt[:, :, TP:TX].bitcast(F32), 0.0)
            c.link(g.memset(vaug[:, :, :, :], 0.0))
            g.memset(vaug[:, :, :, HD:HD + 1], 1.0)
            g.memset(prow[:, :, 0:1], 0.0)
            g.affine_select(out=ident[:, :], in_=ident[:, :], compare_op=ALU.not_equal, fill=1.0, base=0,
                            pattern=[[-1, 128]], channel_multiplier=1)
            same = bmask[:, :].rearrange("p (i n) -> p i n", n=TOKENS)
            c.mark(g.affine_select(out=negsel[:, :, :], in_=negsel[:, :, :].bitcast(F32), compare_op=ALU.not_equal,
                                   fill=-1.0, base=0, pattern=[[-1, HEADS], [0, FEATURES]], channel_multiplier=1))
            g.affine_select(out=tri[:, :], in_=ones_b[:, :], compare_op=ALU.is_ge, fill=0.0, base=-1,
                            pattern=[[1, TT]], channel_multiplier=-1)
            g.affine_select(out=valid[:, :], in_=valid[:, :], compare_op=ALU.is_ge, fill=0.0, base=T - 1,
                            pattern=[[-TT, NT]], channel_multiplier=-1)
            c.link(g.affine_select(out=same, in_=same, compare_op=ALU.is_ge, fill=0.0, base=0,
                                   pattern=[[-TOKENS, GROUP], [0, TOKENS]], channel_multiplier=1))
            g.affine_select(out=same, in_=same, compare_op=ALU.is_ge, fill=0.0, base=TOKENS - 1,
                            pattern=[[TOKENS, GROUP], [0, TOKENS]], channel_multiplier=-1)
            g.affine_select(out=negsel[:, :, :], in_=negsel[:, :, :].bitcast(F32), compare_op=ALU.not_equal,
                            fill=-1.0, base=-32, pattern=[[-1, HEADS], [0, FEATURES]], channel_multiplier=1)
            g.iota(slot_row[:, :], pattern=[[1, max(CAP)]], base=0, channel_multiplier=0,
                   allow_small_or_imprecise_dtypes=True)
            g.iota(expert_id[:, :], pattern=[[1, 10]], base=0, channel_multiplier=0,
                   allow_small_or_imprecise_dtypes=True)
            for r in range(2):
                g.iota(slot_col[:, r, :], pattern=[[ST[r], 2]], base=0, channel_multiplier=1,
                       allow_small_or_imprecise_dtypes=True)
            g.tensor_copy(ident_b[:, :], ident[:, :]).then_inc(const, 1)
            pool.wait_ge(proj_high, 1)
            g.tensor_tensor(bd_low[:, :], bdiag[:, :], bd_high[:, :].bitcast(F32), ALU.subtract)
            g.tensor_tensor(bd2_low[:, :], bdiag2[:, :], bd2_high[:, :].bitcast(F32),
                            ALU.subtract).then_inc(proj_low, 1)

            def low_parts(n, b, up_width):
                pool.wait_ge(hi_up, n + 1)
                g.tensor_tensor(w_low[:, b, 0:up_width], raw_main[:, b, 0:up_width],
                                w_high[:, b, 0:up_width].bitcast(F32), ALU.subtract).then_inc(lo_up, 1)
                pool.wait_ge(hi_dn, n + 1)
                g.tensor_tensor(d_low[:, b, :], raw_main[:, b, up_width:up_width + GW],
                                d_high[:, b, :].bitcast(F32), ALU.subtract).then_inc(lo_dn, 1)

            def make_selector(stage):
                pool.wait_ge(tok_split, stage)
                c.link(g.memset(pick_row[:, :, :].bitcast(F32), 0.0))
                g.affine_select(out=pick_row[:, :, :], in_=pick_row[:, :, :].bitcast(F32),
                                compare_op=ALU.not_equal, fill=1.0, base=0,
                                pattern=[[-1, EXPERTS], [0, 128]], channel_multiplier=1).then_inc(pick_ready, 1)

            def further_low(r, q, k):
                i = q * EXPERTS + k
                x, width = further[r], (UP, FF)[r]
                pool.wait_ge(x["high"], i + 1)
                g.tensor_tensor(w_low[:, 0, 0:width], raw_main[:, 0, 0:width], w_high[:, 0, 0:width].bitcast(F32),
                                ALU.subtract)
                g.tensor_tensor(d_low[:, 0, :], raw_main[:, 0, width:width + GW], d_high[:, 0, :].bitcast(F32),
                                ALU.subtract).then_inc(x["low"], 1)

            low_parts(0, 0, FF)
            make_selector(1)
            low_parts(1, 1, UP)
            low_parts(2, 0, UP)
            with pool.Fori(0, EXPERTS // 2) as p:
                for b in range(2):
                    low_parts(3 + 2 * p + b, 1 - b, UP)
            low_parts(11, 1, FF)
            further_rounds(pool, 0, further_low)
            pool.wait_ge(a_hi, 1)
            g.tensor_tensor(a_low[:, :], a_raw[:, :], a_high[:, :].bitcast(F32), ALU.subtract).then_inc(a_lo, 1)
            make_selector(4)
            with pool.Fori(0, EXPERTS // 2) as p:
                for b in range(2):
                    low_parts(12 + 2 * p + b, b, FF)
            further_rounds(pool, 1, further_low)

        @block.tensor
        def _(pe):
            mm = nc.tensor.matmul

            def five(out_ap, w3, x4, start, stop):
                wh, wl, wr = w3
                xh, xhr, xl, xlr = x4
                pairs = [(wh, xh), (wh, xl), (wl, xh), (wr, xhr), (wr, xlr)]
                for i, (w, x) in enumerate(pairs):
                    last = mm(out_ap, w, x, start=start and i == 0, stop=stop and i == 4, skip_group_check=True)
                return last

            def transpose(out_ap, in_ap, parts=TT):
                return mm(out_ap, in_ap, ident[0:parts, 0:parts], start=True, stop=True, is_transpose=True,
                          skip_group_check=True)

            def keep_warm(groups, bank):
                with pe.Fori(0, groups):
                    for _i in range(8):
                        mm(PS[:, bank, 0:128], ident_b[:, :], ident_b[:, :], start=True, stop=True,
                           skip_group_check=True)

            pe.wait_ge(const, 1)
            pe.wait_ge(tok_in, 32)
            for kt in range(KT):
                pe.wait_ge(patch_in[kt], 16)
                for t in range(NT):
                    mm(PS[0:TT, 3 + t, 0:D], patch_sb[:, kt, cols(t)], tokw_sb[:, kt, :], start=kt == 0, stop=False)
            for t in range(NT):
                mm(PS[0:TT, 3 + t, 0:D], prow[0:1, :, :].rearrange("p a b -> p (a b)"), tokb_sb[0:1, :],
                   start=False, stop=True).then_inc(embedded, 1)
            keep_warm(WARM[0], 0)
            pe.wait_ge(y_ready, 1)
            for t in range(NT):
                transpose(PS[:, 3 + t, 0:TT], xn[:, t, 0:D0])
                transpose(PS[0:D1, 3 + t, 128:128 + TT], xn[:, t, D0:D]).then_inc(yt_done, 1)
            keep_warm(WARM[1], 0)
            pe.wait_ge(yt_ready, NT)
            pe.wait_ge(proj_low, 1)
            for t in range(NT):
                a, b = ((3, 4), (5, 6))[t % 2]
                if t >= 2:
                    pe.wait_ge(u_max, t - 1)
                for i, (y, w) in enumerate(((y_high, bd_high), (y_low, bd_high), (y_high, bd_low))):
                    mm(PS[0:TT, a, :], y[:, cols(t)], w[:, :], start=i == 0, stop=i == 2)
                mm(PS[0:TT, b, 0:256], y_rest[:, cols(t)], bd2_high[:, :], start=True, stop=False)
                mm(PS[0:TT, b, 0:256], y_rest[0:D1, cols(t)], bd2_low[0:D1, :], start=False,
                   stop=True).then_inc(u_done, 1)
            pe.wait_ge(u_max, NT)
            pe.wait_ge(diag_ready, 1)
            for t in range(NT):
                for w in range(2):
                    bank, at = ((7, 0)[w], t * TT) if t < 4 else (1, w * 128)
                    last = transpose(PS[0:HEADS, bank, at:at + TT], md[:, w, t, :])
            last.then_inc(mdt_done, 1)
            keep_warm(WARM[2], 2)
            pe.wait_ge(q_bias, 1)

            def features(c, between):
                for w, bias in ((0, bq), (1, bk)):
                    if c == 0 and w == 1:
                        pe.wait_ge(bias_ready, 1)
                    for half, (lo, hi) in enumerate(((0, HX), (HX, TX))):
                        i = 2 * w + half
                        n = 4 * c + i
                        if n >= 3:
                            pe.wait_ge(exp_done, n - 2)
                        o = PS[:, 3 + n % 3, 0:hi - lo]
                        at = slice(c % 4 * 128, (c % 4 + 1) * 128)
                        if c < 4:
                            mm(o, bd_high[:, at], y_high[:, lo:hi], start=True, stop=False)
                            mm(o, bd_high[:, at], y_low[:, lo:hi], start=False, stop=False)
                            mm(o, bd_low[:, at], y_high[:, lo:hi], start=False, stop=False)
                        else:
                            mm(o, bd2_high[:, at], y_rest[:, lo:hi], start=True, stop=False)
                            mm(o, bd2_low[0:D1, at], y_rest[0:D1, lo:hi], start=False, stop=False)
                        mm(o, negsel[:, 2 * c:2 * c + 2, :].rearrange("h a f -> h (a f)"), bias[:, lo:hi],
                           start=False, stop=True).then_inc(feat_done, 1)
                        between(i)

            def products(c):
                def product(j, t):
                    rows_ = slice(64 * j, 64 * j + 64)
                    bank, at = (j, t * TT) if t < 4 else (7, j * TT)
                    return mm(PS[0:TT, bank, at:at + TT], qkf[rows_, c % 2, 1, cols(t)],
                              qkf[rows_, c % 2, 0, cols(t)], start=True, stop=True)

                product(0, 4).then_inc(tail_done, 1)
                for t in range(4):
                    for j in range(2):
                        product(j, t)
                pe.wait_ge(tail_done, c + 1)
                product(1, 4).then_inc(a_done, 1)

            def with_values(c, part):
                if c < 0 or part < 0:
                    return
                if part == 0:
                    pe.wait_ge(mask_done, 3 * c + 3)
                    if c == 0:
                        pe.wait_ge(vaug_ready, 1)
                    elif c % 2 == 0:
                        pe.wait_ge(ctx_ready, c // 2)
                for t in range(2 * part, min(2 * part + 2, NT)):
                    for j in range(2):
                        bank, at, row = (2, t * TT, (2 * c + j) % 4 * 32) if t < 4 else (6, 0, (2 * c + j) % 4 * 32)
                        last = mm(PS[row:row + 32, bank, at:at + TT], vaug[:, t, 2 * c + j, :],
                                  am[:, c % 2, j, t, :], start=True, stop=True, skip_group_check=True)
                if part == 2:
                    last.then_inc(av_done, 1)

            features(0, lambda i: None)
            for c in range(HEADS // 2):
                pe.wait_ge(eps_done, 2 * c + 2)
                if c:
                    pe.wait_ge(mask_done, 3 * c)
                products(c)
                if c < HEADS // 2 - 1:
                    features(c + 1, lambda i: with_values(c - 1, i - 1))
                else:
                    for i in range(3):
                        with_values(c - 1, i)
            for i in range(3):
                with_values(HEADS // 2 - 1, i)
            pe.wait_ge(exp_done, 2 * HEADS)
            for t in range(NT):
                for g in range(HEADS // 4):
                    pe.wait_ge(ctx_ready, g + 1)
                    last = transpose(PS[0:TT, CTX_BANKS[t], g * 128:(g + 1) * 128], ctx_t[:, g, cols(t)], 128)
                last.then_inc(ctx_done, 1)

            def to_features(stage):
                pe.wait_ge(tok_split, stage + 1)
                for t in range(NT):
                    for j in range(4):
                        last = transpose(PS[:, 3 + t, j * TT:(j + 1) * TT], xtok[:, t, j, :].bitcast(F32))
                    last.then_inc(xt_done, 1)

            def await_xt(stage):
                pe.wait_ge(xt_act, 3 * (stage + 1))
                pe.wait_ge(xt_vec, 2 * (stage + 1))

            def clear_acc():
                for i in range(3):
                    mm(PS[0:TT, i, :], zeros_b[:, 0:TT], zeros_b[:, :], start=True, stop=True, skip_group_check=True)

            def w_slices(b, at):
                return [w[:, b, at:at + 128] for w in (w_high, w_low, w_rest)]

            def step(b, s, pair, x4, width, gated, done=gu_done, between=None):
                for bank, base in ((GATE[pair], 0), (UPB[pair], FF)) if gated else ((GATE[pair], 0),):
                    for i in range(2):
                        last = five(PS[:, bank, i * width:(i + 1) * width], w_slices(b, base + (2 * s + i) * 128),
                                    x4, True, True)
                        if base + i == 0 and between is not None:
                            between()
                last.then_inc(done, 1)

            def down(out_ap, b, hb, at, n, start):
                for i in range(FC):
                    for j, (hp, dp) in enumerate(((h_high, d_high), (h_high, d_low), (h_lowp, d_high))):
                        last = mm(out_ap, hp[:, hb, i, at:at + n], dp[:, b, i * D:(i + 1) * D],
                                  start=start and i == 0 and j == 0, stop=i == FC - 1 and j == 2,
                                  skip_group_check=True)
                return last

            def dense_down(m, n):
                pe.wait_ge(hi_dn, n + 1)
                pe.wait_ge(lo_dn, n + 1)
                pe.wait_ge(low_done, 3 * (m + 1))
                start, width = BLOCKS[m % NB if m < M_ROUTED0 else m - M_COMMON]
                for t, at, k in tiles_of(start, width):
                    last = down(acc(t)[0:k], buf_of(n), m % 2, at, k, False)
                last.then_inc(down_done, 1)

            def dense(m, n, gated, before, extra):
                start, width = BLOCKS[m % NB if m < M_ROUTED0 else m - M_COMMON]
                x4 = [xt[:, j, start:start + width] for j in range(4)]
                for s in range(STEPS):
                    g = 3 * m + s
                    if s == 0:
                        pe.wait_ge(hi_up, n + 1)
                        pe.wait_ge(lo_up, n + 1)
                        pe.wait_ge(rem_lo, n + 1)
                    if g >= 2:
                        pe.wait_ge(act_done, g - 1)
                        if g - 1 > SW0:
                            pe.wait_ge(up_read, min(g - 1, 3 * M_COMMON) - SW0)
                    step(buf_of(n), s, g % 2, x4, width, gated, between=lambda: extra(m, s, 0))
                    if s == 0 and before is not None:
                        dense_down(*before)
                    extra(m, s, 1)

            def nothing(m, s, part):
                pass

            keep_warm(WARM[3], YB)
            to_features(0)
            clear_acc()
            await_xt(0)
            for m in range(NB):
                dense(m, 0, False, (m - 1, 0) if m else None, nothing)
            dense_down(NB - 1, 0)

            def router(r):
                pe.wait_ge(rw_ready, 1)
                for t in range(NT):
                    last = router_tile(r, t)
                last.then_inc(logit_done, 1)

            def router_tile(r, t):
                o = PS[0:TT, YB, t * 10:(t + 1) * 10]
                xh, xhr, xl, xlr = [xt[:, j, cols(t)] for j in range(4)]
                pairs = [(xh, 0), (xl, 0), (xh, 1), (xhr, 2), (xlr, 2)]
                for i, (x, w) in enumerate(pairs):
                    last = mm(o, x, rw[:, r, w, :], start=i == 0, stop=i == 4, skip_group_check=True)
                return last

            def ranks(r):
                def by_expert(t, at):
                    o = PS[0:EXPERTS, YB, at:at + TT]
                    mm(o, farb[:, t, :], ident_b[0:TT, 0:TT], start=True, stop=False, skip_group_check=True)
                    for i in range(t):
                        mm(o, maskb[:, i, :], ones_b[:, :], start=False, stop=False, skip_group_check=True)
                    return mm(o, maskb[:, t, :], tri[:, :], start=False, stop=True, skip_group_check=True)

                pe.wait_ge(mask_ready, r + 1)
                for t in range(4):
                    last = by_expert(t, t * TT)
                last.then_inc(rank_done, 1)
                pe.wait_ge(rank_read, 2 * r + 1)
                by_expert(4, 0)
                for t in range(NT):
                    o = PS[0:TT, YB, 128 + t * EXPERTS:128 + (t + 1) * EXPERTS]
                    mm(o, ident_b[0:TT, 0:TT], farb[:, t, :], start=True, stop=False, skip_group_check=True)
                    for i in range(t):
                        mm(o, ones_b[:, :], maskb[:, i, :], start=False, stop=False, skip_group_check=True)
                    mm(o, tri[:, :], maskb[:, t, :], start=False, stop=True, skip_group_check=True)
                for t in range(NT):
                    last = mm(PS[0:TT, YB, 192:192 + EXPERTS], ones_b[:, :], maskb[:, t, :], start=t == 0,
                              stop=t == NT - 1, skip_group_check=True)
                last.then_inc(rank_done, 1)

            def spread(r, i):
                if i == 0:
                    pe.wait_ge(pick_ready, r + 1)
                    pe.wait_ge(rank_read, 2 * r + 2)
                else:
                    pe.wait_ge(all_read, 2 * EXPERTS * r + i)
                e, half = i // 2, i % 2
                mm(PS[:, YB, 0:HX], pick_row[:, e, :], rank_t[:, half * HX:(half + 1) * HX],
                   start=True, stop=True).then_inc(all_done, 1)

            def extras0(m, s, part):
                g = 3 * m + s - SW0
                if (g, part) == (1, 1):
                    ranks(0)
                if 5 <= g < 13:
                    spread(0, 2 * (g - 5) + part)

            def weights_by_expert():
                for t in range(4):
                    last = transpose(PS[0:EXPERTS + 1, YB, cols(t)], comb[:, t, 0:EXPERTS + 1])
                last.then_inc(comb_done, 1)
                pe.wait_ge(comb_read, 1)
                transpose(PS[0:EXPERTS + 1, YB, 0:TT], comb[:, 4, 0:EXPERTS + 1]).then_inc(comb_done, 1)
                pe.wait_ge(comb_read, 2)

            def extras1(m, s, part):
                g = 3 * (m - M_COMMON) + s
                if (g, part) == (1, 0):
                    ranks(1)
                    pe.wait_ge(rank_read, 4)
                    weights_by_expert()
                if g >= 1:
                    spread(1, 2 * (g - 1) + part)

            def gather_tokens(r, b):
                cap, st = CAP[r], ST[r]
                for j in range(4):
                    bank, at = (GATE[1], UPB[1])[j // 2], (j % 2) * cap
                    for t in range(NT):
                        mm(PS[:, bank, at:at + cap], xtok[:, t, j, :], gat[:, b, t, 0:cap],
                           start=t == 0, stop=t == NT - 1, skip_group_check=True)
                for i in range(STILES[r]):
                    for t in range(NT):
                        last = mm(PS[0:32, (GATE[1], UPB[1])[i], 2 * cap:2 * cap + st], wcur[:, b, t, :],
                                  gat[:, b, t, i * st:(i + 1) * st], start=t == 0, stop=t == NT - 1,
                                  skip_group_check=True)
                return last

            def weight_columns(r):
                st = ST[r]
                for i in range(STILES[r]):
                    mm(PS[0:st, YB, 2 * D + 2 * i:2 * D + 2 * i + 2], w_row[:, i * st:(i + 1) * st], ones_f[:, :],
                       start=True, stop=True, skip_group_check=True)

            def gather(r, k, b, g):
                pe.wait_ge(gat_ready, EXPERTS * r + k + 1)
                pe.wait_ge(act_done, g)
                if r == 0:
                    pe.wait_ge(up_read, g - SW0)
                gather_tokens(r, b).then_inc(gathered, 1)

            def scatter(r, k, last_one=False):
                pe.wait_ge(y_split, EXPERTS * r + k + 1)
                pe.wait_ge(sca_ready, EXPERTS * r + k + 1)
                st = ST[r]
                for t in range(NT):
                    for i in range(STILES[r]):
                        for y in (y_h, y_l):
                            last = mm(acc(t), sca[0:st, i, cols(t)], y[0:st, i, :], start=False, stop=False,
                                      skip_group_check=True)
                last.then_inc(scattered, 1)

            def expert(r, k, b, first, final):
                n0, m0 = ((3, M_ROUTED0), (12, M_ROUTED1))[r]
                n, m = n0 + k, m0 + k
                g = 3 * m
                wb = (n0 + b) % 2
                cap, st, gated = CAP[r], ST[r], r == 0
                x4 = [xg[:, j, 0:cap] for j in range(4)]
                pe.wait_ge(hi_up, n + 1)
                pe.wait_ge(lo_up, n + 1)
                pe.wait_ge(rem_lo, n + 1)
                pe.wait_ge(xg_ready, EXPERTS * r + k + 1)
                pe.wait_ge(act_done, g)
                if gated:
                    pe.wait_ge(up_read, g - SW0)
                step(wb, 0, 0, x4, cap, gated)
                if not first:
                    scatter(r, k - 1)
                step(wb, 1, 1, x4, cap, gated)
                if not first:
                    pe.wait_ge(y_split, EXPERTS * r + k)
                elif r == 1:
                    pe.wait_ge(y_split, EXPERTS)
                weight_columns(r)
                pe.wait_ge(act_done, g + 1)
                if gated:
                    pe.wait_ge(up_read, g + 1 - SW0)
                step(wb, 2, 0, x4, cap, gated)
                if not final:
                    gather(r, k + 1, 1 - b, g + 2)
                pe.wait_ge(hi_dn, n + 1)
                pe.wait_ge(lo_dn, n + 1)
                pe.wait_ge(low_done, g + 3)
                for i in range(STILES[r]):
                    last = down(PS[0:st, YB, i * D:(i + 1) * D], wb, m % 2 if isinstance(m, int) else (m0 + b) % 2,
                                i * st, st, True)
                last.then_inc(down_done, 1)

            def experts(r):
                for b in range(2):
                    expert(r, b, b, b == 0, False)
                with pe.Fori(1, EXPERTS // 2 - 1) as p:
                    for b in range(2):
                        expert(r, 2 * p + b, b, False, False)
                for b in range(2):
                    expert(r, EXPERTS - 2 + b, b, False, b == 1)
                scatter(r, EXPERTS - 1)
                mm(acc(0), zeros_b[:, 0:TT], zeros_b[:, 0:D], start=False, stop=False,
                   skip_group_check=True).then_inc(further[r]["scattered"], 1)
                further_rounds(pe, r, further_unit)
                mm(acc(0), zeros_b[:, 0:TT], zeros_b[:, 0:D], start=False, stop=True,
                   skip_group_check=True).then_inc(mixed, 1)

            def further_unit(r, q, k):
                i = q * EXPERTS + k
                x, cap, st = further[r], CAP[r], ST[r]
                pe.wait_ge(x["table"], i + 1)
                gather_tokens(r, 0).then_inc(x["gathered"], 1)
                pe.wait_ge(x["tokens"], i + 1)
                pe.wait_ge(x["low"], i + 1)
                pe.wait_ge(x["rest"], i + 1)
                x4 = [xg[:, j, 0:cap] for j in range(4)]
                for s in range(STEPS):
                    step(0, s, 0, x4, cap, r == 0, x["products"])
                    pe.wait_ge(x["hidden"], STEPS * i + s + 1)
                weight_columns(r)
                for n in range(STILES[r]):
                    last = down(PS[0:st, YB, n * D:(n + 1) * D], 0, 0, n * st, st, True)
                last.then_inc(x["down"], 1)
                pe.wait_ge(x["outputs_split"], i + 1)
                for t in range(NT):
                    for n in range(STILES[r]):
                        for y in (y_h, y_l):
                            last = mm(acc(t), sca[0:st, n, cols(t)], y[0:st, n, :], start=False, stop=False,
                                      skip_group_check=True)
                last.then_inc(x["scattered"], 1)

            keep_warm(WARM[4], YB)
            to_features(1)
            pe.wait_ge(acc_read, 1)
            clear_acc()
            await_xt(1)
            router(0)
            for m in range(NB, M_ROUTED0):
                n = m // NB
                dense(m, n, True, (m - 1, (m - 1) // NB) if m > NB else None, extras0)
            gather(0, 0, 0, 3 * M_ROUTED0 - 1)
            dense_down(M_ROUTED0 - 1, 2)
            pe.wait_ge(all_read, 16)
            keep_warm(WARM[7], YB)
            experts(0)

            keep_warm(WARM[5], YB)
            to_features(2)
            await_xt(2)
            pe.wait_ge(a_lo, 1)
            pe.wait_ge(a_lor, 1)

            def a_slices(at, n):
                return [w[:, at:at + n] for w in (a_high, a_low, a_rest)]

            i = 0
            for w in range(2):
                for c in range(QK_CHUNKS):
                    for half in range(2):
                        if i >= 4:
                            pe.wait_ge(qk_mid, i - 3)
                        five(PS[:, 3 + i % 4, 0:HX], a_slices((w * QK_CHUNKS + c) * 128, 128),
                             [xt[:, j, half * HX:(half + 1) * HX] for j in range(4)], True, True).then_inc(qk_done, 1)
                        i += 1
            pe.wait_ge(acc_read, 2)
            for t in range(NT):
                xh, xhr, xl, xlr = [xt[:, j, cols(t)] for j in range(4)]
                wh, wl, wr = a_slices(V_COL, D)
                for i, (x, w) in enumerate([(xh, wh), (xl, wh), (xh, wl), (xhr, wr), (xlr, wr)]):
                    last = mm(acc(t), x, w, start=i == 0, stop=i == 4, skip_group_check=True)
            last.then_inc(v_done, 1)
            pe.wait_ge(qk_spiked, 12)
            pe.wait_ge(v_ready, 1)
            for t in range(NT):
                if t:
                    pe.wait_ge(s_masked, 4 * t)
                for c in range(QK_CHUNKS):
                    for j in range(4):
                        last = mm(PS[0:TT, 3 + j, c * TT:(c + 1) * TT], qk_spk[32 * j:32 * j + 32, 1, c, cols(t)],
                                  qk_spk[32 * j:32 * j + 32, 0, c, cols(t)], start=True, stop=True,
                                  skip_group_check=True)
                last.then_inc(s_done, 1)
                pe.wait_ge(s_masked, 4 * t + 4)
                for head in range(HEADS):
                    last = mm(acc(t)[:, head * HD:(head + 1) * HD], am1[:, head % 4, head // 4, :],
                              v_spk[:, t, head * HD:(head + 1) * HD], start=True, stop=True, skip_group_check=True)
                last.then_inc(xa_done, 1)
            pe.wait_ge(xs_ready, 1)
            for t in range(NT):
                for j in range(2):
                    last = transpose(PS[:, 3 + t, j * TT:(j + 1) * TT], xs[:, t, j, :])
                last.then_inc(xst_done, 1)
            pe.wait_ge(xst_ready, NT)
            for t in range(NT):
                wh, wl, wr = a_slices(V_COL + D, D)
                for i, (j, w) in enumerate([(0, wh), (0, wl), (1, wr)]):
                    last = mm(acc(t), xt[:, j, cols(t)], w, start=i == 0, stop=i == 2, skip_group_check=True)
            last.then_inc(o_done, 1)

            keep_warm(WARM[6], YB)
            to_features(3)
            clear_acc()
            await_xt(3)
            router(1)
            for m in range(M_COMMON, M_ROUTED1):
                dense(m, 11, False, (m - 1, 11) if m > M_COMMON else None, extras1)
            gather(1, 0, 0, 3 * M_ROUTED1)
            dense_down(M_ROUTED1 - 1, 11)
            pe.wait_ge(all_read, 32)
            pe.wait_ge(acc_read, 3)
            pe.wait_ge(b2_in, 16)
            clear_acc()
            for t in range(NT):
                mm(acc(t), comb_t[:, cols(t)], b2_sb[:, :], start=False, stop=False, skip_group_check=True)
            keep_warm(WARM[8], YB)
            experts(1)

        @block.scalar
        def _(act):
            s = nc.scalar
            act.dma_start(tokb_sb[:, :], tok_b).then_inc(tok_in, 16)
            for i in range(GROUP):
                act.dma_start(clspos_sb[i * TOKENS:(i + 1) * TOKENS, :], cls_pos).then_inc(clspos_in, 16)
            act.dma_start(row_sb[:, :, :].rearrange("p a d -> p (a d)"),
                          rows.rearrange("a d -> (a d)").partition_broadcast(TT)).then_inc(rows_in, 16)
            act.wait_ge(pool_step, 1)
            for head in range(HEADS):
                tile_, i = (bdiag, head) if head < 8 else (bdiag2, head - 8)
                act.dma_start(tile_[i * HD:(i + 1) * HD, i * FEATURES:(i + 1) * FEATURES],
                              proj_t).then_inc(proj_in, 16)
            for i in range(HEADS - 8):
                act.dma_start(bdiag2[D1 + i * HD:D1 + (i + 1) * HD, i * FEATURES:(i + 1) * FEATURES],
                              proj_t).then_inc(proj_in, 16)
            act.dma_start(rw_raw[:, :, :], router_w[0:D0]).then_inc(router_in, 16)
            act.dma_start(rw_rraw[:, :, :], router_w[D0:D]).then_inc(router_in, 16)
            act.dma_start(rb[:, :], router_b.partition_broadcast(TT)).then_inc(router_in, 16)
            act.dma_start(b2_sb[:, :], moe_b2).then_inc(b2_in, 16)

            def deviation(i):
                act.wait_ge(var_ready, i + 1)
                s.activation(std[:, :], veps[:, :], ACT.Sqrt).then_inc(std_ready, 1)

            act.wait_ge(proj_in, 16 * (2 * HEADS - 8))
            s.activation(bd_high[:, :], bdiag[:, :], ACT.Copy)
            s.activation(bd2_high[:, :], bdiag2[:, :], ACT.Copy).then_inc(proj_high, 1)
            deviation(0)
            deviation(1)
            act.wait_ge(y_ready, 1)
            for t in range(NT):
                act.wait_ge(yt_done, t + 1)
                s.activation(y_high[:, cols(t)], PS[:, 3 + t, 0:TT], ACT.Copy)
                s.activation(y_rest[0:D1, cols(t)], PS[0:D1, 3 + t, 128:128 + TT], ACT.Copy).then_inc(yt_high, 1)
            act.wait_ge(const, 1)
            s.activation(vaug[:, :, :, 0:HD], xn[:, :, :].rearrange("p t (h d) -> p t h d", d=HD),
                         ACT.Copy).then_inc(vaug_ready, 1)
            act.wait_ge(router_in, 48)
            s.activation(rw[:, :, 0, :], rw_raw[:, :, :], ACT.Copy)
            s.activation(rw[0:D1, :, 2, :], rw_rraw[:, :, :], ACT.Copy).then_inc(rw_high, 1)

            def high_up(n, b, fill, width, done):
                act.wait_ge(raw_in[b], 32 * (fill + 1))
                if done is not None:
                    act.wait_ge(down_done, done)
                if width == FF:
                    s.activation(bias1[:, b, :], raw_main[:, b, FF + GW:MAIN_G], ACT.Copy)
                s.activation(w_high[:, b, 0:width], raw_main[:, b, 0:width], ACT.Copy).then_inc(hi_up, 1)

            def high_rest(b, width):
                s.activation(w_rest[0:D1, b, 0:width], raw_rem[:, b, 0:width], ACT.Copy).then_inc(hi_rest, 1)

            def high_down(b, width):
                s.activation(d_high[:, b, :], raw_main[:, b, width:width + GW], ACT.Copy).then_inc(hi_dn, 1)

            high_up(0, 0, 0, FF, None)
            high_rest(0, FF)
            high_down(0, FF)

            def context(g):
                act.wait_ge(av_done, 2 * g + 2)
                s.activation(ctx_t[:, g, 0:4 * TT], PS[:, 2, 0:4 * TT], ACT.Copy)
                s.activation(ctx_t[:, g, 4 * TT:TP], PS[:, 6, 0:TT], ACT.Copy).then_inc(ctx_ready, 1)

            def exps(c):
                for w in range(2):
                    for half, (lo, hi) in enumerate(((0, HX), (HX, TP))):
                        i = 2 * w + half
                        act.wait_ge(feat_done, 4 * c + i + 1)
                        if c >= 2:
                            act.wait_ge(a_done, c - 1)
                        s.activation(qkf[:, c % 2, w, lo:hi], PS[:, 3 + (4 * c + i) % 3, 0:hi - lo], ACT.Exp,
                                     scale=0.5).then_inc(exp_done, 1)

            exps(0)
            for c in range(HEADS // 2):
                if c < HEADS // 2 - 1:
                    exps(c + 1)
                if c and c % 2 == 0:
                    context(c // 2 - 1)
            context(HEADS // 4 - 1)

            def xt_out(stage):
                for t in (0, 2, 4):
                    act.wait_ge(xt_done, NT * stage + t + 1)
                    s.activation(xt[:, :, cols(t)], chunk2(PS[:, 3 + t, 0:4 * TT], TT), ACT.Copy).then_inc(xt_act, 1)

            def hidden(m, n, b, s_, pair, ring, width, gated):
                g = 3 * m + s_
                act.wait_ge(gu_done, g + 1)
                if not (isinstance(g, int) and g < 2):
                    act.wait_ge(low_done, g - 1)
                if gated:
                    s.activation(act_out[:, ring, 0:2 * width], PS[:, GATE[pair], 0:2 * width],
                                 ACT.Silu).then_inc(act_done, 1)
                    return
                act.wait_ge(hi_up, n + 1)
                for i in range(2):
                    at = slice(i * width, (i + 1) * width)
                    last = s.activation(act_out[:, ring, at], PS[:, GATE[pair], at], ACT.Gelu,
                                        bias=bias1[:, b, 2 * s_ + i:2 * s_ + i + 1])
                last.then_inc(act_done, 1)

            def spread_out(r, i):
                act.wait_ge(all_done, 2 * EXPERTS * r + i + 1)
                e, half = i // 2, i % 2
                s.activation(rank_all[:, e, half * HX:(half + 1) * HX], PS[:, YB, 0:HX], ACT.Copy).then_inc(all_read, 1)

            def tokens_out(r):
                cap, st = CAP[r], ST[r]
                for i in range(STILES[r]):
                    s.activation(w_row[:, i * st:(i + 1) * st], PS[0:32, (GATE[1], UPB[1])[i], 2 * cap:2 * cap + st],
                                 ACT.Copy)
                s.activation(xg[:, 0:2, 0:cap], chunk2(PS[:, GATE[1], 0:2 * cap], cap), ACT.Copy)
                return s.activation(xg[:, 2:4, 0:cap], chunk2(PS[:, UPB[1], 0:2 * cap], cap), ACT.Copy)

            def gathered_out(r, k):
                act.wait_ge(gathered, EXPERTS * r + k + 1)
                tokens_out(r).then_inc(xg_ready, 1)

            def dense(m, n, gated, extra):
                width = BLOCKS[m % NB if m < M_ROUTED0 else m - M_COMMON][1]
                for i in range(STEPS):
                    g = 3 * m + i
                    hidden(m, n, n % 2, i, g % 2, g % 2, width, gated)
                    at = g - (3 * NB * n if m < M_ROUTED0 else 3 * M_COMMON)
                    nb, next_width = (n + 1) % 2, UP if 1 <= n + 1 <= 10 else FF
                    if at == 1:
                        high_up(n + 1, nb, (n + 1) // 2, next_width, None if n == 0 else blocks_done(n - 1))
                    if at == 2:
                        high_rest(nb, next_width)
                    if at == 4:
                        high_down(nb, next_width)
                    extra(m, i)

            def nothing(m, i):
                pass

            def extras0(m, i):
                g = 3 * m + i - SW0
                if 5 <= g < 13:
                    spread_out(0, 2 * (g - 5))
                    spread_out(0, 2 * (g - 5) + 1)

            def extras1(m, i):
                g = 3 * (m - M_COMMON) + i
                if g >= 1:
                    spread_out(1, 2 * (g - 1))
                    spread_out(1, 2 * (g - 1) + 1)

            def expert(r, k, p, b, final):
                n0, m0 = ((3, M_ROUTED0), (12, M_ROUTED1))[r]
                n, m = n0 + k, m0 + k
                wb, gated, cap = (n0 + b) % 2, r == 0, CAP[r]
                ring = (m0 + b) % 2
                more = not final or r == 0
                width = UP if r == 0 and not final else FF
                nb = 1 - wb
                if more:
                    high_up(n + 1, nb, (n0 + 1 + b) // 2 + p, width, m)
                hidden(m, n, wb, 0, 0, ring, cap, gated)
                if more:
                    high_rest(nb, width)
                hidden(m, n, wb, 1, 1, 1 - ring, cap, gated)
                if more:
                    high_down(nb, width)
                hidden(m, n, wb, 2, 0, ring, cap, gated)
                if not final:
                    gathered_out(r, k + 1)

            def experts(r):
                for b in range(2):
                    expert(r, b, 0, b, False)
                with act.Fori(1, EXPERTS // 2 - 1) as p:
                    for b in range(2):
                        expert(r, 2 * p + b, p, b, False)
                for b in range(2):
                    expert(r, EXPERTS - 2 + b, EXPERTS // 2 - 1, b, b == 1)
                further_rounds(act, r, further_unit)

            def further_unit(r, q, k):
                i = q * EXPERTS + k
                x, cap, width = further[r], CAP[r], (UP, FF)[r]
                act.wait_ge(x["loaded"], 32 * i + 32)
                s.activation(w_high[:, 0, 0:width], raw_main[:, 0, 0:width], ACT.Copy)
                if r:
                    s.activation(bias1[:, 0, :], raw_main[:, 0, FF + GW:MAIN_G], ACT.Copy)
                s.activation(w_rest[0:D1, 0, 0:width], raw_rem[:, 0, 0:width], ACT.Copy)
                s.activation(d_high[:, 0, :], raw_main[:, 0, width:width + GW], ACT.Copy).then_inc(x["high"], 1)
                act.wait_ge(x["high"], i + 1)
                act.wait_ge(x["gathered"], i + 1)
                tokens_out(r).then_inc(x["tokens"], 1)
                for n in range(STEPS):
                    act.wait_ge(x["products"], STEPS * i + n + 1)
                    for c in range(2):
                        at = slice(c * cap, (c + 1) * cap)
                        last = s.activation(act_out[:, 0, at], PS[:, GATE[0], at], ACT.Gelu,
                                            bias=bias1[:, 0, 2 * n + c:2 * n + c + 1]) if r else \
                            s.activation(act_out[:, 0, at], PS[:, GATE[0], at], ACT.Silu)
                    last.then_inc(x["activated"], 1)

            def router(r):
                act.wait_ge(shift_ready, r + 1)
                s.activation(lexp[:, :, :], shifted[:, :, :], ACT.Exp).then_inc(lexp_ready, 1)

            deviation(2)
            xt_out(0)
            for m in range(NB):
                dense(m, 0, False, nothing)
            deviation(3)
            xt_out(1)
            router(0)
            for m in range(NB, M_ROUTED0):
                dense(m, m // NB, True, extras0)
            gathered_out(0, 0)
            experts(0)
            deviation(4)
            act.wait_ge(bn_var, 1)
            s.activation(col_std[:, :], col_ve[:, :], ACT.Sqrt)
            s.activation(row_std[:, :, :], row_ve[:, :, :], ACT.Sqrt).then_inc(bn_std, 1)
            act.wait_ge(a1_in, 32)
            s.activation(a_high[:, :], a_raw[:, :], ACT.Copy)
            s.activation(a_rest[0:D1, :], a_rraw[:, :], ACT.Copy).then_inc(a_hi, 1)
            xt_out(2)
            for t in range(NT):
                act.wait_ge(xst_done, t + 1)
                s.activation(xt[:, 0:2, cols(t)], chunk2(PS[:, 3 + t, 0:2 * TT], TT), ACT.Copy).then_inc(xst_ready, 1)
            deviation(5)
            xt_out(3)
            router(1)
            for m in range(M_COMMON, M_ROUTED1):
                dense(m, 11, False, extras1)
            gathered_out(1, 0)
            experts(1)

        @block.vector
        def _(dve):
            v = nc.vector
            c = Chain(dve, vec)

            def over_tiles(row):
                return row.to_broadcast([TT, NT, D])

            def layernorm(src, dst, i):
                for t in range(NT):
                    c.mark(v.bn_stats(stats[:, t, :], src[:, t, :]))
                c.settle()
                for t in range(NT):
                    c.mark(v.bn_aggr(mv[:, t, :], stats[:, t, :]))
                c.settle()
                v.tensor_scalar(veps[:, :], mv[:, :, 1], LN_EPS, None, ALU.add).then_inc(var_ready, 1)
                dve.wait_ge(std_ready, i + 1)
                c.link(v.reciprocal(rstd[:, :], std[:, :]))
                for t in range(NT):
                    c.mark(v.tensor_scalar(dst[:, t, :], src[:, t, :], mv[:, t, 0:1], rstd[:, t:t + 1],
                                           ALU.subtract, ALU.mult))
                c.settle()

            def split_tokens():
                c.mark(v.tensor_copy(xtok[:, :, 0, :], xn[:, :, 0:D0]))
                for i in range(2):
                    c.mark(v.tensor_copy(xtok[:, :, 1, i * D1:(i + 1) * D1], xn[:, :, D0:D]))
                c.settle()
                v.tensor_tensor(xtok[:, :, 2, :], xn[:, :, 0:D0], xtok[:, :, 0, :].bitcast(F32), ALU.subtract)
                for i in range(2):
                    last = v.tensor_tensor(xtok[:, :, 3, i * D1:(i + 1) * D1], xn[:, :, D0:D],
                                           xtok[:, :, 1, i * D1:(i + 1) * D1].bitcast(F32), ALU.subtract)
                last.then_inc(tok_split, 1)

            def xt_out(stage):
                for t in (1, 3):
                    dve.wait_ge(xt_done, NT * stage + t + 1)
                    v.tensor_copy(xt[:, :, cols(t)], chunk2(PS[:, 3 + t, 0:4 * TT], TT)).then_inc(xt_vec, 1)

            def per_bank(f):
                for bank in range(3):
                    ts = slice(2 * bank, min(2 * bank + 2, NT))
                    last = f(ts, chunk2(PS[0:TT, bank, 0:(ts.stop - ts.start) * D], D))
                return last

            dve.wait_ge(clspos_in, 16 * GROUP)
            for t in range(NT):
                dve.wait_ge(embedded, t + 1)
                c.mark(v.tensor_tensor(h[:, t, :], PS[0:TT, 3 + t, 0:D], clspos_sb[:, :], ALU.add))
            c.settle()
            layernorm(h, x0, 0)
            layernorm(x0, xn, 1)
            dve.wait_ge(rows_in, 16)
            c.link(v.tensor_tensor(xn[:, :, :], xn[:, :, :], over_tiles(row_sb[:, 0:1, :]), ALU.mult))
            v.tensor_tensor(xn[:, :, :], xn[:, :, :], over_tiles(row_sb[:, 1:2, :]), ALU.add).then_inc(y_ready, 1)
            dve.wait_ge(y_ready, 1)
            c.link(v.tensor_tensor(sq[:, :, :], xn[:, :, :], xn[:, :, :], ALU.mult))
            c.link(v.tensor_reduce(md[:, 1, :, :], sq[:, :, :].rearrange("p t (h d) -> p t h d", d=HD), AXX, ALU.add))
            v.tensor_scalar(md[:, 1, :, :], md[:, 1, :, :], 0.25, None, ALU.mult).then_inc(diag_ready, 1)
            for t in range(NT):
                dve.wait_ge(yt_high, t + 1)
                v.tensor_tensor(y_low[:, cols(t)], PS[:, 3 + t, 0:TT], y_high[:, cols(t)].bitcast(F32), ALU.subtract)
                v.tensor_tensor(y_rest[D1:D0, cols(t)], PS[0:D1, 3 + t, 128:128 + TT],
                                y_rest[0:D1, cols(t)].bitcast(F32), ALU.subtract).then_inc(yt_ready, 1)
            for t in range(NT):
                dve.wait_ge(u_done, t + 1)
                a, b = ((3, 4), (5, 6))[t % 2]
                v.tensor_reduce(md[:, 0, t, 0:8], chunk2(PS[0:TT, a, :], FEATURES), AXX, ALU.max)
                v.tensor_reduce(md[:, 0, t, 8:12], chunk2(PS[0:TT, b, 0:256], FEATURES), AXX, ALU.max).then_inc(u_max, 1)
            dve.wait_ge(mdt_done, 1)
            c.mark(v.tensor_copy(mx_t[:, 0:4 * TT], PS[0:HEADS, 7, 0:4 * TT]))
            c.mark(v.tensor_copy(mx_t[:, 4 * TT:TP], PS[0:HEADS, 1, 0:TT]))
            c.mark(v.tensor_copy(dg_t[:, 0:4 * TT], PS[0:HEADS, 0, 0:4 * TT]))
            c.mark(v.tensor_copy(dg_t[:, 4 * TT:TP], PS[0:HEADS, 1, 128:128 + TT]))
            c.settle()
            def split_bias(bias, w):
                c.link(v.tensor_copy(bias[0:HEADS, 0:TP], bsum[:, w, :]))
                return v.tensor_tensor(bias[32:32 + HEADS, 0:TP], bsum[:, w, :], bias[0:HEADS, 0:TP].bitcast(F32),
                                       ALU.subtract)

            c.link(v.tensor_tensor(bsum[:, 0, :], mx_t[:, :], dg_t[:, :], ALU.add))
            split_bias(bq, 0).then_inc(q_bias, 1)
            c.link(v.tensor_reduce(stab[:, :], chunk2(mx_t[:, :], TOKENS), AXX, ALU.max))
            c.link(v.tensor_tensor(chunk2(bsum[:, 1, :], TOKENS), chunk2(dg_t[:, :], TOKENS),
                                   stab[:, :].unsqueeze(2).to_broadcast([HEADS, NT * GROUP, TOKENS]), ALU.add))
            split_bias(bk, 1).then_inc(bias_ready, 1)
            dve.wait_ge(rw_high, 1)
            v.tensor_tensor(rw[:, :, 1, :], rw_raw[:, :, :], rw[:, :, 0, :].bitcast(F32), ALU.subtract)
            v.tensor_tensor(rw[D1:D0, :, 2, :], rw_rraw[:, :, :], rw[0:D1, :, 2, :].bitcast(F32),
                            ALU.subtract).then_inc(rw_ready, 1)

            def rem_low(n, b, width):
                dve.wait_ge(hi_rest, n + 1)
                v.tensor_tensor(w_rest[D1:D0, b, 0:width], raw_rem[:, b, 0:width],
                                w_rest[0:D1, b, 0:width].bitcast(F32), ALU.subtract).then_inc(rem_lo, 1)

            rem_low(0, 0, FF)

            def add_eps(c_):
                for w in range(2):
                    dve.wait_ge(exp_done, 4 * c_ + 2 * w + 2)
                    f = qkf[:, c_ % 2, w, :]
                    v.tensor_scalar(f, f, FEATURE_EPS, None, ALU.add).then_inc(eps_done, 1)

            def masks(c_):
                dve.wait_ge(a_done, c_ + 1)
                if c_ >= 2:
                    dve.wait_ge(av_done, c_ - 1)
                for j in range(2):
                    v.tensor_tensor(am[:, c_ % 2, j, 0:4, :], chunk2(PS[0:TT, j, 0:4 * TT], TT),
                                    bmask[:, :].unsqueeze(1).to_broadcast([TT, 4, TT]),
                                    ALU.mult).then_inc(mask_done, 1)
                v.tensor_tensor(am[:, c_ % 2, :, 4, :], chunk2(PS[0:TT, 7, 0:2 * TT], TT),
                                bmask[:, :].unsqueeze(1).to_broadcast([TT, 2, TT]), ALU.mult).then_inc(mask_done, 1)

            add_eps(0)
            for c_ in range(HEADS // 2):
                masks(c_)
                if c_ < HEADS // 2 - 1:
                    add_eps(c_ + 1)
            def context(t):
                return chunk2(PS[0:TT, CTX_BANKS[t], 0:32 * HEADS], 32)

            for t in range(NT):
                dve.wait_ge(ctx_done, t + 1)
                c.mark(v.reciprocal(rden[:, t, :], context(t)[:, :, HD]))
            c.settle()
            for t in range(NT):
                c.mark(v.tensor_tensor(chunk2(xn[:, t, :], HD), context(t)[:, :, 0:HD],
                                       rden[:, t, :].unsqueeze(2).to_broadcast([TT, HEADS, HD]), ALU.mult))
            c.settle()
            c.link(v.tensor_tensor(x0[:, :, :], x0[:, :, :], xn[:, :, :], ALU.add))
            layernorm(x0, xn, 2)
            c.link(v.tensor_tensor(xn[:, :, :], xn[:, :, :], over_tiles(row_sb[:, 2:3, :]), ALU.mult))
            c.link(v.tensor_tensor(xn[:, :, :], xn[:, :, :], over_tiles(row_sb[:, 3:4, :]), ALU.add))
            split_tokens()
            xt_out(0)
            c.link(v.tensor_tensor(x0[:, :, :], x0[:, :, :], over_tiles(row_sb[:, 4:5, :]), ALU.add))
            c.link(v.tensor_tensor(h[:, :, :], h[:, :, :], x0[:, :, :], ALU.add))

            def hidden(m, s_, hb, ring, pair, width, gated, factor):
                g = 3 * m + s_
                if s_ == 0 and not (isinstance(m, int) and m < 2):
                    dve.wait_ge(down_done, m - 1)
                dve.wait_ge(act_done, g + 1)
                src = act_out[:, ring, 0:2 * width]
                if gated:
                    dve.wait_ge(low_done, g)
                    v.scalar_tensor_tensor(out=prod[:, 0:2 * width], in0=PS[:, UPB[pair], 0:2 * width],
                                           scalar=factor, in1=src, op0=ALU.mult, op1=ALU.mult).then_inc(up_read, 1)
                    dve.wait_ge(up_read, g + 1 - SW0)
                    src = prod[:, 0:2 * width]
                hi_ = h_high[:, hb, 2 * s_:2 * s_ + 2, 0:width]
                v.tensor_copy(hi_, chunk2(src, width)).then_inc(high_done, 1)
                dve.wait_ge(high_done, g + 1)
                v.tensor_tensor(h_lowp[:, hb, 2 * s_:2 * s_ + 2, 0:width], chunk2(src, width), hi_.bitcast(F32),
                                ALU.subtract).then_inc(low_done, 1)

            def dense(m, n, gated, factor):
                width = BLOCKS[m % NB if m < M_ROUTED0 else m - M_COMMON][1]
                for i in range(STEPS):
                    g = 3 * m + i
                    hidden(m, i, m % 2, g % 2, g % 2, width, gated, factor)
                    if g == (3 * NB * n if m < M_ROUTED0 else 3 * M_COMMON) + 3:
                        rem_low(n + 1, (n + 1) % 2, UP if 1 <= n + 1 <= 10 else FF)

            def add_acc(which):
                last = per_bank(lambda ts, a: v.tensor_tensor(h[:, ts, :], h[:, ts, :], a, ALU.add))
                last.then_inc(acc_read, 1)
                dve.wait_ge(acc_read, which)

            def router(r):
                ne = EXPERTS + r
                e_ = slice(0, ne)
                dve.wait_ge(logit_done, r + 1)
                psum = chunk2(PS[0:TT, YB, 0:NT * 10], 10)
                if r:
                    c.link(v.tensor_tensor(logit[:, :, :], psum,
                                           rb[:, :].unsqueeze(1).to_broadcast([TT, NT, 10]), ALU.add))
                else:
                    c.link(v.tensor_copy(logit[:, :, :], psum))
                c.link(v.tensor_reduce(lmax[:, :], logit[:, :, e_], AXX, ALU.max))
                v.tensor_tensor(shifted[:, :, :], logit[:, :, :],
                                lmax[:, :].unsqueeze(2).to_broadcast([TT, NT, 10]), ALU.subtract).then_inc(shift_ready, 1)
                dve.wait_ge(lexp_ready, r + 1)
                c.link(v.tensor_reduce(lsum[:, :], lexp[:, :, e_], AXX, ALU.add))
                c.link(v.reciprocal(linv[:, :], lsum[:, :]))
                c.link(v.tensor_tensor(prob[:, :, e_], lexp[:, :, e_],
                                       linv[:, :].unsqueeze(2).to_broadcast([TT, NT, ne]), ALU.mult))
                for t in range(NT):
                    c.mark(v.max(top8[:, t, :], prob[:, t, e_]))
                c.settle()
                for t in range(NT):
                    c.mark(v.max_index(idx8[:, t, :], top8[:, t, :], prob[:, t, e_]))
                c.settle()
                c.link(v.tensor_copy(idxf[:, :, :], idx8[:, :, :]))

                def chosen(out_, i):
                    c.mark(v.tensor_tensor(out_[:, :, e_], expert_id[:, e_].unsqueeze(1).to_broadcast([TT, NT, ne]),
                                           idxf[:, :, i:i + 1].to_broadcast([TT, NT, ne]), ALU.is_equal))

                def weighted(out_, pick, w):
                    c.link(v.tensor_tensor(out_, pick, w.to_broadcast([TT, NT, pick.shape[2]]), ALU.mult))

                chosen(pick1, 0)
                if r == 0:
                    chosen(pick2, 1)
                    c.settle()
                    c.link(v.tensor_tensor(maskf[:, :, :], pick1[:, :, e_], pick2[:, :, e_], ALU.add))
                    c.link(v.tensor_tensor(lsum[:, :], top8[:, :, 0], top8[:, :, 1], ALU.add))
                    c.link(v.tensor_scalar(lsum[:, :], lsum[:, :], 1e-8, None, ALU.add))
                    c.link(v.reciprocal(linv[:, :], lsum[:, :]))
                    c.link(v.tensor_tensor(topw[:, :, :], top8[:, :, 0:2],
                                           linv[:, :].unsqueeze(2).to_broadcast([TT, NT, 2]), ALU.mult))
                    weighted(comb[:, :, e_], pick1[:, :, e_], topw[:, :, 0:1])
                    weighted(pick1[:, :, e_], pick2[:, :, e_], topw[:, :, 1:2])
                    c.link(v.tensor_tensor(comb[:, :, e_], comb[:, :, e_], pick1[:, :, e_], ALU.add))
                else:
                    c.settle()
                    c.link(v.tensor_copy(maskf[:, :, :], pick1[:, :, 1:ne]))
                    c.link(v.tensor_scalar(c0p[:, :, 0], top8[:, :, 0], -1.0, 1.0, ALU.mult, ALU.add))
                    c.link(v.tensor_tensor(c0p[:, :, 1], top8[:, :, 0], pick1[:, :, 0], ALU.mult))
                    c.link(v.tensor_tensor(c0[:, :], c0p[:, :, 0], c0p[:, :, 1], ALU.add))
                    weighted(comb[:, :, 1:ne], pick1[:, :, 1:ne], top8[:, :, 0:1])
                    c.link(v.tensor_copy(comb[:, :, 0], c0[:, :]))
                c.link(v.tensor_tensor(maskf[:, :, :], maskf[:, :, :],
                                       valid[:, :].unsqueeze(2).to_broadcast([TT, NT, EXPERTS]), ALU.mult))
                v.tensor_copy(maskb[:, :, :], maskf[:, :, :])
                v.tensor_scalar(farb[:, :, :], maskf[:, :, :], -1024.0, 1024.0, ALU.mult, ALU.add).then_inc(mask_ready, 1)
                w = comb[:, :, ne - EXPERTS:ne]
                c.link(v.tensor_copy(wtab[:, :, :, 0], w))
                c.link(v.tensor_tensor(wtab[:, :, :, 1], w, wtab[:, :, :, 0].bitcast(F32), ALU.subtract))
                c.link(v.memset(rank_t[:, TP:TX].bitcast(F32), 0.0))
                dve.wait_ge(rank_done, 2 * r + 1)
                v.tensor_copy(rank_t[:, 0:4 * TT], PS[0:EXPERTS, YB, 0:4 * TT]).then_inc(rank_read, 1)
                dve.wait_ge(rank_done, 2 * r + 2)
                c.mark(v.tensor_copy(rank_t[:, 4 * TT:TP], PS[0:EXPERTS, YB, 0:TT]))
                c.mark(v.tensor_reduce(most[:, :], PS[0:TT, YB, 192:192 + EXPERTS], AXX, ALU.max))
                v.tensor_copy(rank[:, :, :], chunk2(PS[0:TT, YB, 128:128 + NT * EXPERTS], EXPERTS)).then_inc(rank_read, 1)
                dve.wait_ge(rank_read, 2 * r + 2)

            def gather_table(r, k, b):
                cap = CAP[r]
                e = slice(k, k + 1) if isinstance(k, int) else bass.ds(k, 1)
                for t in range(NT):
                    v.tensor_scalar(gat[:, b, t, 0:cap], slot_row[:, 0:cap], rank[:, t, e], None, ALU.is_equal)
                v.tensor_copy(wcur[:, b, :, 0:2], wtab[:, :, e, :].rearrange("p t e w -> p t (e w)").bitcast(F32))\
                 .then_inc(gat_ready, 1)

            def weighted_outputs(r, high, count):
                st = ST[r]
                for i in range(STILES[r]):
                    last = v.tensor_scalar(y_h[0:st, i, :], PS[0:st, YB, i * D:(i + 1) * D], slot_w[0:st, i:i + 1],
                                           None, ALU.mult)
                last.then_inc(high, 1)
                dve.wait_ge(high, count)
                for i in range(STILES[r]):
                    last = v.scalar_tensor_tensor(out=y_l[0:st, i, :], in0=PS[0:st, YB, i * D:(i + 1) * D],
                                                  scalar=slot_w[0:st, i:i + 1], in1=y_h[0:st, i, :].bitcast(F32),
                                                  op0=ALU.mult, op1=ALU.subtract)
                return last

            def expert(r, k, b, first, final):
                n0, m0 = ((3, M_ROUTED0), (12, M_ROUTED1))[r]
                n, m = n0 + k, m0 + k
                cap, st, gated, wb = CAP[r], ST[r], r == 0, (n0 + b) % 2
                ring = (m0 + b) % 2
                e = slice(k, k + 1) if isinstance(k, int) else bass.ds(k, 1)
                hidden(m, 0, ring, ring, 0, cap, gated, 1.0)
                if not final:
                    dve.wait_ge(down_done, m)
                    gather_table(r, k + 1, 1 - b)
                hidden(m, 1, ring, 1 - ring, 1, cap, gated, 1.0)
                if first:
                    dve.wait_ge(all_read, 2 * EXPERTS * (r + 1))
                if not first or r == 1:
                    dve.wait_ge(scattered, EXPERTS * r + k)
                for i in range(STILES[r]):
                    last = v.tensor_scalar(sca[0:st, i, :], rank_all[0:st, e, :].rearrange("p e t -> p (e t)"),
                                           slot_col[0:st, r, i:i + 1], None, ALU.is_equal)
                last.then_inc(sca_ready, 1)
                hidden(m, 2, ring, ring, 0, cap, gated, 1.0)
                if not final or r == 0:
                    rem_low(n + 1, 1 - wb, UP if r == 0 and not final else FF)
                dve.wait_ge(down_done, m + 1)
                ns = STILES[r]
                v.tensor_copy(slot_w[0:st, 0:ns], chunk2(PS[0:st, YB, 2 * D:2 * D + 2 * ns], 2)[:, :, 0])\
                 .then_inc(slotw, 1)
                dve.wait_ge(slotw, EXPERTS * r + k + 1)
                weighted_outputs(r, out_high, EXPERTS * r + k + 1).then_inc(y_split, 1)

            def further_unit(r, q, k):
                i = q * EXPERTS + k
                x, cap, st, ns, width = further[r], CAP[r], ST[r], STILES[r], (UP, FF)[r]
                dve.wait_ge(x["scattered"], i + 1)
                dve.wait_ge(x["slots"], 2 * q + 4)
                e = bass.ds(k, 1)
                for t in range(NT):
                    v.tensor_scalar(gat[:, 0, t, 0:cap], slot_row_x[:, 0:cap], rank[:, t, e], None, ALU.is_equal)
                for n in range(ns):
                    v.tensor_scalar(sca[0:st, n, :], rank_all[0:st, e, :].rearrange("p e t -> p (e t)"),
                                    slot_col_x[0:st, n:n + 1], None, ALU.is_equal)
                v.tensor_copy(wcur[:, 0, :, 0:2], wtab[:, :, e, :].rearrange("p t e w -> p t (e w)").bitcast(F32))\
                 .then_inc(x["table"], 1)
                dve.wait_ge(x["high"], i + 1)
                v.tensor_tensor(w_rest[D1:D0, 0, 0:width], raw_rem[:, 0, 0:width],
                                w_rest[0:D1, 0, 0:width].bitcast(F32), ALU.subtract).then_inc(x["rest"], 1)
                for n in range(STEPS):
                    dve.wait_ge(x["activated"], STEPS * i + n + 1)
                    src = act_out[:, 0, 0:2 * cap]
                    if r == 0:
                        v.tensor_tensor(prod[:, 0:2 * cap], PS[:, UPB[0], 0:2 * cap], src,
                                        ALU.mult).then_inc(x["gated"], 1)
                        dve.wait_ge(x["gated"], STEPS * i + n + 1)
                        src = prod[:, 0:2 * cap]
                    hi_ = h_high[:, 0, 2 * n:2 * n + 2, 0:cap]
                    v.tensor_copy(hi_, chunk2(src, cap)).then_inc(x["hidden_high"], 1)
                    dve.wait_ge(x["hidden_high"], STEPS * i + n + 1)
                    v.tensor_tensor(h_lowp[:, 0, 2 * n:2 * n + 2, 0:cap], chunk2(src, cap), hi_.bitcast(F32),
                                    ALU.subtract).then_inc(x["hidden"], 1)
                    dve.wait_ge(x["hidden"], STEPS * i + n + 1)
                dve.wait_ge(x["down"], i + 1)
                v.tensor_copy(slot_w[0:st, 0:ns], chunk2(PS[0:st, YB, 2 * D:2 * D + 2 * ns], 2)[:, :, 0])\
                 .then_inc(x["weights"], 1)
                dve.wait_ge(x["weights"], i + 1)
                weighted_outputs(r, x["outputs_high"], i + 1).then_inc(x["outputs_split"], 1)

            def experts(r):
                for b in range(2):
                    expert(r, b, b, b == 0, False)
                with dve.Fori(1, EXPERTS // 2 - 1) as p:
                    for b in range(2):
                        expert(r, 2 * p + b, b, False, False)
                for b in range(2):
                    expert(r, EXPERTS - 2 + b, b, False, b == 1)
                dve.wait_ge(scattered, EXPERTS * (r + 1))

                def next_slots(q):
                    dve.wait_ge(further[r]["scattered"], q * EXPERTS + 1)
                    dve.wait_ge(further[r]["slots"], 2 * q + 2)
                    v.tensor_scalar(slot_row_x[:, :], slot_row_x[:, :], float(CAP[r]), None,
                                    ALU.add).then_inc(further[r]["slots"], 1)
                    v.tensor_scalar(slot_col_x[:, :], slot_col_x[:, :], float(CAP[r]), None,
                                    ALU.add).then_inc(further[r]["slots"], 1)

                v.tensor_copy(slot_row_x[:, :], slot_row[:, :]).then_inc(further[r]["slots"], 1)
                v.tensor_copy(slot_col_x[:, :], slot_col[:, r, :]).then_inc(further[r]["slots"], 1)
                further_rounds(dve, r, further_unit, next_slots)

            def count_rounds(r):
                further_n = -(-T // CAP[r]) - 1
                for q in range(further_n):
                    c.mark(v.tensor_scalar(over[:, q:q + 1], most[:, :], float(CAP[r] * (q + 1)), None, ALU.is_gt))
                c.settle()
                c.link(v.tensor_reduce(rounds_f[:, r:r + 1], over[:, 0:further_n], AXX, ALU.add))
                v.tensor_copy(rounds[:, r:r + 1], rounds_f[:, r:r + 1]).then_inc(rounds_ready, 1)

            for m in range(NB):
                dense(m, 0, False, 1.0)
            dve.wait_ge(down_done, NB)
            add_acc(1)
            layernorm(h, xn, 3)
            split_tokens()
            xt_out(1)
            router(0)
            for m in range(NB, M_ROUTED0):
                dense(m, m // NB, True, 0.5)
            gather_table(0, 0, 0)
            count_rounds(0)
            experts(0)
            dve.wait_ge(mixed, 1)
            add_acc(2)
            layernorm(h, xn, 4)
            split_tokens()
            dve.wait_ge(a1bn_in, 32)
            v.tensor_scalar(col_ve[:, :], col_raw[:, 4, :], LN_EPS, None, ALU.add)
            v.tensor_scalar(row_ve[:, :, :], row_raw[:, :, 4, :], LN_EPS, None, ALU.add).then_inc(bn_var, 1)
            xt_out(2)
            dve.wait_ge(a_hi, 1)
            v.tensor_tensor(a_rest[D1:D0, :], a_rraw[:, :], a_rest[0:D1, :].bitcast(F32),
                            ALU.subtract).then_inc(a_lor, 1)
            dve.wait_ge(bn_std, 1)
            for raw, sd, is_, inv, mi, shift in (
                    (lambda i: col_raw[:, i, :], col_std[:, :], col_is[:, :], col_inv[:, :], col_mi[:, :], col_shift[:, :]),
                    (lambda i: row_raw[:, :, i, :], row_std[:, :, :], row_is[:, :, :], row_inv[:, :, :],
                     row_mi[:, :, :], row_shift[:, :, :])):
                c.link(v.reciprocal(is_, sd))
                c.link(v.tensor_tensor(inv, raw(1), is_, ALU.mult))
                c.link(v.tensor_tensor(mi, raw(3), inv, ALU.mult))
                c.link(v.tensor_tensor(shift, raw(2), mi, ALU.subtract))
            for i in range(12):
                w, cc, half = i // 6, i // 2 % QK_CHUNKS, i % 2
                col = w * QK_CHUNKS + cc
                dve.wait_ge(qk_done, i + 1)
                if i >= 2:
                    dve.wait_ge(qk_spiked, i - 1)
                v.tensor_scalar(ymid[:, i % 2, :], PS[:, 3 + i % 4, 0:HX], col_raw[:, 0, col:col + 1],
                                col_inv[:, col:col + 1], ALU.add, ALU.mult).then_inc(qk_mid, 1)
                dve.wait_ge(qk_mid, i + 1)
                v.tensor_scalar(qk_spk[:, w, cc, half * HX:(half + 1) * HX], ymid[:, i % 2, :],
                                col_shift[:, col:col + 1], 2.0, ALU.add, ALU.is_ge).then_inc(qk_spiked, 1)

            def normalise(i):
                def row(a):
                    return a[:, i:i + 1, :]
                last = per_bank(lambda ts, a: v.tensor_tensor(
                    bt1[:, ts, :], a, row_raw[:, i, 0:1, :].to_broadcast([TT, ts.stop - ts.start, D]), ALU.add))
                c.link(last)
                c.link(v.tensor_tensor(bt2[:, :, :], bt1[:, :, :], over_tiles(row(row_inv)), ALU.mult))
                c.link(v.tensor_tensor(bt1[:, :, :], bt2[:, :, :], over_tiles(row(row_shift)), ALU.add))

            dve.wait_ge(v_done, 1)
            normalise(0)
            v.tensor_scalar(v_spk[:, :, :], bt1[:, :, :], 2.0, None, ALU.is_ge).then_inc(v_ready, 1)
            for t in range(NT):
                dve.wait_ge(s_done, t + 1)
                if t:
                    dve.wait_ge(xa_done, t)
                for j in range(4):
                    v.tensor_tensor(am1[:, j, :, :], chunk2(PS[0:TT, 3 + j, 0:QK_CHUNKS * TT], TT),
                                    bmask[:, :].unsqueeze(1).to_broadcast([TT, QK_CHUNKS, TT]),
                                    ALU.mult).then_inc(s_masked, 1)
            dve.wait_ge(xa_done, NT)
            for lo, hi, out_ in ((0, D0, lambda ts: xs[:, ts, 0, :]), (D0, D, lambda ts: xs[:, ts, 1, 0:D1]),
                                 (D0, D, lambda ts: xs[:, ts, 1, D1:D0])):
                last = per_bank(lambda ts, a: v.tensor_scalar(out_(ts), a[:, :, lo:hi], SCALE1, 1.0,
                                                              ALU.mult, ALU.is_ge))
            last.then_inc(xs_ready, 1)
            dve.wait_ge(o_done, 1)
            normalise(1)
            c.link(v.tensor_scalar(bt2[:, :, :], bt1[:, :, :], 2.0, None, ALU.is_ge))
            c.link(v.tensor_tensor(h[:, :, :], h[:, :, :], bt2[:, :, :], ALU.add))
            layernorm(h, xn, 5)
            split_tokens()
            xt_out(3)
            router(1)
            dve.wait_ge(comb_done, 1)
            v.tensor_copy(comb_t[:, 0:4 * TT], PS[0:EXPERTS + 1, YB, 0:4 * TT]).then_inc(comb_read, 1)
            dve.wait_ge(comb_done, 2)
            v.tensor_copy(comb_t[:, 4 * TT:TP], PS[0:EXPERTS + 1, YB, 0:TT]).then_inc(comb_read, 1)
            for m in range(M_COMMON, M_ROUTED1):
                dense(m, 11, False, 1.0)
            gather_table(1, 0, 0)
            count_rounds(1)
            dve.wait_ge(down_done, M_ROUTED1)
            for t in range(NT):
                last = v.scalar_tensor_tensor(out=h[:, t, :], in0=acc(t), scalar=c0[:, t:t + 1], in1=h[:, t, :],
                                              op0=ALU.mult, op1=ALU.add)
            last.then_inc(acc_read, 1)
            experts(1)
            dve.wait_ge(mixed, 2)
            last = per_bank(lambda ts, a: v.tensor_tensor(h[:, ts, :], h[:, ts, :], a, ALU.add))
            last.then_inc(y_out, 1)


_OUT = (T, D)


def _launch_arrays(i):
    f = {k: np.asarray(v) for k, v in i.items()}

    def split_rows(w):
        return w[..., :D0, :], w[..., D0:, :]

    def chunked(w):
        return w.reshape(-1, FC, 128, D).transpose(0, 2, 1, 3).reshape(-1, 128, GW)

    x = f["x"].reshape(IMAGES, GRID, PATCH, GRID, PATCH, CHANNELS).transpose(2, 4, 5, 0, 1, 3)
    patches = np.zeros((PATCH_DIM, NT * GROUP, TOKENS), np.float32)
    patches[:, :IMAGES, 1:] = x.reshape(PATCH_DIM, IMAGES, GRID * GRID)
    swi = np.concatenate([f["L0_ffn_shared_gate"], f["L0_ffn_routed_gate"]]), \
        np.concatenate([f["L0_ffn_shared_up"], f["L0_ffn_routed_up"]]), \
        np.concatenate([f["L0_ffn_shared_down"], f["L0_ffn_routed_down"]])
    up_main, up_rem = split_rows(np.concatenate([swi[0].transpose(0, 2, 1), swi[1].transpose(0, 2, 1)], axis=2))
    g1 = np.concatenate([f["L0_attn_W1"][None], f["L1_ffn_W1"]])
    g2 = np.concatenate([f["L0_attn_W2"][None], f["L1_ffn_W2"]])
    gb = np.concatenate([f["L0_attn_b1"][None], f["L1_ffn_b1"]]).reshape(-1, FC, 128).transpose(0, 2, 1)
    g_main, g_rem = split_rows(g1)
    wt = f["L1_attn_W"].transpose(0, 2, 1)
    qk = np.zeros((D, 2, HEADS, 32), np.float32)
    qk[..., :HD] = wt[:2].transpose(1, 0, 2).reshape(D, 2, HEADS, HD)
    a1 = np.concatenate([qk.reshape(D, -1), wt[2], wt[3]], axis=1)
    bn = np.stack([f["L1_attn_b"], f["L1_attn_bn_gamma"], f["L1_attn_bn_beta"], f["L1_attn_bn_mean"],
                   f["L1_attn_bn_var"]])
    col = np.zeros((5, 2, HEADS, 32), np.float32)
    col[..., :HD] = bn[:, :2].reshape(5, 2, HEADS, HD)
    router = np.zeros((D, 2, 10), np.float32)
    router[:, 0, :EXPERTS] = f["L0_ffn_gate_w"].T
    router[:, 1, :EXPERTS + 1] = f["L1_ffn_Ws"]
    router_b = np.zeros((10,), np.float32)
    router_b[:EXPERTS + 1] = f["L1_ffn_bs"]
    arrays = dict(
        patches=patches.reshape(KT, 128, TP).transpose(1, 0, 2),
        tok_w=f["L0_tok_W"].reshape(KT, 128, D).transpose(1, 0, 2),
        tok_b=f["L0_tok_b"].reshape(1, D),
        cls_pos=np.concatenate([f["cls_tok"].reshape(1, D), f["L0_tok_pos_emb"]]),
        proj_t=f["L0_attn_proj"].T,
        rows=np.stack([f["L0_attn_ln1_g"], f["L0_attn_ln1_b"], f["L0_attn_ln2_g"], f["L0_attn_ln2_b"],
                       f["L0_attn_b2"]]),
        router_w=router, router_b=router_b,
        sw_main=np.concatenate([up_main, chunked(swi[2].transpose(0, 2, 1))], axis=2), sw_rem=up_rem,
        ge_main=np.concatenate([g_main, chunked(g2), gb], axis=2), ge_rem=g_rem,
        a1_main=a1[:D0], a1_rem=a1[D0:],
        a1_col=col.reshape(5, 2 * QK_CHUNKS, 128).transpose(2, 0, 1),
        a1_row=bn[:, 2:].transpose(1, 0, 2),
        moe_b2=f["L1_ffn_b2"],
    )
    return {k: np.ascontiguousarray(a) for k, a in arrays.items()}


def kernel(**inputs):
    import concourse.bacc as bacc
    from concourse.bass_utils import run_bass_kernel_spmd

    nc = bacc.Bacc("TRN2", target_bir_lowering=False, num_devices=1)
    arrays = _launch_arrays(inputs)
    args = {k: nc.dram_tensor(f"in_{k}", a.shape, F32, kind="ExternalInput").ap() for k, a in arrays.items()}
    out = nc.dram_tensor("out", _OUT, F32, kind="ExternalOutput").ap()
    tower_kernel(nc, out=out, **args)
    r = run_bass_kernel_spmd(nc, [{f"in_{k}": a for k, a in arrays.items()}], core_ids=[0])
    return r.results[0]["out"].reshape(IMAGES, TOKENS, D)
```

```python
import numpy as np
import concourse.bass as bass
from concourse import mybir
from contextlib import ExitStack

F32 = mybir.dt.float32
F32R = mybir.dt.float32r
BF16 = mybir.dt.bfloat16
I32 = mybir.dt.int32
U32 = mybir.dt.uint32
ALU = mybir.AluOpType
ACT = mybir.ActivationFunctionType
AXX = mybir.AxisListType.X

IMAGES, GRID, PATCH, CHANNELS = 32, 4, 16, 3
TOKENS = GRID * GRID + 1
D, FF, HEADS, FEATURES = 192, 768, 12, 64
HD = D // HEADS
PATCH_DIM = PATCH * PATCH * CHANNELS
EXPERTS = 8
GROUP = 7
TT = GROUP * TOKENS
NT = -(-IMAGES // GROUP)
TP = NT * TT
TX = TP + 1
HX = TX // 2
T = IMAGES * TOKENS
D0, D1 = 128, D - 128
KT = PATCH_DIM // 128
FC = FF // 128
STEPS = FC // 2
BLK = 2 * TT
BLOCKS = [(0, BLK, 2), (BLK, T - BLK, 1)]
WIDE = T - BLK
NB = len(BLOCKS)
DENSE_STEPS = sum(FC // n for _, _, n in BLOCKS)
WARM = (22, 2, 11, 20, 11, 13, 13, 2, 5)
LN_EPS = 1e-5
FEATURE_EPS = 1e-4
UP, GW = 2 * FF, FC * D
MAIN_S, MAIN_G = UP + GW, FF + GW + FC
QK_CHUNKS = 3
A1 = 2 * QK_CHUNKS * 128 + 2 * D
V_COL = 2 * QK_CHUNKS * 128
SCALE1 = float(HD) ** -0.125
M_ROUTED0 = 3 * NB
M_COMMON = M_ROUTED0 + EXPERTS
M_ROUTED1 = M_COMMON + NB
RANK_STEPS = ((5, 7, 8), (3, 5, 6))
SPREAD0 = RANK_STEPS[0][1] + 2
SPREADS1 = [range(0)] + [range(i, min(i + 4, 2 * EXPERTS)) for i in range(0, 2 * EXPERTS, 4)] + [range(0)]
SW0 = DENSE_STEPS
G_ROUTED0 = 3 * DENSE_STEPS
G_COMMON = G_ROUTED0 + EXPERTS * STEPS
G_ROUTED1 = G_COMMON + DENSE_STEPS


def tiles_of(start, width):
    return [(start // TT + i, i * TT, min(TT, width - i * TT)) for i in range(-(-width // TT))]


def dense_plan(m):
    i = m if m < M_ROUTED0 else m - M_COMMON
    start, width, n = BLOCKS[i % NB]
    first = (i // NB) * DENSE_STEPS + sum(FC // b[2] for b in BLOCKS[:i % NB])
    return start, width, n, first + (0 if m < M_ROUTED0 else G_COMMON)


def tower_kernel(nc, patches, tok_w, tok_b, cls_pos, proj_t, rows, router_w, router_b, sw_main, sw_rem,
                 ge_main, ge_rem, a1_main, a1_rem, a1_col, a1_row, moe_b2, out, caps=(192, 128)):
    CAP = caps
    STILES = [-(-c // 128) for c in CAP]
    ST = [c // n for c, n in zip(CAP, STILES)]
    ctx = ExitStack()
    with ctx:
        def sem(name):
            return ctx.enter_context(nc.semaphore(name))

        SIZE = {F32: 4, F32R: 4, I32: 4, U32: 4, BF16: 2}
        place = [-(-nc.sbuf_base // 64) * 64]

        def sb(name, shape, dt=F32):
            offset = place[0]
            width = int(np.prod(shape[1:])) * SIZE[dt]
            place[0] = offset + -(-width // 32) * 32
            return nc.alloc_sbuf_tensor_at(name, shape, dt, offset=offset)

        h = sb("h", [TT, NT, D])
        x0 = sb("x0", [TT, NT, D])
        xn = sb("xn", [TT, NT, D])
        xtok = sb("xtok", [TT, NT, 4, 128], F32R)
        xt = sb("xt", [128, 4, TX], F32R)
        raw_main = sb("raw_main", [128, 2, MAIN_S])
        raw_rem = sb("raw_rem", [D1, 2, UP])
        w_high = sb("w_high", [128, 2, UP], F32R)
        w_low = sb("w_low", [128, 2, UP], F32R)
        w_rest = sb("w_rest", [128, 2, UP], F32R)
        d_high = sb("d_high", [128, 2, GW], F32R)
        d_low = sb("d_low", [128, 2, GW], F32R)
        bias1 = sb("bias1", [128, 2, FC])
        row_sb = sb("row_sb", [TT, 5, D])
        ident = sb("ident", [128, 128])
        ident_b = sb("ident_b", [128, 128], BF16)
        bmask = sb("bmask", [TT, TT])
        valid = sb("valid", [TT, NT])
        tri = sb("tri", [TT, TT], BF16)
        ones_b = sb("ones_b", [TT, TT], BF16)
        zeros_b = sb("zeros_b", [1, 512], BF16)
        slot_row = sb("slot_row", [TT, max(CAP)])
        slot_col = sb("slot_col", [128, 2, 2])
        expert_id = sb("expert_id", [TT, 10])
        stats = sb("stats", [TT, NT, 6])
        mv = sb("mv", [TT, NT, 2])
        veps = sb("veps", [TT, NT])
        std = sb("std", [TT, NT])
        rstd = sb("rstd", [TT, NT])
        rw_raw = sb("rw_raw", [128, 2, 10])
        rw_rraw = sb("rw_rraw", [D1, 2, 10])
        rw = sb("rw", [128, 2, 3, 10], F32R)
        rb = sb("rb", [TT, 10])
        logit = sb("logit", [TT, NT, 10])
        lmax = sb("lmax", [TT, NT])
        shifted = sb("shifted", [TT, NT, 10])
        lexp = sb("lexp", [TT, NT, 10])
        lsum = sb("lsum", [TT, NT])
        linv = sb("linv", [TT, NT])
        prob = sb("prob", [TT, NT, 10])
        top8 = sb("top8", [TT, NT, 8])
        idx8 = sb("idx8", [TT, NT, 8], U32)
        idxf = sb("idxf", [TT, NT, 8])
        pick1 = sb("pick1", [TT, NT, 10])
        pick2 = sb("pick2", [TT, NT, 10])
        topw = sb("topw", [TT, NT, 2])
        comb = sb("comb", [TT, NT, 10])
        maskf = sb("maskf", [TT, NT, EXPERTS])
        maskb = sb("maskb", [TT, NT, EXPERTS], BF16)
        farb = sb("farb", [TT, NT, EXPERTS], BF16)
        rank = sb("rank", [TT, NT, EXPERTS])
        wtab = sb("wtab", [TT, NT, EXPERTS, 2], F32R)
        wcur = sb("wcur", [TT, 2, NT, 32], F32R)
        w_row = sb("w_row", [32, max(CAP)], F32R)
        ones_f = sb("ones_f", [32, 2], F32R)
        slot_w = sb("slot_w", [128, 2])
        slot_row_x = sb("slot_row_x", [TT, max(CAP)])
        slot_col_x = sb("slot_col_x", [128, 2])
        most = sb("most", [TT, 1])
        over = sb("over", [TT, 8])
        rounds_f = sb("rounds_f", [TT, 2])
        rounds = sb("rounds", [TT, 2], I32)
        c0 = sb("c0", [TT, NT])
        c0p = sb("c0p", [TT, NT, 2])
        b2_sb = sb("b2_sb", [EXPERTS + 1, D])
        shared_base = place[0]

        bdiag = sb("bdiag", [128, 8 * FEATURES])
        patch_base = place[0]
        patch_sb = sb("patch_sb", [128, KT, TP])
        tokw_sb = sb("tokw_sb", [128, KT, D])
        patch_end = place[0]
        tokb_sb = sb("tokb_sb", [1, D])
        prow = sb("prow", [1, GROUP, TOKENS])
        clspos_sb = sb("clspos_sb", [TT, D])
        bdiag2 = sb("bdiag2", [128, 4 * FEATURES])
        bd_high = sb("bd_high", [128, 8 * FEATURES], F32R)
        bd_low = sb("bd_low", [128, 8 * FEATURES], F32R)
        bd2_high = sb("bd2_high", [128, 4 * FEATURES], F32R)
        bd2_low = sb("bd2_low", [128, 4 * FEATURES], F32R)
        negsel = sb("negsel", [128, HEADS, FEATURES], F32R)
        vaug = sb("vaug", [TT, NT, HEADS, 32])
        sq = sb("sq", [TT, NT, D])
        y_high = sb("y_high", [128, TX], F32R)
        y_low = sb("y_low", [128, TX], F32R)
        y_rest = sb("y_rest", [128, TX], F32R)
        md = sb("md", [TT, 2, NT, HEADS])
        mx_t = sb("mx_t", [HEADS, TP])
        dg_t = sb("dg_t", [HEADS, TP])
        stab = sb("stab", [HEADS, NT * GROUP])
        bsum = sb("bsum", [HEADS, 2, TP])
        bq = sb("bq", [128, TX], F32R)
        bk = sb("bk", [128, TX], F32R)
        qkf = sb("qkf", [128, 2, 2, TP])
        rden = sb("rden", [TT, NT, HEADS])
        top_a = place[0]
        place[0] = patch_base
        am = sb("am", [TT, 2, 2, NT, TT])
        ctx_t = sb("ctx_t", [128, HEADS // 4, TP])
        assert place[0] <= patch_end

        place[0] = shared_base
        xg = sb("xg", [128, 4, max(CAP)], F32R)
        act_out = sb("act_out", [128, 2, 2 * BLK])
        prod = sb("prod", [128, 2 * BLK])
        h_high = sb("h_high", [128, 2, FC, WIDE], F32R)
        h_lowp = sb("h_lowp", [128, 2, FC, WIDE], F32R)
        rank_all = sb("rank_all", [128, EXPERTS, TX])
        gat = sb("gat", [TT, 2, NT, max(CAP)], F32R)
        rank_t = sb("rank_t", [EXPERTS, TX], F32R)
        selector_base = place[0]
        sca = sb("sca", [128, 2, TX], F32R)
        outputs_base = place[0]
        y_h = sb("y_h", [128, 2, D], F32R)
        y_l = sb("y_l", [128, 2, D], F32R)
        top_b = place[0]
        place[0] = selector_base
        pick_row = sb("pick_row", [EXPERTS, EXPERTS, 128], F32R)
        assert place[0] <= outputs_base
        place[0] = outputs_base
        comb_t = sb("comb_t", [EXPERTS + 1, TP])
        assert place[0] <= top_b

        place[0] = shared_base
        a_raw = sb("a_raw", [128, A1])
        a_rraw = sb("a_rraw", [D1, A1])
        a_high = sb("a_high", [128, A1], F32R)
        a_low = sb("a_low", [128, A1], F32R)
        a_rest = sb("a_rest", [128, A1], F32R)
        col_raw = sb("col_raw", [128, 5, 2 * QK_CHUNKS])
        col_ve = sb("col_ve", [128, 2 * QK_CHUNKS])
        col_std = sb("col_std", [128, 2 * QK_CHUNKS])
        col_is = sb("col_is", [128, 2 * QK_CHUNKS])
        col_bi = sb("col_bi", [128, 2 * QK_CHUNKS])
        col_sum = sb("col_sum", [128, 2 * QK_CHUNKS])
        col_least = sb("col_least", [128, 2 * QK_CHUNKS])
        col_inv = sb("col_inv", [128, 2 * QK_CHUNKS])
        col_mi = sb("col_mi", [128, 2 * QK_CHUNKS])
        col_shift = sb("col_shift", [128, 2 * QK_CHUNKS])
        row_raw = sb("row_raw", [TT, 2, 5, D])
        row_ve = sb("row_ve", [TT, 2, D])
        row_std = sb("row_std", [TT, 2, D])
        row_is = sb("row_is", [TT, 2, D])
        row_bi = sb("row_bi", [TT, 2, D])
        row_sum = sb("row_sum", [TT, 2, D])
        row_least = sb("row_least", [TT, 2, D])
        row_inv = sb("row_inv", [TT, 2, D])
        row_mi = sb("row_mi", [TT, 2, D])
        row_shift = sb("row_shift", [TT, 2, D])
        qk_spk = sb("qk_spk", [128, 2, QK_CHUNKS, TX], BF16)
        bt1 = sb("bt1", [TT, NT, D])
        bt2 = sb("bt2", [TT, NT, D])
        v_spk = sb("v_spk", [TT, NT, D], BF16)
        am1 = sb("am1", [TT, 2, 4, QK_CHUNKS, TT], BF16)
        xs = sb("xs", [TT, NT, 2, 128])
        top_c = place[0]
        assert max(top_a, top_b, top_c) <= nc.sbuf_usable_end, (top_a, top_b, top_c, nc.sbuf_usable_end)

        PS = ctx.enter_context(nc.psum_tensor("PS", [128, 8, 512], F32))
        YB = 7
        CTX_BANKS = (3, 4, 5, 0, 1)
        GATE, UPB = (3, 5), (4, 6)

        def acc(t):
            return PS[0:TT, t // 2, (t % 2) * D:(t % 2 + 1) * D]

        def cols(t):
            return slice(t * TT, (t + 1) * TT)

        def buf_of(n):
            return n % 2

        def blocks_done(n):
            return NB * (n + 1) if n < 3 else M_ROUTED0 + n - 2 if n < 11 else M_ROUTED1 + max(n - 11, 0)

        def chunk2(ap, n):
            return ap.rearrange("p (c n) -> p c n", n=n)

        patch_in = [sem(f"patch_in{i}") for i in range(KT)]
        tok_in = sem("tok_in"); clspos_in = sem("clspos_in"); rows_in = sem("rows_in")
        proj_in = sem("proj_in"); proj_high = sem("proj_high"); proj_low = sem("proj_low"); router_in = sem("router_in"); b2_in = sem("b2_in")
        raw_in = [sem("raw_in0"), sem("raw_in1")]; a1_in = sem("a1_in"); a1bn_in = sem("a1bn_in")
        const = sem("const")
        vec = sem("vec"); pool_step = sem("pool_step")
        embedded = sem("embedded"); var_ready = sem("var_ready"); std_ready = sem("std_ready")
        y_ready = sem("y_ready"); vaug_ready = sem("vaug_ready"); yt_done = sem("yt_done"); yt_ready = sem("yt_ready")
        yt_high = sem("yt_high"); tail_done = sem("tail_done"); q_bias = sem("q_bias")
        u_done = sem("u_done"); u_max = sem("u_max"); diag_ready = sem("diag_ready"); mdt_done = sem("mdt_done")
        bias_ready = sem("bias_ready"); feat_done = sem("feat_done"); exp_done = sem("exp_done")
        eps_done = sem("eps_done"); a_done = sem("a_done"); mask_done = sem("mask_done"); av_done = sem("av_done")
        ctx_ready = sem("ctx_ready"); ctx_done = sem("ctx_done")
        tile_norm = sem("tile_norm"); tile_high = sem("tile_high"); tok_split = sem("tok_split"); xt_done = sem("xt_done"); xt_act = sem("xt_act"); xt_vec = sem("xt_vec")
        hi_up = sem("hi_up"); hi_rest = sem("hi_rest"); hi_dn = sem("hi_dn"); lo_up = sem("lo_up"); lo_dn = sem("lo_dn"); rem_lo = sem("rem_lo")
        gu_done = sem("gu_done"); act_done = sem("act_done"); up_read = sem("up_read"); high_done = sem("high_done")
        low_done = sem("low_done"); down_done = sem("down_done"); acc_read = sem("acc_read")
        rw_high = sem("rw_high"); rw_ready = sem("rw_ready")
        logit_done = sem("logit_done"); shift_ready = sem("shift_ready"); lexp_ready = sem("lexp_ready")
        mask_ready = sem("mask_ready"); rank_done = sem("rank_done"); rank_read = sem("rank_read")
        all_done = sem("all_done"); all_read = sem("all_read"); all_read_v = sem("all_read_v"); comb_done = sem("comb_done"); comb_read = sem("comb_read")
        gat_ready = sem("gat_ready"); pick_ready = sem("pick_ready"); gathered = sem("gathered"); xg_ready = sem("xg_ready")
        slotw = sem("slotw"); out_high = sem("out_high")
        y_split = sem("y_split"); sca_ready = sem("sca_ready"); scattered = sem("scattered")
        a_hi = sem("a_hi"); a_lo = sem("a_lo"); a_lor = sem("a_lor"); bn_var = sem("bn_var"); bn_std = sem("bn_std"); bn_inv = sem("bn_inv"); row_ready = sem("row_ready")
        qk_done = sem("qk_done"); qk_spiked = sem("qk_spiked")
        v_done = sem("v_done"); v_ready = sem("v_ready"); s_done = sem("s_done"); s_masked = sem("s_masked")
        xa_done = sem("xa_done"); xs_ready = sem("xs_ready"); xst_done = sem("xst_done"); xst_ready = sem("xst_ready")
        rounds_ready = sem("rounds_ready"); mixed = sem("mixed")
        further = [{n: sem(f"further{r}_{n}") for n in (
            "loaded", "high", "low", "rest", "slots", "table", "gathered", "tokens", "products", "activated",
            "gated", "hidden_high", "hidden", "down", "weights", "outputs_high", "outputs_split",
            "scattered")} for r in range(2)]
        o_done = sem("o_done"); y_out = sem("y_out"); stored = sem("stored")

        class Chain:
            def __init__(self, eng, steps):
                self.eng, self.steps, self.n = eng, steps, 0

            def mark(self, ins):
                ins.then_inc(self.steps, 1)
                self.n += 1

            def link(self, ins):
                self.mark(ins)
                self.eng.wait_ge(self.steps, self.n)

            def settle(self):
                self.eng.wait_ge(self.steps, self.n)

        def count_of_rounds(eng, r):
            eng.wait_ge(rounds_ready, r + 1)
            return eng.value_load(rounds[0:1, r:r + 1], min_val=0, max_val=-(-T // CAP[r]) - 1)

        def further_rounds(eng, r, n, unit, begin=None):
            with eng.If(n):
                with eng.Fori(0, n) as q:
                    if begin is not None:
                        begin(q)
                    with eng.Fori(0, EXPERTS) as k:
                        unit(r, q, k)

        block = ctx.enter_context(nc.Block())

        @block.sync
        def _(sp):
            sp.dma_start(tokw_sb[:, :, :], tok_w).then_inc(tok_in, 16)
            for kt in range(KT):
                sp.dma_start(patch_sb[:, kt, :], patches[:, kt, :]).then_inc(patch_in[kt], 16)

            def load(n, b, main, rem, width, rem_width):
                sp.dma_start(raw_main[:, b, 0:width], main).then_inc(raw_in[b], 16)
                sp.dma_start(raw_rem[:, b, 0:rem_width], rem).then_inc(raw_in[b], 16)

            def release(n):
                sp.wait_ge(lo_dn, n + 1)
                sp.wait_ge(rem_lo, n + 1)

            def one(a, i):
                return a[bass.ds(i, 1), :, :].rearrange("e p n -> p (e n)")

            load(0, 0, one(ge_main, 0), one(ge_rem, 0), MAIN_G, FF)
            load(1, 1, one(sw_main, 0), one(sw_rem, 0), MAIN_S, UP)
            release(0)
            load(2, 0, one(sw_main, 1), one(sw_rem, 1), MAIN_S, UP)
            with sp.Fori(0, EXPERTS // 2) as p:
                for b in range(2):
                    k = 2 * p + b
                    release(1 + k)
                    load(3 + k, 1 - b, one(sw_main, 2 + k), one(sw_rem, 2 + k), MAIN_S, UP)
            release(9)
            load(11, 1, one(ge_main, 1), one(ge_rem, 1), MAIN_G, FF)

            def further_load(r, q, k):
                i = q * EXPERTS + k
                x = further[r]
                main, rem, first, width = ((sw_main, sw_rem, 2, UP), (ge_main, ge_rem, 2, FF))[r]
                sp.wait_ge(x["scattered"], i + 1)
                cols_ = MAIN_S if r == 0 else MAIN_G
                sp.dma_start(raw_main[:, 0, 0:cols_], one(main, first + k)).then_inc(x["loaded"], 16)
                sp.dma_start(raw_rem[:, 0, 0:width], one(rem, first + k)).then_inc(x["loaded"], 16)

            sp.wait_ge(scattered, EXPERTS)
            further_rounds(sp, 0, count_of_rounds(sp, 0), further_load)
            sp.wait_ge(mixed, 1)
            sp.wait_ge(acc_read, 2)
            sp.dma_start(a_raw[:, :], a1_main).then_inc(a1_in, 16)
            sp.dma_start(a_rraw[:, :], a1_rem).then_inc(a1_in, 16)
            sp.dma_start(col_raw[:, :, :], a1_col).then_inc(a1bn_in, 16)
            sp.dma_start(row_raw[:, :, :, :].rearrange("p a b d -> p (a b d)"),
                         a1_row.rearrange("a b d -> (a b d)").partition_broadcast(TT)).then_inc(a1bn_in, 16)
            with sp.Fori(0, EXPERTS // 2) as p:
                for b in range(2):
                    k = 2 * p + b
                    release(10 + k)
                    load(12 + k, b, one(ge_main, 2 + k), one(ge_rem, 2 + k), MAIN_G, FF)
            sp.wait_ge(scattered, 2 * EXPERTS)
            further_rounds(sp, 1, count_of_rounds(sp, 1), further_load)
            sp.wait_ge(y_out, 1)
            sp.dma_start(out[0:4 * TT, :].rearrange("(t p) d -> p t d", p=TT), h[:, 0:4, :]).then_inc(stored, 16)
            sp.dma_start(out[4 * TT:T, :], h[0:T - 4 * TT, 4, :]).then_inc(stored, 16)
            sp.wait_ge(stored, 32)

        @block.gpsimd
        def _(pool):
            c = Chain(pool, pool_step)
            g = nc.gpsimd
            g.memset(bdiag[:, :], 0.0)
            c.mark(g.memset(bdiag2[:, :], 0.0))
            g.memset(ident[:, :], 0.0)
            g.memset(bmask[:, :], 1.0)
            g.memset(valid[:, :], 1.0)
            g.memset(ones_b[:, :], 1.0)
            g.memset(zeros_b[:, :], 0.0)
            g.memset(ones_f[:, :].bitcast(F32), 1.0)
            g.memset(wcur[:, :, :, :].bitcast(F32), 0.0)
            g.memset(prow[:, :, :], 1.0)
            g.memset(negsel[:, :, :].bitcast(F32), 0.0)
            g.memset(bq[:, :].bitcast(F32), 0.0)
            g.memset(bk[:, :].bitcast(F32), 0.0)
            for y in (y_high, y_low, y_rest):
                g.memset(y[:, TP:TX].bitcast(F32), 0.0)
            g.memset(xt[:, :, TP:TX].bitcast(F32), 0.0)
            c.link(g.memset(vaug[:, :, :, :], 0.0))
            g.memset(vaug[:, :, :, HD:HD + 1], 1.0)
            g.memset(prow[:, :, 0:1], 0.0)
            g.affine_select(out=ident[:, :], in_=ident[:, :], compare_op=ALU.not_equal, fill=1.0, base=0,
                            pattern=[[-1, 128]], channel_multiplier=1)
            same = bmask[:, :].rearrange("p (i n) -> p i n", n=TOKENS)
            c.mark(g.affine_select(out=negsel[:, :, :], in_=negsel[:, :, :].bitcast(F32), compare_op=ALU.not_equal,
                                   fill=-1.0, base=0, pattern=[[-1, HEADS], [0, FEATURES]], channel_multiplier=1))
            g.affine_select(out=tri[:, :], in_=ones_b[:, :], compare_op=ALU.is_ge, fill=0.0, base=-1,
                            pattern=[[1, TT]], channel_multiplier=-1)
            g.affine_select(out=valid[:, :], in_=valid[:, :], compare_op=ALU.is_ge, fill=0.0, base=T - 1,
                            pattern=[[-TT, NT]], channel_multiplier=-1)
            c.link(g.affine_select(out=same, in_=same, compare_op=ALU.is_ge, fill=0.0, base=0,
                                   pattern=[[-TOKENS, GROUP], [0, TOKENS]], channel_multiplier=1))
            g.affine_select(out=same, in_=same, compare_op=ALU.is_ge, fill=0.0, base=TOKENS - 1,
                            pattern=[[TOKENS, GROUP], [0, TOKENS]], channel_multiplier=-1)
            g.affine_select(out=negsel[:, :, :], in_=negsel[:, :, :].bitcast(F32), compare_op=ALU.not_equal,
                            fill=-1.0, base=-32, pattern=[[-1, HEADS], [0, FEATURES]], channel_multiplier=1)
            g.iota(slot_row[:, :], pattern=[[1, max(CAP)]], base=0, channel_multiplier=0,
                   allow_small_or_imprecise_dtypes=True)
            g.iota(expert_id[:, :], pattern=[[1, 10]], base=0, channel_multiplier=0,
                   allow_small_or_imprecise_dtypes=True)
            for r in range(2):
                g.iota(slot_col[:, r, :], pattern=[[ST[r], 2]], base=0, channel_multiplier=1,
                       allow_small_or_imprecise_dtypes=True)
            g.tensor_copy(ident_b[:, :], ident[:, :]).then_inc(const, 1)
            pool.wait_ge(proj_high, 1)
            g.tensor_tensor(bd_low[:, :], bdiag[:, :], bd_high[:, :].bitcast(F32), ALU.subtract)
            g.tensor_tensor(bd2_low[:, :], bdiag2[:, :], bd2_high[:, :].bitcast(F32),
                            ALU.subtract).then_inc(proj_low, 1)

            def low_parts(n, b, up_width):
                pool.wait_ge(hi_up, n + 1)
                g.tensor_tensor(w_low[:, b, 0:up_width], raw_main[:, b, 0:up_width],
                                w_high[:, b, 0:up_width].bitcast(F32), ALU.subtract).then_inc(lo_up, 1)
                pool.wait_ge(hi_dn, n + 1)
                g.tensor_tensor(d_low[:, b, :], raw_main[:, b, up_width:up_width + GW],
                                d_high[:, b, :].bitcast(F32), ALU.subtract).then_inc(lo_dn, 1)

            def make_selector(stage):
                pool.wait_ge(tok_split, NT * stage)
                c.link(g.memset(pick_row[:, :, :].bitcast(F32), 0.0))
                g.affine_select(out=pick_row[:, :, :], in_=pick_row[:, :, :].bitcast(F32),
                                compare_op=ALU.not_equal, fill=1.0, base=0,
                                pattern=[[-1, EXPERTS], [0, 128]], channel_multiplier=1).then_inc(pick_ready, 1)

            def further_low(r, q, k):
                i = q * EXPERTS + k
                x, width = further[r], (UP, FF)[r]
                pool.wait_ge(x["high"], i + 1)
                g.tensor_tensor(w_low[:, 0, 0:width], raw_main[:, 0, 0:width], w_high[:, 0, 0:width].bitcast(F32),
                                ALU.subtract)
                g.tensor_tensor(d_low[:, 0, :], raw_main[:, 0, width:width + GW], d_high[:, 0, :].bitcast(F32),
                                ALU.subtract).then_inc(x["low"], 1)

            low_parts(0, 0, FF)
            make_selector(1)
            low_parts(1, 1, UP)
            low_parts(2, 0, UP)
            with pool.Fori(0, EXPERTS // 2) as p:
                for b in range(2):
                    low_parts(3 + 2 * p + b, 1 - b, UP)
            low_parts(11, 1, FF)
            further_rounds(pool, 0, count_of_rounds(pool, 0), further_low)
            pool.wait_ge(a_hi, 1)
            g.tensor_tensor(a_low[:, 0:V_COL], a_raw[:, 0:V_COL], a_high[:, 0:V_COL].bitcast(F32),
                            ALU.subtract).then_inc(a_lo, 1)
            pool.wait_ge(bn_inv, 1)
            c.link(g.tensor_tensor(row_inv[:, :, :], row_raw[:, :, 1, :], row_is[:, :, :], ALU.mult))
            c.mark(g.tensor_tensor(row_mi[:, :, :], row_raw[:, :, 3, :], row_inv[:, :, :], ALU.mult))
            c.link(g.tensor_tensor(row_bi[:, :, :], row_raw[:, :, 0, :], row_inv[:, :, :], ALU.mult))
            c.link(g.tensor_tensor(row_shift[:, :, :], row_raw[:, :, 2, :], row_mi[:, :, :], ALU.subtract))
            c.link(g.tensor_tensor(row_sum[:, :, :], row_bi[:, :, :], row_shift[:, :, :], ALU.add))
            g.tensor_scalar(row_least[:, :, :], row_sum[:, :, :], -1.0, 2.0, ALU.mult, ALU.add).then_inc(row_ready, 1)
            make_selector(4)
            with pool.Fori(0, EXPERTS // 2) as p:
                for b in range(2):
                    low_parts(12 + 2 * p + b, b, FF)
            further_rounds(pool, 1, count_of_rounds(pool, 1), further_low)

        @block.tensor
        def _(pe):
            mm = nc.tensor.matmul

            def five(out_ap, w3, x4, start, stop):
                wh, wl, wr = w3
                xh, xhr, xl, xlr = x4
                pairs = [(wh, xh), (wh, xl), (wl, xh), (wr, xhr), (wr, xlr)]
                for i, (w, x) in enumerate(pairs):
                    last = mm(out_ap, w, x, start=start and i == 0, stop=stop and i == 4, skip_group_check=True)
                return last

            def transpose(out_ap, in_ap, parts=TT):
                return mm(out_ap, in_ap, ident[0:parts, 0:parts], start=True, stop=True, is_transpose=True,
                          skip_group_check=True)

            def keep_warm(groups, bank):
                with pe.Fori(0, groups):
                    for _i in range(8):
                        mm(PS[:, bank, 0:128], ident_b[:, :], ident_b[:, :], start=True, stop=True,
                           skip_group_check=True)

            pe.wait_ge(tok_in, 32)
            for kt in range(KT):
                pe.wait_ge(patch_in[kt], 16)
                for t in range(NT):
                    mm(PS[0:TT, 3 + t, 0:D], patch_sb[:, kt, cols(t)], tokw_sb[:, kt, :], start=kt == 0, stop=False)
            pe.wait_ge(const, 1)
            for t in range(NT):
                mm(PS[0:TT, 3 + t, 0:D], prow[0:1, :, :].rearrange("p a b -> p (a b)"), tokb_sb[0:1, :],
                   start=False, stop=True).then_inc(embedded, 1)
            keep_warm(WARM[0], 0)
            pe.wait_ge(y_ready, 1)
            for t in range(NT):
                transpose(PS[:, 3 + t, 0:TT], xn[:, t, 0:D0])
                transpose(PS[0:D1, 3 + t, 128:128 + TT], xn[:, t, D0:D]).then_inc(yt_done, 1)
            keep_warm(WARM[1], 0)
            pe.wait_ge(yt_ready, NT)
            pe.wait_ge(proj_low, 1)
            for t in range(NT):
                a, b = ((3, 4), (5, 6))[t % 2]
                if t >= 2:
                    pe.wait_ge(u_max, t - 1)
                for i, (y, w) in enumerate(((y_high, bd_high), (y_low, bd_high), (y_high, bd_low))):
                    mm(PS[0:TT, a, :], y[:, cols(t)], w[:, :], start=i == 0, stop=i == 2)
                mm(PS[0:TT, b, 0:256], y_rest[:, cols(t)], bd2_high[:, :], start=True, stop=False)
                mm(PS[0:TT, b, 0:256], y_rest[0:D1, cols(t)], bd2_low[0:D1, :], start=False,
                   stop=True).then_inc(u_done, 1)
            pe.wait_ge(u_max, NT)
            pe.wait_ge(diag_ready, 1)
            for t in range(NT):
                for w in range(2):
                    bank, at = ((7, 0)[w], t * TT) if t < 4 else (1, w * 128)
                    last = transpose(PS[0:HEADS, bank, at:at + TT], md[:, w, t, :])
            last.then_inc(mdt_done, 1)
            keep_warm(WARM[2], 2)
            pe.wait_ge(q_bias, 1)

            def features(c, between):
                for w, bias in ((0, bq), (1, bk)):
                    if c == 0 and w == 1:
                        pe.wait_ge(bias_ready, 1)
                    for half, (lo, hi) in enumerate(((0, HX), (HX, TX))):
                        i = 2 * w + half
                        n = 4 * c + i
                        if n >= 3:
                            pe.wait_ge(exp_done, n - 2)
                        o = PS[:, 3 + n % 3, 0:hi - lo]
                        at = slice(c % 4 * 128, (c % 4 + 1) * 128)
                        if c < 4:
                            mm(o, bd_high[:, at], y_high[:, lo:hi], start=True, stop=False)
                            mm(o, bd_high[:, at], y_low[:, lo:hi], start=False, stop=False)
                            mm(o, bd_low[:, at], y_high[:, lo:hi], start=False, stop=False)
                        else:
                            mm(o, bd2_high[:, at], y_rest[:, lo:hi], start=True, stop=False)
                            mm(o, bd2_low[0:D1, at], y_rest[0:D1, lo:hi], start=False, stop=False)
                        mm(o, negsel[:, 2 * c:2 * c + 2, :].rearrange("h a f -> h (a f)"), bias[:, lo:hi],
                           start=False, stop=True).then_inc(feat_done, 1)
                        between(i)

            def products(c):
                def product(j, t):
                    rows_ = slice(64 * j, 64 * j + 64)
                    bank, at = (j, t * TT) if t < 4 else (7, j * TT)
                    return mm(PS[0:TT, bank, at:at + TT], qkf[rows_, c % 2, 1, cols(t)],
                              qkf[rows_, c % 2, 0, cols(t)], start=True, stop=True)

                product(0, 4).then_inc(tail_done, 1)
                for t in range(4):
                    for j in range(2):
                        product(j, t)
                pe.wait_ge(tail_done, c + 1)
                product(1, 4).then_inc(a_done, 1)

            def with_values(c, part):
                if c < 0 or part < 0:
                    return
                if part == 0:
                    pe.wait_ge(mask_done, 3 * c + 3)
                    if c == 0:
                        pe.wait_ge(vaug_ready, 1)
                    elif c % 2 == 0:
                        pe.wait_ge(ctx_ready, c // 2)
                for t in range(2 * part, min(2 * part + 2, NT)):
                    for j in range(2):
                        bank, at, row = (2, t * TT, (2 * c + j) % 4 * 32) if t < 4 else (6, 0, (2 * c + j) % 4 * 32)
                        last = mm(PS[row:row + 32, bank, at:at + TT], vaug[:, t, 2 * c + j, :],
                                  am[:, c % 2, j, t, :], start=True, stop=True, skip_group_check=True)
                if part == 2:
                    last.then_inc(av_done, 1)

            features(0, lambda i: None)
            for c in range(HEADS // 2):
                pe.wait_ge(eps_done, 2 * c + 2)
                if c:
                    pe.wait_ge(mask_done, 3 * c)
                products(c)
                if c < HEADS // 2 - 1:
                    features(c + 1, lambda i: with_values(c - 1, i - 1))
                else:
                    for i in range(3):
                        with_values(c - 1, i)
            for i in range(3):
                with_values(HEADS // 2 - 1, i)
            pe.wait_ge(exp_done, 2 * HEADS)
            for t in range(NT):
                for g in range(HEADS // 4):
                    pe.wait_ge(ctx_ready, g + 1)
                    last = transpose(PS[0:TT, CTX_BANKS[t], g * 128:(g + 1) * 128], ctx_t[:, g, cols(t)], 128)
                last.then_inc(ctx_done, 1)

            def to_features(stage):
                for t in range(NT):
                    pe.wait_ge(tok_split, NT * stage + t + 1)
                    for j in range(4):
                        last = transpose(PS[:, 3 + t, j * TT:(j + 1) * TT], xtok[:, t, j, :].bitcast(F32))
                    last.then_inc(xt_done, 1)

            def await_xt(stage):
                pe.wait_ge(xt_act, 3 * (stage + 1))
                pe.wait_ge(xt_vec, 2 * (stage + 1))

            def clear_acc():
                for i in range(3):
                    mm(PS[0:TT, i, :], zeros_b[:, 0:TT], zeros_b[:, :], start=True, stop=True, skip_group_check=True)

            def w_slices(b, at):
                return [w[:, b, at:at + 128] for w in (w_high, w_low, w_rest)]

            def step(b, s, pair, x4, width, gated, done=gu_done, between=None, n=2):
                for bank, base in ((GATE[pair], 0), (UPB[pair], FF)) if gated else ((GATE[pair], 0),):
                    for i in range(n):
                        last = five(PS[:, bank, i * width:(i + 1) * width], w_slices(b, base + (n * s + i) * 128),
                                    x4, True, True)
                        if base + i == 0 and between is not None:
                            between()
                last.then_inc(done, 1)

            def down(out_ap, b, hb, at, n, start, first_step=None, chunks=1):
                for i in range(FC):
                    if first_step is not None and i % chunks == 0:
                        pe.wait_ge(low_done, first_step + i // chunks + 1)
                    for j, (hp, dp) in enumerate(((h_high, d_high), (h_high, d_low), (h_lowp, d_high))):
                        last = mm(out_ap, hp[:, hb, i, at:at + n], dp[:, b, i * D:(i + 1) * D],
                                  start=start and i == 0 and j == 0, stop=i == FC - 1 and j == 2,
                                  skip_group_check=True)
                return last

            def dense_down(m, n):
                pe.wait_ge(hi_dn, n + 1)
                pe.wait_ge(lo_dn, n + 1)
                start, width, chunks, first = dense_plan(m)
                for t, at, k in tiles_of(start, width):
                    last = down(acc(t)[0:k], buf_of(n), m % 2, at, k, False, first if at == 0 else None, chunks)
                last.then_inc(down_done, 1)

            def dense(m, n, gated, before, extra):
                start, width, chunks, first = dense_plan(m)
                x4 = [xt[:, j, start:start + width] for j in range(4)]
                for s in range(FC // chunks):
                    g = first + s
                    if s == 0:
                        pe.wait_ge(hi_up, n + 1)
                        pe.wait_ge(lo_up, n + 1)
                        pe.wait_ge(rem_lo, n + 1)
                    if g >= 2:
                        pe.wait_ge(act_done, g - 1)
                        if g - 1 > SW0:
                            pe.wait_ge(up_read, min(g - 1, G_COMMON) - SW0)
                    step(buf_of(n), s, g % 2, x4, width, gated, between=lambda: extra(g, 0), n=chunks)
                    if s == 0 and before is not None:
                        dense_down(*before)
                    extra(g, 1)

            def nothing(g, part):
                pass

            keep_warm(WARM[3], YB)
            to_features(0)
            clear_acc()
            await_xt(0)
            for m in range(NB):
                dense(m, 0, False, (m - 1, 0) if m else None, nothing)
            dense_down(NB - 1, 0)

            def router(r):
                pe.wait_ge(rw_ready, 1)
                for t in range(NT):
                    last = router_tile(r, t)
                last.then_inc(logit_done, 1)

            def router_tile(r, t):
                o = PS[0:TT, YB, t * 10:(t + 1) * 10]
                xh, xhr, xl, xlr = [xt[:, j, cols(t)] for j in range(4)]
                pairs = [(xh, 0), (xl, 0), (xh, 1), (xhr, 2), (xlr, 2)]
                for i, (x, w) in enumerate(pairs):
                    last = mm(o, x, rw[:, r, w, :], start=i == 0, stop=i == 4, skip_group_check=True)
                return last

            def ranks_by_expert(t, at):
                o = PS[0:EXPERTS, YB, at:at + TT]
                mm(o, farb[:, t, :], ident_b[0:TT, 0:TT], start=True, stop=False, skip_group_check=True)
                for i in range(t):
                    mm(o, maskb[:, i, :], ones_b[:, :], start=False, stop=False, skip_group_check=True)
                return mm(o, maskb[:, t, :], tri[:, :], start=False, stop=True, skip_group_check=True)

            def ranks_first(r):
                pe.wait_ge(mask_ready, r + 1)
                for t in range(4):
                    last = ranks_by_expert(t, t * TT)
                last.then_inc(rank_done, 1)

            def ranks_second(r):
                pe.wait_ge(rank_read, 2 * r + 1)
                ranks_by_expert(4, 0)
                for t in range(NT):
                    o = PS[0:TT, YB, 128 + t * EXPERTS:128 + (t + 1) * EXPERTS]
                    mm(o, ident_b[0:TT, 0:TT], farb[:, t, :], start=True, stop=False, skip_group_check=True)
                    for i in range(t):
                        mm(o, ones_b[:, :], maskb[:, i, :], start=False, stop=False, skip_group_check=True)
                    mm(o, tri[:, :], maskb[:, t, :], start=False, stop=True, skip_group_check=True)
                for t in range(NT):
                    last = mm(PS[0:TT, YB, 192:192 + EXPERTS], ones_b[:, :], maskb[:, t, :], start=t == 0,
                              stop=t == NT - 1, skip_group_check=True)
                last.then_inc(rank_done, 1)

            def spread(r, i):
                if i == 0:
                    pe.wait_ge(pick_ready, r + 1)
                    pe.wait_ge(rank_read, 2 * r + 2)
                elif r == 0:
                    pe.wait_ge(all_read, i)
                elif i >= 2 and i % 2 == 0:
                    pe.wait_ge(all_read, 2 * EXPERTS + i // 2)
                elif i >= 2:
                    pe.wait_ge(all_read_v, i // 2)
                e, half = i // 2, i % 2
                mm(PS[:, (YB, UPB[half])[r], 0:HX], pick_row[:, e, :], rank_t[:, half * HX:(half + 1) * HX],
                   start=True, stop=True).then_inc(all_done, 1)

            def extras0(g, part):
                g = g - SW0
                if (g, part) == (RANK_STEPS[0][0], 0):
                    ranks_first(0)
                if (g, part) == (RANK_STEPS[0][1], 0):
                    ranks_second(0)
                if SPREAD0 <= g < SPREAD0 + EXPERTS:
                    spread(0, 2 * (g - SPREAD0) + part)

            def weights_by_expert(i):
                if i:
                    pe.wait_ge(comb_read, 1)
                else:
                    pe.wait_ge(rank_read, 4)
                for t in range(4) if i == 0 else (4,):
                    last = transpose(PS[0:EXPERTS + 1, YB, (t % 4) * TT:(t % 4 + 1) * TT], comb[:, t, 0:EXPERTS + 1])
                last.then_inc(comb_done, 1)

            def extras1(g, part):
                g = g - G_COMMON
                if (g, part) == (RANK_STEPS[1][0], 0):
                    ranks_first(1)
                if (g, part) == (RANK_STEPS[1][1], 0):
                    ranks_second(1)
                if g in (6, 7) and part == 0:
                    weights_by_expert(g - 6)
                if g >= 6:
                    for i in SPREADS1[2 * (g - 6) + part]:
                        spread(1, i)

            def gather_tokens(r, b):
                cap, st = CAP[r], ST[r]
                for j in range(4):
                    bank, at = (GATE[1], UPB[1])[j // 2], (j % 2) * cap
                    for t in range(NT):
                        mm(PS[:, bank, at:at + cap], xtok[:, t, j, :], gat[:, b, t, 0:cap],
                           start=t == 0, stop=t == NT - 1, skip_group_check=True)
                for i in range(STILES[r]):
                    for t in range(NT):
                        last = mm(PS[0:32, (GATE[1], UPB[1])[i], 2 * cap:2 * cap + st], wcur[:, b, t, :],
                                  gat[:, b, t, i * st:(i + 1) * st], start=t == 0, stop=t == NT - 1,
                                  skip_group_check=True)
                return last

            def weight_columns(r):
                st = ST[r]
                for i in range(STILES[r]):
                    mm(PS[0:st, YB, 2 * D + 2 * i:2 * D + 2 * i + 2], w_row[:, i * st:(i + 1) * st], ones_f[:, :],
                       start=True, stop=True, skip_group_check=True)

            def gather(r, k, b, g):
                pe.wait_ge(gat_ready, EXPERTS * r + k + 1)
                pe.wait_ge(act_done, g)
                if r == 0:
                    pe.wait_ge(up_read, g - SW0)
                gather_tokens(r, b).then_inc(gathered, 1)

            def scatter(r, k, last_one=False):
                pe.wait_ge(y_split, EXPERTS * r + k + 1)
                pe.wait_ge(sca_ready, EXPERTS * r + k + 1)
                st = ST[r]
                for t in range(NT):
                    for i in range(STILES[r]):
                        for y in (y_h, y_l):
                            last = mm(acc(t), sca[0:st, i, cols(t)], y[0:st, i, :], start=False, stop=False,
                                      skip_group_check=True)
                last.then_inc(scattered, 1)

            def expert(r, k, b, first, final):
                n0, m0 = ((3, M_ROUTED0), (12, M_ROUTED1))[r]
                n, m = n0 + k, m0 + k
                g = (G_ROUTED0, G_ROUTED1)[r] + STEPS * k
                wb = (n0 + b) % 2
                cap, st, gated = CAP[r], ST[r], r == 0
                x4 = [xg[:, j, 0:cap] for j in range(4)]
                pe.wait_ge(hi_up, n + 1)
                pe.wait_ge(lo_up, n + 1)
                pe.wait_ge(rem_lo, n + 1)
                pe.wait_ge(xg_ready, EXPERTS * r + k + 1)
                pe.wait_ge(act_done, g)
                if gated:
                    pe.wait_ge(up_read, g - SW0)
                step(wb, 0, 0, x4, cap, gated)
                if not first:
                    scatter(r, k - 1)
                elif r:
                    pe.wait_ge(acc_read, 3)
                    pe.wait_ge(b2_in, 16)
                    clear_acc()
                    for t in range(NT):
                        mm(acc(t), comb_t[:, cols(t)], b2_sb[:, :], start=False, stop=False, skip_group_check=True)
                    keep_warm(WARM[8], YB)
                step(wb, 1, 1, x4, cap, gated)
                if not first:
                    pe.wait_ge(y_split, EXPERTS * r + k)
                elif r == 1:
                    pe.wait_ge(y_split, EXPERTS)
                weight_columns(r)
                pe.wait_ge(act_done, g + 1)
                if gated:
                    pe.wait_ge(up_read, g + 1 - SW0)
                step(wb, 2, 0, x4, cap, gated)
                if not final:
                    gather(r, k + 1, 1 - b, g + 2)
                pe.wait_ge(hi_dn, n + 1)
                pe.wait_ge(lo_dn, n + 1)
                for i in range(STILES[r]):
                    last = down(PS[0:st, YB, i * D:(i + 1) * D], wb, (m0 + b) % 2,
                                i * st, st, True, g if i == 0 else None, 2)
                last.then_inc(down_done, 1)

            def experts(r):
                n_rounds = count_of_rounds(pe, r)
                for b in range(2):
                    expert(r, b, b, b == 0, False)
                with pe.Fori(1, EXPERTS // 2 - 1) as p:
                    for b in range(2):
                        expert(r, 2 * p + b, b, False, False)
                for b in range(2):
                    expert(r, EXPERTS - 2 + b, b, False, b == 1)
                scatter(r, EXPERTS - 1)
                mm(acc(0), zeros_b[:, 0:TT], zeros_b[:, 0:D], start=False, stop=False,
                   skip_group_check=True).then_inc(further[r]["scattered"], 1)
                further_rounds(pe, r, n_rounds, further_unit)
                mm(acc(0), zeros_b[:, 0:TT], zeros_b[:, 0:D], start=False, stop=True,
                   skip_group_check=True).then_inc(mixed, 1)

            def further_unit(r, q, k):
                i = q * EXPERTS + k
                x, cap, st = further[r], CAP[r], ST[r]
                pe.wait_ge(x["table"], i + 1)
                gather_tokens(r, 0).then_inc(x["gathered"], 1)
                pe.wait_ge(x["tokens"], i + 1)
                pe.wait_ge(x["low"], i + 1)
                pe.wait_ge(x["rest"], i + 1)
                x4 = [xg[:, j, 0:cap] for j in range(4)]
                for s in range(STEPS):
                    step(0, s, 0, x4, cap, r == 0, x["products"])
                    pe.wait_ge(x["hidden"], STEPS * i + s + 1)
                weight_columns(r)
                for n in range(STILES[r]):
                    last = down(PS[0:st, YB, n * D:(n + 1) * D], 0, 0, n * st, st, True)
                last.then_inc(x["down"], 1)
                pe.wait_ge(x["outputs_split"], i + 1)
                for t in range(NT):
                    for n in range(STILES[r]):
                        for y in (y_h, y_l):
                            last = mm(acc(t), sca[0:st, n, cols(t)], y[0:st, n, :], start=False, stop=False,
                                      skip_group_check=True)
                last.then_inc(x["scattered"], 1)

            keep_warm(WARM[4], YB)
            to_features(1)
            pe.wait_ge(acc_read, 1)
            clear_acc()
            await_xt(1)
            router(0)
            for m in range(NB, M_ROUTED0):
                n = m // NB
                dense(m, n, True, (m - 1, (m - 1) // NB) if m > NB else None, extras0)
            gather(0, 0, 0, G_ROUTED0 - 1)
            dense_down(M_ROUTED0 - 1, 2)
            pe.wait_ge(all_read, 16)
            keep_warm(WARM[7], YB)
            experts(0)

            keep_warm(WARM[5], YB)
            to_features(2)
            await_xt(2)
            pe.wait_ge(a_lo, 1)
            pe.wait_ge(a_lor, 1)

            def a_slices(at, n):
                return [w[:, at:at + n] for w in (a_high, a_low, a_rest)]

            i = 0
            for w in range(2):
                for c in range(QK_CHUNKS):
                    for half in range(2):
                        if i >= 4:
                            pe.wait_ge(qk_spiked, i - 3)
                        five(PS[:, 3 + i % 4, 0:HX], a_slices((w * QK_CHUNKS + c) * 128, 128),
                             [xt[:, j, half * HX:(half + 1) * HX] for j in range(4)], True, True).then_inc(qk_done, 1)
                        i += 1
            pe.wait_ge(acc_read, 2)
            for t in range(NT):
                xh, xhr, xl, xlr = [xt[:, j, cols(t)] for j in range(4)]
                wh, wl, wr = a_slices(V_COL, D)
                for i, (x, w) in enumerate([(xh, wh), (xl, wh), (xh, wl), (xhr, wr), (xlr, wr)]):
                    last = mm(acc(t), x, w, start=i == 0, stop=i == 4, skip_group_check=True)
            last.then_inc(v_done, 1)
            def spike_products(t):
                for j in range(4):
                    if t:
                        pe.wait_ge(s_masked, 4 * (t - 1) + j + 1)
                    for c in range(QK_CHUNKS):
                        last = mm(PS[0:TT, 3 + j, c * TT:(c + 1) * TT], qk_spk[32 * j:32 * j + 32, 1, c, cols(t)],
                                  qk_spk[32 * j:32 * j + 32, 0, c, cols(t)], start=True, stop=True,
                                  skip_group_check=True)
                    last.then_inc(s_done, 1)

            pe.wait_ge(qk_spiked, 12)
            spike_products(0)
            for t in range(NT):
                if t < NT - 1:
                    spike_products(t + 1)
                if t == 0:
                    pe.wait_ge(v_ready, 1)
                pe.wait_ge(s_masked, 4 * t + 4)
                for head in range(HEADS):
                    last = mm(acc(t)[:, head * HD:(head + 1) * HD], am1[:, t % 2, head % 4, head // 4, :],
                              v_spk[:, t, head * HD:(head + 1) * HD], start=True, stop=True, skip_group_check=True)
                last.then_inc(xa_done, 1)
            pe.wait_ge(xs_ready, 1)
            for t in range(NT):
                for j in range(2):
                    last = transpose(PS[:, 3 + t, j * TT:(j + 1) * TT], xs[:, t, j, :])
                last.then_inc(xst_done, 1)
            pe.wait_ge(xst_ready, NT)
            for t in range(NT):
                wh, wl, wr = a_slices(V_COL + D, D)
                for i, (j, w) in enumerate([(0, wh), (0, wl), (1, wr)]):
                    last = mm(acc(t), xt[:, j, cols(t)], w, start=i == 0, stop=i == 2, skip_group_check=True)
            last.then_inc(o_done, 1)

            keep_warm(WARM[6], YB)
            to_features(3)
            clear_acc()
            await_xt(3)
            router(1)
            for m in range(M_COMMON, M_ROUTED1):
                dense(m, 11, False, (m - 1, 11) if m > M_COMMON else None, extras1)
            pe.wait_ge(all_read, 3 * EXPERTS)
            pe.wait_ge(all_read_v, EXPERTS)
            gather(1, 0, 0, G_ROUTED1)
            dense_down(M_ROUTED1 - 1, 11)
            pe.wait_ge(comb_read, 2)
            experts(1)

        @block.scalar
        def _(act):
            s = nc.scalar
            act.dma_start(tokb_sb[:, :], tok_b).then_inc(tok_in, 16)
            for i in range(GROUP):
                act.dma_start(clspos_sb[i * TOKENS:(i + 1) * TOKENS, :], cls_pos).then_inc(clspos_in, 16)
            act.dma_start(row_sb[:, :, :].rearrange("p a d -> p (a d)"),
                          rows.rearrange("a d -> (a d)").partition_broadcast(TT)).then_inc(rows_in, 16)
            act.wait_ge(pool_step, 1)
            for head in range(HEADS):
                tile_, i = (bdiag, head) if head < 8 else (bdiag2, head - 8)
                act.dma_start(tile_[i * HD:(i + 1) * HD, i * FEATURES:(i + 1) * FEATURES],
                              proj_t).then_inc(proj_in, 16)
            for i in range(HEADS - 8):
                act.dma_start(bdiag2[D1 + i * HD:D1 + (i + 1) * HD, i * FEATURES:(i + 1) * FEATURES],
                              proj_t).then_inc(proj_in, 16)
            act.dma_start(rw_raw[:, :, :], router_w[0:D0]).then_inc(router_in, 16)
            act.dma_start(rw_rraw[:, :, :], router_w[D0:D]).then_inc(router_in, 16)
            act.dma_start(rb[:, :], router_b.partition_broadcast(TT)).then_inc(router_in, 16)
            act.dma_start(b2_sb[:, :], moe_b2).then_inc(b2_in, 16)

            def deviation(i):
                act.wait_ge(var_ready, i + 1)
                s.activation(std[:, :], veps[:, :], ACT.Sqrt).then_inc(std_ready, 1)

            act.wait_ge(proj_in, 16 * (2 * HEADS - 8))
            s.activation(bd_high[:, :], bdiag[:, :], ACT.Copy)
            s.activation(bd2_high[:, :], bdiag2[:, :], ACT.Copy).then_inc(proj_high, 1)
            deviation(0)
            deviation(1)
            act.wait_ge(y_ready, 1)
            for t in range(NT):
                act.wait_ge(yt_done, t + 1)
                s.activation(y_high[:, cols(t)], PS[:, 3 + t, 0:TT], ACT.Copy)
                s.activation(y_rest[0:D1, cols(t)], PS[0:D1, 3 + t, 128:128 + TT], ACT.Copy).then_inc(yt_high, 1)
            act.wait_ge(const, 1)
            s.activation(vaug[:, :, :, 0:HD], xn[:, :, :].rearrange("p t (h d) -> p t h d", d=HD),
                         ACT.Copy).then_inc(vaug_ready, 1)
            act.wait_ge(router_in, 48)
            s.activation(rw[:, :, 0, :], rw_raw[:, :, :], ACT.Copy)
            s.activation(rw[0:D1, :, 2, :], rw_rraw[:, :, :], ACT.Copy).then_inc(rw_high, 1)

            def high_up(n, b, fill, width, done):
                act.wait_ge(raw_in[b], 32 * (fill + 1))
                if done is not None:
                    act.wait_ge(down_done, done)
                if width == FF:
                    s.activation(bias1[:, b, :], raw_main[:, b, FF + GW:MAIN_G], ACT.Copy)
                s.activation(w_high[:, b, 0:width], raw_main[:, b, 0:width], ACT.Copy).then_inc(hi_up, 1)

            def high_rest(b, width):
                s.activation(w_rest[0:D1, b, 0:width], raw_rem[:, b, 0:width], ACT.Copy).then_inc(hi_rest, 1)

            def high_down(b, width):
                s.activation(d_high[:, b, :], raw_main[:, b, width:width + GW], ACT.Copy).then_inc(hi_dn, 1)

            def high_half(n, at):
                b, width = (n + 1) % 2, UP if 1 <= n + 1 <= 10 else FF
                half = (at - 1) % 2
                at_up = slice(half * width // 2, (half + 1) * width // 2)
                at_dn = slice(half * GW // 2, (half + 1) * GW // 2)
                if at == 1:
                    act.wait_ge(raw_in[b], 32 * ((n + 1) // 2 + 1))
                    if n:
                        act.wait_ge(down_done, blocks_done(n - 1))
                    if width == FF:
                        s.activation(bias1[:, b, :], raw_main[:, b, FF + GW:MAIN_G], ACT.Copy)
                if at in (1, 2):
                    last, done = s.activation(w_high[:, b, at_up], raw_main[:, b, at_up], ACT.Copy), hi_up
                elif at in (3, 4):
                    last, done = s.activation(w_rest[0:D1, b, at_up], raw_rem[:, b, at_up], ACT.Copy), hi_rest
                else:
                    down_half = raw_main[:, b, width:width + GW][:, at_dn]
                    last, done = s.activation(d_high[:, b, at_dn], down_half, ACT.Copy), hi_dn
                if half:
                    last.then_inc(done, 1)

            high_up(0, 0, 0, FF, None)
            high_rest(0, FF)
            high_down(0, FF)

            def context(g):
                act.wait_ge(av_done, 2 * g + 2)
                s.activation(ctx_t[:, g, 0:4 * TT], PS[:, 2, 0:4 * TT], ACT.Copy)
                s.activation(ctx_t[:, g, 4 * TT:TP], PS[:, 6, 0:TT], ACT.Copy).then_inc(ctx_ready, 1)

            def exps(c):
                for w in range(2):
                    for half, (lo, hi) in enumerate(((0, HX), (HX, TP))):
                        i = 2 * w + half
                        act.wait_ge(feat_done, 4 * c + i + 1)
                        if c >= 2:
                            act.wait_ge(a_done, c - 1)
                        s.activation(qkf[:, c % 2, w, lo:hi], PS[:, 3 + (4 * c + i) % 3, 0:hi - lo], ACT.Exp,
                                     scale=0.5).then_inc(exp_done, 1)

            exps(0)
            for c in range(HEADS // 2):
                if c < HEADS // 2 - 1:
                    exps(c + 1)
                if c and c % 2 == 0:
                    context(c // 2 - 1)
            context(HEADS // 4 - 1)

            def high_tokens(stage):
                for t in range(NT):
                    act.wait_ge(tile_norm, NT * stage + t + 1)
                    s.activation(xtok[:, t, 0, :], xn[:, t, 0:D0], ACT.Copy)
                    s.activation(chunk2(xtok[:, t, 1, :], D1), xn[:, t:t + 1, D0:D].to_broadcast([TT, 2, D1]),
                                 ACT.Copy).then_inc(tile_high, 1)

            def xt_out(stage):
                for t in (0, 2, 4):
                    act.wait_ge(xt_done, NT * stage + t + 1)
                    s.activation(xt[:, :, cols(t)], chunk2(PS[:, 3 + t, 0:4 * TT], TT), ACT.Copy).then_inc(xt_act, 1)

            def hidden(g, n, b, c0_, chunks, pair, ring, width, gated):
                act.wait_ge(gu_done, g + 1)
                if not (isinstance(g, int) and g < 2):
                    act.wait_ge(low_done, g - 1)
                if gated:
                    s.activation(act_out[:, ring, 0:chunks * width], PS[:, GATE[pair], 0:chunks * width],
                                 ACT.Silu).then_inc(act_done, 1)
                    return
                act.wait_ge(hi_up, n + 1)
                for i in range(chunks):
                    at = slice(i * width, (i + 1) * width)
                    last = s.activation(act_out[:, ring, at], PS[:, GATE[pair], at], ACT.Gelu,
                                        bias=bias1[:, b, c0_ + i:c0_ + i + 1])
                last.then_inc(act_done, 1)

            def spread_out(r, i):
                act.wait_ge(all_done, 2 * EXPERTS * r + i + 1)
                e, half = i // 2, i % 2
                s.activation(rank_all[:, e, half * HX:(half + 1) * HX], PS[:, (YB, UPB[half])[r], 0:HX], ACT.Copy).then_inc(all_read, 1)

            def tokens_out(r):
                cap, st = CAP[r], ST[r]
                for i in range(STILES[r]):
                    s.activation(w_row[:, i * st:(i + 1) * st], PS[0:32, (GATE[1], UPB[1])[i], 2 * cap:2 * cap + st],
                                 ACT.Copy)
                s.activation(xg[:, 0:2, 0:cap], chunk2(PS[:, GATE[1], 0:2 * cap], cap), ACT.Copy)
                return s.activation(xg[:, 2:4, 0:cap], chunk2(PS[:, UPB[1], 0:2 * cap], cap), ACT.Copy)

            def gathered_out(r, k):
                act.wait_ge(gathered, EXPERTS * r + k + 1)
                tokens_out(r).then_inc(xg_ready, 1)

            def dense(m, n, gated, extra):
                _, width, chunks, first = dense_plan(m)
                for i in range(FC // chunks):
                    g = first + i
                    extra(g, 0)
                    hidden(g, n, n % 2, chunks * i, chunks, g % 2, g % 2, width, gated)
                    extra(g, 1)
                    at = g - (DENSE_STEPS * n if m < M_ROUTED0 else G_COMMON)
                    if 1 <= at <= 6:
                        high_half(n, at)

            def nothing(g, part):
                pass

            def extras0(g, part):
                g = g - SW0
                if SPREAD0 <= g < SPREAD0 + EXPERTS:
                    spread_out(0, 2 * (g - SPREAD0) + part)

            def extras1(g, part):
                g = g - G_COMMON
                if g >= 6:
                    for i in SPREADS1[2 * (g - 6) + part][::2]:
                        spread_out(1, i)

            def expert(r, k, p, b, final):
                n0, m0 = ((3, M_ROUTED0), (12, M_ROUTED1))[r]
                n, m = n0 + k, m0 + k
                wb, gated, cap = (n0 + b) % 2, r == 0, CAP[r]
                g0 = (G_ROUTED0, G_ROUTED1)[r]
                g, ring = g0 + STEPS * k, (g0 + b) % 2
                more = not final or r == 0
                width = UP if r == 0 and not final else FF
                nb = 1 - wb
                if more:
                    high_up(n + 1, nb, (n0 + 1 + b) // 2 + p, width, m)
                hidden(g, n, wb, 0, 2, 0, ring, cap, gated)
                if more:
                    high_rest(nb, width)
                hidden(g + 1, n, wb, 2, 2, 1, 1 - ring, cap, gated)
                if more:
                    high_down(nb, width)
                hidden(g + 2, n, wb, 4, 2, 0, ring, cap, gated)
                if not final:
                    gathered_out(r, k + 1)

            def experts(r):
                for b in range(2):
                    expert(r, b, 0, b, False)
                with act.Fori(1, EXPERTS // 2 - 1) as p:
                    for b in range(2):
                        expert(r, 2 * p + b, p, b, False)
                for b in range(2):
                    expert(r, EXPERTS - 2 + b, EXPERTS // 2 - 1, b, b == 1)
                further_rounds(act, r, count_of_rounds(act, r), further_unit)

            def further_unit(r, q, k):
                i = q * EXPERTS + k
                x, cap, width = further[r], CAP[r], (UP, FF)[r]
                act.wait_ge(x["loaded"], 32 * i + 32)
                s.activation(w_high[:, 0, 0:width], raw_main[:, 0, 0:width], ACT.Copy)
                if r:
                    s.activation(bias1[:, 0, :], raw_main[:, 0, FF + GW:MAIN_G], ACT.Copy)
                s.activation(w_rest[0:D1, 0, 0:width], raw_rem[:, 0, 0:width], ACT.Copy)
                s.activation(d_high[:, 0, :], raw_main[:, 0, width:width + GW], ACT.Copy).then_inc(x["high"], 1)
                act.wait_ge(x["high"], i + 1)
                act.wait_ge(x["gathered"], i + 1)
                tokens_out(r).then_inc(x["tokens"], 1)
                for n in range(STEPS):
                    act.wait_ge(x["products"], STEPS * i + n + 1)
                    for c in range(2):
                        at = slice(c * cap, (c + 1) * cap)
                        last = s.activation(act_out[:, 0, at], PS[:, GATE[0], at], ACT.Gelu,
                                            bias=bias1[:, 0, 2 * n + c:2 * n + c + 1]) if r else \
                            s.activation(act_out[:, 0, at], PS[:, GATE[0], at], ACT.Silu)
                    last.then_inc(x["activated"], 1)

            def router(r):
                act.wait_ge(shift_ready, r + 1)
                s.activation(lexp[:, :, :], shifted[:, :, :], ACT.Exp).then_inc(lexp_ready, 1)

            deviation(2)
            high_tokens(0)
            xt_out(0)
            for m in range(NB):
                dense(m, 0, False, nothing)
            deviation(3)
            high_tokens(1)
            xt_out(1)
            router(0)
            for m in range(NB, M_ROUTED0):
                dense(m, m // NB, True, extras0)
            gathered_out(0, 0)
            experts(0)
            deviation(4)
            high_tokens(2)
            act.wait_ge(a1_in, 32)
            s.activation(a_high[:, :], a_raw[:, :], ACT.Copy).then_inc(a_hi, 1)
            s.activation(a_rest[0:D1, :], a_rraw[:, :], ACT.Copy).then_inc(a_hi, 1)
            act.wait_ge(bn_var, 1)
            s.activation(col_std[:, :], col_ve[:, :], ACT.Sqrt)
            s.activation(row_std[:, :, :], row_ve[:, :, :], ACT.Sqrt).then_inc(bn_std, 1)
            xt_out(2)
            for t in range(NT):
                act.wait_ge(xst_done, t + 1)
                s.activation(xt[:, 0:2, cols(t)], chunk2(PS[:, 3 + t, 0:2 * TT], TT), ACT.Copy).then_inc(xst_ready, 1)
            deviation(5)
            high_tokens(3)
            xt_out(3)
            router(1)
            for m in range(M_COMMON, M_ROUTED1):
                dense(m, 11, False, extras1)
            gathered_out(1, 0)
            experts(1)

        @block.vector
        def _(dve):
            v = nc.vector
            c = Chain(dve, vec)

            def over_tiles(row):
                return row.to_broadcast([TT, NT, D])

            def row_factors(src, i):
                for t in range(NT):
                    c.mark(v.bn_stats(stats[:, t, :], src[:, t, :]))
                c.settle()
                for t in range(NT):
                    c.mark(v.bn_aggr(mv[:, t, :], stats[:, t, :]))
                c.settle()
                v.tensor_scalar(veps[:, :], mv[:, :, 1], LN_EPS, None, ALU.add).then_inc(var_ready, 1)
                dve.wait_ge(std_ready, i + 1)
                c.link(v.reciprocal(rstd[:, :], std[:, :]))

            def normalised(src, dst, t):
                return v.tensor_scalar(dst[:, t, :], src[:, t, :], mv[:, t, 0:1], rstd[:, t:t + 1],
                                       ALU.subtract, ALU.mult)

            def layernorm(src, dst, i):
                row_factors(src, i)
                for t in range(NT):
                    c.mark(normalised(src, dst, t))
                c.settle()

            def split_tokens(stage):
                for t in range(NT):
                    dve.wait_ge(tile_high, NT * stage + t + 1)
                    v.tensor_tensor(xtok[:, t, 2, :], xn[:, t, 0:D0], xtok[:, t, 0, :].bitcast(F32), ALU.subtract)
                    v.tensor_tensor(chunk2(xtok[:, t, 3, :], D1), xn[:, t:t + 1, D0:D].to_broadcast([TT, 2, D1]),
                                    chunk2(xtok[:, t, 1, :].bitcast(F32), D1), ALU.subtract).then_inc(tok_split, 1)

            def layer_input(src, i, stage):
                row_factors(src, i)
                for t in range(NT):
                    normalised(src, xn, t).then_inc(tile_norm, 1)
                split_tokens(stage)

            def xt_out(stage):
                for t in (1, 3):
                    dve.wait_ge(xt_done, NT * stage + t + 1)
                    v.tensor_copy(xt[:, :, cols(t)], chunk2(PS[:, 3 + t, 0:4 * TT], TT)).then_inc(xt_vec, 1)

            def per_bank(f):
                for bank in range(3):
                    ts = slice(2 * bank, min(2 * bank + 2, NT))
                    last = f(ts, chunk2(PS[0:TT, bank, 0:(ts.stop - ts.start) * D], D))
                return last

            dve.wait_ge(clspos_in, 16 * GROUP)
            for t in range(NT):
                dve.wait_ge(embedded, t + 1)
                c.mark(v.tensor_tensor(h[:, t, :], PS[0:TT, 3 + t, 0:D], clspos_sb[:, :], ALU.add))
            c.settle()
            layernorm(h, x0, 0)
            layernorm(x0, xn, 1)
            dve.wait_ge(rows_in, 16)
            c.link(v.tensor_tensor(xn[:, :, :], xn[:, :, :], over_tiles(row_sb[:, 0:1, :]), ALU.mult))
            v.tensor_tensor(xn[:, :, :], xn[:, :, :], over_tiles(row_sb[:, 1:2, :]), ALU.add).then_inc(y_ready, 1)
            dve.wait_ge(y_ready, 1)
            for t in range(NT):
                dve.wait_ge(yt_high, t + 1)
                v.tensor_tensor(y_low[:, cols(t)], PS[:, 3 + t, 0:TT], y_high[:, cols(t)].bitcast(F32), ALU.subtract)
                v.tensor_tensor(y_rest[D1:D0, cols(t)], PS[0:D1, 3 + t, 128:128 + TT],
                                y_rest[0:D1, cols(t)].bitcast(F32), ALU.subtract).then_inc(yt_ready, 1)
            c.link(v.tensor_tensor(sq[:, :, :], xn[:, :, :], xn[:, :, :], ALU.mult))
            c.link(v.tensor_reduce(md[:, 1, :, :], sq[:, :, :].rearrange("p t (h d) -> p t h d", d=HD), AXX, ALU.add))
            v.tensor_scalar(md[:, 1, :, :], md[:, 1, :, :], 0.25, None, ALU.mult).then_inc(diag_ready, 1)
            for t in range(NT):
                dve.wait_ge(u_done, t + 1)
                a, b = ((3, 4), (5, 6))[t % 2]
                v.tensor_reduce(md[:, 0, t, 0:8], chunk2(PS[0:TT, a, :], FEATURES), AXX, ALU.max)
                v.tensor_reduce(md[:, 0, t, 8:12], chunk2(PS[0:TT, b, 0:256], FEATURES), AXX, ALU.max).then_inc(u_max, 1)
            dve.wait_ge(mdt_done, 1)
            c.mark(v.tensor_copy(mx_t[:, 0:4 * TT], PS[0:HEADS, 7, 0:4 * TT]))
            c.mark(v.tensor_copy(mx_t[:, 4 * TT:TP], PS[0:HEADS, 1, 0:TT]))
            c.mark(v.tensor_copy(dg_t[:, 0:4 * TT], PS[0:HEADS, 0, 0:4 * TT]))
            c.mark(v.tensor_copy(dg_t[:, 4 * TT:TP], PS[0:HEADS, 1, 128:128 + TT]))
            c.settle()
            def split_bias(bias, w):
                c.link(v.tensor_copy(bias[0:HEADS, 0:TP], bsum[:, w, :]))
                return v.tensor_tensor(bias[32:32 + HEADS, 0:TP], bsum[:, w, :], bias[0:HEADS, 0:TP].bitcast(F32),
                                       ALU.subtract)

            c.link(v.tensor_tensor(bsum[:, 0, :], mx_t[:, :], dg_t[:, :], ALU.add))
            split_bias(bq, 0).then_inc(q_bias, 1)
            c.link(v.tensor_reduce(stab[:, :], chunk2(mx_t[:, :], TOKENS), AXX, ALU.max))
            c.link(v.tensor_tensor(chunk2(bsum[:, 1, :], TOKENS), chunk2(dg_t[:, :], TOKENS),
                                   stab[:, :].unsqueeze(2).to_broadcast([HEADS, NT * GROUP, TOKENS]), ALU.add))
            split_bias(bk, 1).then_inc(bias_ready, 1)
            dve.wait_ge(rw_high, 1)
            v.tensor_tensor(rw[:, :, 1, :], rw_raw[:, :, :], rw[:, :, 0, :].bitcast(F32), ALU.subtract)
            v.tensor_tensor(rw[D1:D0, :, 2, :], rw_rraw[:, :, :], rw[0:D1, :, 2, :].bitcast(F32),
                            ALU.subtract).then_inc(rw_ready, 1)

            def rem_low(n, b, width):
                dve.wait_ge(hi_rest, n + 1)
                v.tensor_tensor(w_rest[D1:D0, b, 0:width], raw_rem[:, b, 0:width],
                                w_rest[0:D1, b, 0:width].bitcast(F32), ALU.subtract).then_inc(rem_lo, 1)

            def rem_low_half(n, b, width, half):
                dve.wait_ge(hi_rest, n + 1)
                at = slice(half * width // 2, (half + 1) * width // 2)
                last = v.tensor_tensor(w_rest[D1:D0, b, at], raw_rem[:, b, at], w_rest[0:D1, b, at].bitcast(F32),
                                       ALU.subtract)
                if half:
                    last.then_inc(rem_lo, 1)

            rem_low(0, 0, FF)

            def add_eps(c_):
                for w in range(2):
                    dve.wait_ge(exp_done, 4 * c_ + 2 * w + 2)
                    f = qkf[:, c_ % 2, w, :]
                    v.tensor_scalar(f, f, FEATURE_EPS, None, ALU.add).then_inc(eps_done, 1)

            def masks(c_):
                dve.wait_ge(a_done, c_ + 1)
                if c_ >= 2:
                    dve.wait_ge(av_done, c_ - 1)
                for j in range(2):
                    v.tensor_tensor(am[:, c_ % 2, j, 0:4, :], chunk2(PS[0:TT, j, 0:4 * TT], TT),
                                    bmask[:, :].unsqueeze(1).to_broadcast([TT, 4, TT]),
                                    ALU.mult).then_inc(mask_done, 1)
                v.tensor_tensor(am[:, c_ % 2, :, 4, :], chunk2(PS[0:TT, 7, 0:2 * TT], TT),
                                bmask[:, :].unsqueeze(1).to_broadcast([TT, 2, TT]), ALU.mult).then_inc(mask_done, 1)

            add_eps(0)
            for c_ in range(HEADS // 2):
                masks(c_)
                if c_ < HEADS // 2 - 1:
                    add_eps(c_ + 1)
            def context(t):
                return chunk2(PS[0:TT, CTX_BANKS[t], 0:32 * HEADS], 32)

            for t in range(NT):
                dve.wait_ge(ctx_done, t + 1)
                c.mark(v.reciprocal(rden[:, t, :], context(t)[:, :, HD]))
            c.settle()
            for t in range(NT):
                c.mark(v.tensor_tensor(chunk2(xn[:, t, :], HD), context(t)[:, :, 0:HD],
                                       rden[:, t, :].unsqueeze(2).to_broadcast([TT, HEADS, HD]), ALU.mult))
            c.settle()
            c.link(v.tensor_tensor(x0[:, :, :], x0[:, :, :], xn[:, :, :], ALU.add))
            row_factors(x0, 2)
            for t in range(NT):
                c.link(normalised(x0, xn, t))
                c.link(v.tensor_tensor(xn[:, t, :], xn[:, t, :], row_sb[:, 2, :], ALU.mult))
                v.tensor_tensor(xn[:, t, :], xn[:, t, :], row_sb[:, 3, :], ALU.add).then_inc(tile_norm, 1)
            split_tokens(0)
            xt_out(0)
            c.link(v.tensor_tensor(x0[:, :, :], x0[:, :, :], over_tiles(row_sb[:, 4:5, :]), ALU.add))
            c.link(v.tensor_tensor(h[:, :, :], h[:, :, :], x0[:, :, :], ALU.add))

            def hidden(g, m, c0_, chunks, hb, ring, pair, width, gated, factor):
                if c0_ == 0 and not (isinstance(m, int) and m < 2):
                    dve.wait_ge(down_done, m - 1)
                dve.wait_ge(act_done, g + 1)
                src = act_out[:, ring, 0:chunks * width]
                if gated:
                    dve.wait_ge(low_done, g)
                    v.scalar_tensor_tensor(out=prod[:, 0:chunks * width], in0=PS[:, UPB[pair], 0:chunks * width],
                                           scalar=factor, in1=src, op0=ALU.mult, op1=ALU.mult).then_inc(up_read, 1)
                    dve.wait_ge(up_read, g + 1 - SW0)
                    src = prod[:, 0:chunks * width]
                hi_ = h_high[:, hb, c0_:c0_ + chunks, 0:width]
                v.tensor_copy(hi_, chunk2(src, width)).then_inc(high_done, 1)
                dve.wait_ge(high_done, g + 1)
                v.tensor_tensor(h_lowp[:, hb, c0_:c0_ + chunks, 0:width], chunk2(src, width), hi_.bitcast(F32),
                                ALU.subtract).then_inc(low_done, 1)

            def dense(m, n, gated, factor):
                _, width, chunks, first = dense_plan(m)
                for i in range(FC // chunks):
                    g = first + i
                    if n == 11 and g - G_COMMON >= 6:
                        spreads_out(g - G_COMMON, 0)
                    hidden(g, m, chunks * i, chunks, m % 2, g % 2, g % 2, width, gated, factor)
                    if n:
                        extras(*((0, g - SW0) if n < 3 else (1, g - G_COMMON)))
                    at = g - (DENSE_STEPS * n if m < M_ROUTED0 else G_COMMON)
                    for half in range(2):
                        if at == (5 + half if gated else DENSE_STEPS - 1):
                            rem_low_half(n + 1, (n + 1) % 2, UP if 1 <= n + 1 <= 10 else FF, half)

            def add_acc(which):
                last = per_bank(lambda ts, a: v.tensor_tensor(h[:, ts, :], h[:, ts, :], a, ALU.add))
                last.then_inc(acc_read, 1)
                dve.wait_ge(acc_read, which)

            def router_logits(r):
                e_ = slice(0, EXPERTS + r)
                dve.wait_ge(logit_done, r + 1)
                psum = chunk2(PS[0:TT, YB, 0:NT * 10], 10)
                if r:
                    c.link(v.tensor_tensor(logit[:, :, :], psum,
                                           rb[:, :].unsqueeze(1).to_broadcast([TT, NT, 10]), ALU.add))
                else:
                    c.link(v.tensor_copy(logit[:, :, :], psum))
                c.link(v.tensor_reduce(lmax[:, :], logit[:, :, e_], AXX, ALU.max))
                v.tensor_tensor(shifted[:, :, :], logit[:, :, :],
                                lmax[:, :].unsqueeze(2).to_broadcast([TT, NT, 10]), ALU.subtract).then_inc(shift_ready, 1)

            def router_choice(r):
                ne = EXPERTS + r
                e_ = slice(0, ne)
                dve.wait_ge(lexp_ready, r + 1)
                c.link(v.tensor_reduce(lsum[:, :], lexp[:, :, e_], AXX, ALU.add))
                c.link(v.reciprocal(linv[:, :], lsum[:, :]))
                c.link(v.tensor_tensor(prob[:, :, e_], lexp[:, :, e_],
                                       linv[:, :].unsqueeze(2).to_broadcast([TT, NT, ne]), ALU.mult))
                for t in range(NT):
                    c.mark(v.max(top8[:, t, :], prob[:, t, e_]))
                c.settle()
                for t in range(NT):
                    c.mark(v.max_index(idx8[:, t, :], top8[:, t, :], prob[:, t, e_]))
                c.settle()
                c.link(v.tensor_copy(idxf[:, :, :], idx8[:, :, :]))

            def router_weights(r):
                ne = EXPERTS + r
                e_ = slice(0, ne)

                def chosen(out_, i):
                    c.mark(v.tensor_tensor(out_[:, :, e_], expert_id[:, e_].unsqueeze(1).to_broadcast([TT, NT, ne]),
                                           idxf[:, :, i:i + 1].to_broadcast([TT, NT, ne]), ALU.is_equal))

                def weighted(out_, pick, w):
                    c.link(v.tensor_tensor(out_, pick, w.to_broadcast([TT, NT, pick.shape[2]]), ALU.mult))

                chosen(pick1, 0)
                if r == 0:
                    chosen(pick2, 1)
                    c.settle()
                    c.link(v.tensor_tensor(maskf[:, :, :], pick1[:, :, e_], pick2[:, :, e_], ALU.add))
                    c.link(v.tensor_tensor(lsum[:, :], top8[:, :, 0], top8[:, :, 1], ALU.add))
                    c.link(v.tensor_scalar(lsum[:, :], lsum[:, :], 1e-8, None, ALU.add))
                    c.link(v.reciprocal(linv[:, :], lsum[:, :]))
                    c.link(v.tensor_tensor(topw[:, :, :], top8[:, :, 0:2],
                                           linv[:, :].unsqueeze(2).to_broadcast([TT, NT, 2]), ALU.mult))
                    weighted(comb[:, :, e_], pick1[:, :, e_], topw[:, :, 0:1])
                    weighted(pick1[:, :, e_], pick2[:, :, e_], topw[:, :, 1:2])
                    c.link(v.tensor_tensor(comb[:, :, e_], comb[:, :, e_], pick1[:, :, e_], ALU.add))
                else:
                    c.settle()
                    c.link(v.tensor_copy(maskf[:, :, :], pick1[:, :, 1:ne]))
                    c.link(v.tensor_scalar(c0p[:, :, 0], top8[:, :, 0], -1.0, 1.0, ALU.mult, ALU.add))
                    c.link(v.tensor_tensor(c0p[:, :, 1], top8[:, :, 0], pick1[:, :, 0], ALU.mult))
                    c.link(v.tensor_tensor(c0[:, :], c0p[:, :, 0], c0p[:, :, 1], ALU.add))
                    weighted(comb[:, :, 1:ne], pick1[:, :, 1:ne], top8[:, :, 0:1])
                    c.link(v.tensor_copy(comb[:, :, 0], c0[:, :]))
                c.link(v.tensor_tensor(maskf[:, :, :], maskf[:, :, :],
                                       valid[:, :].unsqueeze(2).to_broadcast([TT, NT, EXPERTS]), ALU.mult))
                v.tensor_copy(maskb[:, :, :], maskf[:, :, :])
                v.tensor_scalar(farb[:, :, :], maskf[:, :, :], -1024.0, 1024.0, ALU.mult, ALU.add).then_inc(mask_ready, 1)
                w = comb[:, :, ne - EXPERTS:ne]
                c.link(v.tensor_copy(wtab[:, :, :, 0], w))
                c.link(v.tensor_tensor(wtab[:, :, :, 1], w, wtab[:, :, :, 0].bitcast(F32), ALU.subtract))
                c.link(v.memset(rank_t[:, TP:TX].bitcast(F32), 0.0))

            def ranks_out_first(r):
                dve.wait_ge(rank_done, 2 * r + 1)
                v.tensor_copy(rank_t[:, 0:4 * TT], PS[0:EXPERTS, YB, 0:4 * TT]).then_inc(rank_read, 1)

            def ranks_out_second(r):
                dve.wait_ge(rank_done, 2 * r + 2)
                c.mark(v.tensor_copy(rank_t[:, 4 * TT:TP], PS[0:EXPERTS, YB, 0:TT]))
                c.mark(v.tensor_reduce(most[:, :], PS[0:TT, YB, 192:192 + EXPERTS], AXX, ALU.max))
                v.tensor_copy(rank[:, :, :], chunk2(PS[0:TT, YB, 128:128 + NT * EXPERTS], EXPERTS)).then_inc(rank_read, 1)
                dve.wait_ge(rank_read, 2 * r + 2)

            def spreads_out(g, part):
                for i in SPREADS1[2 * (g - 6) + part][1::2]:
                    dve.wait_ge(all_done, 2 * EXPERTS + i + 1)
                    v.tensor_copy(rank_all[:, i // 2, HX:TX], PS[:, UPB[1], 0:HX]).then_inc(all_read_v, 1)

            def extras(r, g):
                if g == 0:
                    router_choice(r)
                if g == 1:
                    router_weights(r)
                if g == RANK_STEPS[r][0]:
                    ranks_out_first(r)
                if g == RANK_STEPS[r][1]:
                    ranks_out_second(r)
                if r == 1 and g == 6:
                    dve.wait_ge(comb_done, 1)
                    v.tensor_copy(comb_t[:, 0:4 * TT], PS[0:EXPERTS + 1, YB, 0:4 * TT]).then_inc(comb_read, 1)
                if r == 1 and g == 7:
                    dve.wait_ge(comb_done, 2)
                    v.tensor_copy(comb_t[:, 4 * TT:TP], PS[0:EXPERTS + 1, YB, 0:TT]).then_inc(comb_read, 1)
                if r == 1 and g >= 6:
                    spreads_out(g, 1)
                if g == RANK_STEPS[r][2]:
                    gather_table(r, 0, 0)
                    count_rounds(r)

            def gather_table(r, k, b):
                cap = CAP[r]
                e = slice(k, k + 1) if isinstance(k, int) else bass.ds(k, 1)
                for t in range(NT):
                    v.tensor_scalar(gat[:, b, t, 0:cap], slot_row[:, 0:cap], rank[:, t, e], None, ALU.is_equal)
                v.tensor_copy(wcur[:, b, :, 0:2], wtab[:, :, e, :].rearrange("p t e w -> p t (e w)").bitcast(F32))\
                 .then_inc(gat_ready, 1)

            def weighted_outputs(r, high, count):
                st = ST[r]
                for i in range(STILES[r]):
                    last = v.tensor_scalar(y_h[0:st, i, :], PS[0:st, YB, i * D:(i + 1) * D], slot_w[0:st, i:i + 1],
                                           None, ALU.mult)
                last.then_inc(high, 1)
                dve.wait_ge(high, count)
                for i in range(STILES[r]):
                    last = v.scalar_tensor_tensor(out=y_l[0:st, i, :], in0=PS[0:st, YB, i * D:(i + 1) * D],
                                                  scalar=slot_w[0:st, i:i + 1], in1=y_h[0:st, i, :].bitcast(F32),
                                                  op0=ALU.mult, op1=ALU.subtract)
                return last

            def expert(r, k, b, first, final):
                n0, m0 = ((3, M_ROUTED0), (12, M_ROUTED1))[r]
                n, m = n0 + k, m0 + k
                cap, st, gated, wb = CAP[r], ST[r], r == 0, (n0 + b) % 2
                g0 = (G_ROUTED0, G_ROUTED1)[r]
                g, ring, hb = g0 + STEPS * k, (g0 + b) % 2, (m0 + b) % 2
                e = slice(k, k + 1) if isinstance(k, int) else bass.ds(k, 1)
                hidden(g, m, 0, 2, hb, ring, 0, cap, gated, 1.0)
                if not final:
                    dve.wait_ge(down_done, m)
                    gather_table(r, k + 1, 1 - b)
                hidden(g + 1, m, 2, 2, hb, 1 - ring, 1, cap, gated, 1.0)
                if first:
                    dve.wait_ge(all_read, 2 * EXPERTS + r * EXPERTS)
                    if r:
                        dve.wait_ge(all_read_v, EXPERTS)
                if not first or r == 1:
                    dve.wait_ge(scattered, EXPERTS * r + k)
                for i in range(STILES[r]):
                    last = v.tensor_scalar(sca[0:st, i, :], rank_all[0:st, e, :].rearrange("p e t -> p (e t)"),
                                           slot_col[0:st, r, i:i + 1], None, ALU.is_equal)
                last.then_inc(sca_ready, 1)
                hidden(g + 2, m, 4, 2, hb, ring, 0, cap, gated, 1.0)
                if not final or r == 0:
                    rem_low(n + 1, 1 - wb, UP if r == 0 and not final else FF)
                dve.wait_ge(down_done, m + 1)
                ns = STILES[r]
                v.tensor_copy(slot_w[0:st, 0:ns], chunk2(PS[0:st, YB, 2 * D:2 * D + 2 * ns], 2)[:, :, 0])\
                 .then_inc(slotw, 1)
                dve.wait_ge(slotw, EXPERTS * r + k + 1)
                weighted_outputs(r, out_high, EXPERTS * r + k + 1).then_inc(y_split, 1)

            def further_unit(r, q, k):
                i = q * EXPERTS + k
                x, cap, st, ns, width = further[r], CAP[r], ST[r], STILES[r], (UP, FF)[r]
                dve.wait_ge(x["scattered"], i + 1)
                dve.wait_ge(x["slots"], 2 * q + 4)
                e = bass.ds(k, 1)
                for t in range(NT):
                    v.tensor_scalar(gat[:, 0, t, 0:cap], slot_row_x[:, 0:cap], rank[:, t, e], None, ALU.is_equal)
                for n in range(ns):
                    v.tensor_scalar(sca[0:st, n, :], rank_all[0:st, e, :].rearrange("p e t -> p (e t)"),
                                    slot_col_x[0:st, n:n + 1], None, ALU.is_equal)
                v.tensor_copy(wcur[:, 0, :, 0:2], wtab[:, :, e, :].rearrange("p t e w -> p t (e w)").bitcast(F32))\
                 .then_inc(x["table"], 1)
                dve.wait_ge(x["high"], i + 1)
                v.tensor_tensor(w_rest[D1:D0, 0, 0:width], raw_rem[:, 0, 0:width],
                                w_rest[0:D1, 0, 0:width].bitcast(F32), ALU.subtract).then_inc(x["rest"], 1)
                for n in range(STEPS):
                    dve.wait_ge(x["activated"], STEPS * i + n + 1)
                    src = act_out[:, 0, 0:2 * cap]
                    if r == 0:
                        v.tensor_tensor(prod[:, 0:2 * cap], PS[:, UPB[0], 0:2 * cap], src,
                                        ALU.mult).then_inc(x["gated"], 1)
                        dve.wait_ge(x["gated"], STEPS * i + n + 1)
                        src = prod[:, 0:2 * cap]
                    hi_ = h_high[:, 0, 2 * n:2 * n + 2, 0:cap]
                    v.tensor_copy(hi_, chunk2(src, cap)).then_inc(x["hidden_high"], 1)
                    dve.wait_ge(x["hidden_high"], STEPS * i + n + 1)
                    v.tensor_tensor(h_lowp[:, 0, 2 * n:2 * n + 2, 0:cap], chunk2(src, cap), hi_.bitcast(F32),
                                    ALU.subtract).then_inc(x["hidden"], 1)
                    dve.wait_ge(x["hidden"], STEPS * i + n + 1)
                dve.wait_ge(x["down"], i + 1)
                v.tensor_copy(slot_w[0:st, 0:ns], chunk2(PS[0:st, YB, 2 * D:2 * D + 2 * ns], 2)[:, :, 0])\
                 .then_inc(x["weights"], 1)
                dve.wait_ge(x["weights"], i + 1)
                weighted_outputs(r, x["outputs_high"], i + 1).then_inc(x["outputs_split"], 1)

            def experts(r):
                n_rounds = count_of_rounds(dve, r)
                for b in range(2):
                    expert(r, b, b, b == 0, False)
                with dve.Fori(1, EXPERTS // 2 - 1) as p:
                    for b in range(2):
                        expert(r, 2 * p + b, b, False, False)
                for b in range(2):
                    expert(r, EXPERTS - 2 + b, b, False, b == 1)
                dve.wait_ge(scattered, EXPERTS * (r + 1))

                def next_slots(q):
                    dve.wait_ge(further[r]["scattered"], q * EXPERTS + 1)
                    dve.wait_ge(further[r]["slots"], 2 * q + 2)
                    v.tensor_scalar(slot_row_x[:, :], slot_row_x[:, :], float(CAP[r]), None,
                                    ALU.add).then_inc(further[r]["slots"], 1)
                    v.tensor_scalar(slot_col_x[:, :], slot_col_x[:, :], float(CAP[r]), None,
                                    ALU.add).then_inc(further[r]["slots"], 1)

                v.tensor_copy(slot_row_x[:, :], slot_row[:, :]).then_inc(further[r]["slots"], 1)
                v.tensor_copy(slot_col_x[:, :], slot_col[:, r, :]).then_inc(further[r]["slots"], 1)
                further_rounds(dve, r, n_rounds, further_unit, next_slots)

            def count_rounds(r):
                further_n = -(-T // CAP[r]) - 1
                for q in range(further_n):
                    c.mark(v.tensor_scalar(over[:, q:q + 1], most[:, :], float(CAP[r] * (q + 1)), None, ALU.is_gt))
                c.settle()
                c.link(v.tensor_reduce(rounds_f[:, r:r + 1], over[:, 0:further_n], AXX, ALU.add))
                v.tensor_copy(rounds[:, r:r + 1], rounds_f[:, r:r + 1]).then_inc(rounds_ready, 1)

            for m in range(NB):
                dense(m, 0, False, 1.0)
            dve.wait_ge(down_done, NB - 1)
            c.mark(v.tensor_tensor(h[:, 0:2, :], h[:, 0:2, :], chunk2(PS[0:TT, 0, 0:2 * D], D), ALU.add))
            dve.wait_ge(down_done, NB)
            c.mark(v.tensor_tensor(h[:, 2:4, :], h[:, 2:4, :], chunk2(PS[0:TT, 1, 0:2 * D], D), ALU.add))
            v.tensor_tensor(h[:, 4, :], h[:, 4, :], PS[0:TT, 2, 0:D], ALU.add).then_inc(acc_read, 1)
            c.settle()
            dve.wait_ge(acc_read, 1)
            layer_input(h, 3, 1)
            xt_out(1)
            router_logits(0)
            for m in range(NB, M_ROUTED0):
                dense(m, m // NB, True, 0.5)
            experts(0)
            dve.wait_ge(mixed, 1)
            add_acc(2)
            layer_input(h, 4, 2)
            dve.wait_ge(a1bn_in, 32)
            v.tensor_scalar(col_ve[:, :], col_raw[:, 4, :], LN_EPS, None, ALU.add)
            v.tensor_scalar(row_ve[:, :, :], row_raw[:, :, 4, :], LN_EPS, None, ALU.add).then_inc(bn_var, 1)
            xt_out(2)
            dve.wait_ge(a_hi, 2)
            v.tensor_tensor(a_low[:, V_COL:A1], a_raw[:, V_COL:A1], a_high[:, V_COL:A1].bitcast(F32), ALU.subtract)
            v.tensor_tensor(a_rest[D1:D0, :], a_rraw[:, :], a_rest[0:D1, :].bitcast(F32),
                            ALU.subtract).then_inc(a_lor, 1)
            dve.wait_ge(bn_std, 1)
            c.link(v.reciprocal(col_is[:, :], col_std[:, :]))
            c.link(v.tensor_tensor(col_inv[:, :], col_raw[:, 1, :], col_is[:, :], ALU.mult))
            c.mark(v.tensor_tensor(col_mi[:, :], col_raw[:, 3, :], col_inv[:, :], ALU.mult))
            c.link(v.tensor_tensor(col_bi[:, :], col_raw[:, 0, :], col_inv[:, :], ALU.mult))
            c.link(v.tensor_tensor(col_shift[:, :], col_raw[:, 2, :], col_mi[:, :], ALU.subtract))
            c.link(v.tensor_tensor(col_sum[:, :], col_bi[:, :], col_shift[:, :], ALU.add))
            c.link(v.tensor_scalar(col_least[:, :], col_sum[:, :], -1.0, 2.0, ALU.mult, ALU.add))
            v.reciprocal(row_is[:, :, :], row_std[:, :, :]).then_inc(bn_inv, 1)
            for i in range(12):
                w, cc, half = i // 6, i // 2 % QK_CHUNKS, i % 2
                col = w * QK_CHUNKS + cc
                dve.wait_ge(qk_done, i + 1)
                v.tensor_scalar(qk_spk[:, w, cc, half * HX:(half + 1) * HX], PS[:, 3 + i % 4, 0:HX],
                                col_inv[:, col:col + 1], col_least[:, col:col + 1], ALU.mult,
                                ALU.is_ge).then_inc(qk_spiked, 1)

            def spikes(i, out_):
                def row(a, ts):
                    return a[:, i:i + 1, :].to_broadcast([TT, ts.stop - ts.start, D])
                c.link(per_bank(lambda ts, a: v.tensor_tensor(bt1[:, ts, :], a, row(row_inv, ts), ALU.mult)))
                return v.tensor_tensor(out_, bt1[:, :, :], row(row_least, slice(0, NT)), ALU.is_ge)

            def mask_products(t):
                for j in range(4):
                    dve.wait_ge(s_done, 4 * t + j + 1)
                    if t >= 2 and j == 0:
                        dve.wait_ge(xa_done, t - 1)
                    v.tensor_tensor(am1[:, t % 2, j, :, :], chunk2(PS[0:TT, 3 + j, 0:QK_CHUNKS * TT], TT),
                                    bmask[:, :].unsqueeze(1).to_broadcast([TT, QK_CHUNKS, TT]),
                                    ALU.mult).then_inc(s_masked, 1)

            mask_products(0)
            dve.wait_ge(row_ready, 1)
            dve.wait_ge(v_done, 1)
            spikes(0, v_spk[:, :, :]).then_inc(v_ready, 1)
            for t in range(1, NT):
                mask_products(t)
            dve.wait_ge(xa_done, NT)
            for lo, hi, out_ in ((0, D0, lambda ts: xs[:, ts, 0, :]), (D0, D, lambda ts: xs[:, ts, 1, 0:D1]),
                                 (D0, D, lambda ts: xs[:, ts, 1, D1:D0])):
                last = per_bank(lambda ts, a: v.tensor_scalar(out_(ts), a[:, :, lo:hi], SCALE1, 1.0,
                                                              ALU.mult, ALU.is_ge))
            last.then_inc(xs_ready, 1)
            dve.wait_ge(o_done, 1)
            c.link(spikes(1, bt2[:, :, :]))
            c.link(v.tensor_tensor(h[:, :, :], h[:, :, :], bt2[:, :, :], ALU.add))
            layer_input(h, 5, 3)
            xt_out(3)
            router_logits(1)
            for m in range(M_COMMON, M_ROUTED1):
                dense(m, 11, False, 1.0)
            dve.wait_ge(down_done, M_ROUTED1)
            for t in range(NT):
                last = v.scalar_tensor_tensor(out=h[:, t, :], in0=acc(t), scalar=c0[:, t:t + 1], in1=h[:, t, :],
                                              op0=ALU.mult, op1=ALU.add)
            last.then_inc(acc_read, 1)
            experts(1)
            dve.wait_ge(mixed, 2)
            last = per_bank(lambda ts, a: v.tensor_tensor(h[:, ts, :], h[:, ts, :], a, ALU.add))
            last.then_inc(y_out, 1)


_OUT = (T, D)


def _launch_arrays(i):
    f = {k: np.asarray(v) for k, v in i.items()}

    def split_rows(w):
        return w[..., :D0, :], w[..., D0:, :]

    def chunked(w):
        return w.reshape(-1, FC, 128, D).transpose(0, 2, 1, 3).reshape(-1, 128, GW)

    x = f["x"].reshape(IMAGES, GRID, PATCH, GRID, PATCH, CHANNELS).transpose(2, 4, 5, 0, 1, 3)
    patches = np.zeros((PATCH_DIM, NT * GROUP, TOKENS), np.float32)
    patches[:, :IMAGES, 1:] = x.reshape(PATCH_DIM, IMAGES, GRID * GRID)
    swi = np.concatenate([f["L0_ffn_shared_gate"], f["L0_ffn_routed_gate"]]), \
        np.concatenate([f["L0_ffn_shared_up"], f["L0_ffn_routed_up"]]), \
        np.concatenate([f["L0_ffn_shared_down"], f["L0_ffn_routed_down"]])
    up_main, up_rem = split_rows(np.concatenate([swi[0].transpose(0, 2, 1), swi[1].transpose(0, 2, 1)], axis=2))
    g1 = np.concatenate([f["L0_attn_W1"][None], f["L1_ffn_W1"]])
    g2 = np.concatenate([f["L0_attn_W2"][None], f["L1_ffn_W2"]])
    gb = np.concatenate([f["L0_attn_b1"][None], f["L1_ffn_b1"]]).reshape(-1, FC, 128).transpose(0, 2, 1)
    g_main, g_rem = split_rows(g1)
    wt = f["L1_attn_W"].transpose(0, 2, 1)
    qk = np.zeros((D, 2, HEADS, 32), np.float32)
    qk[..., :HD] = wt[:2].transpose(1, 0, 2).reshape(D, 2, HEADS, HD)
    a1 = np.concatenate([qk.reshape(D, -1), wt[2], wt[3]], axis=1)
    bn = np.stack([f["L1_attn_b"], f["L1_attn_bn_gamma"], f["L1_attn_bn_beta"], f["L1_attn_bn_mean"],
                   f["L1_attn_bn_var"]])
    col = np.zeros((5, 2, HEADS, 32), np.float32)
    col[..., :HD] = bn[:, :2].reshape(5, 2, HEADS, HD)
    router = np.zeros((D, 2, 10), np.float32)
    router[:, 0, :EXPERTS] = f["L0_ffn_gate_w"].T
    router[:, 1, :EXPERTS + 1] = f["L1_ffn_Ws"]
    router_b = np.zeros((10,), np.float32)
    router_b[:EXPERTS + 1] = f["L1_ffn_bs"]
    arrays = dict(
        patches=patches.reshape(KT, 128, TP).transpose(1, 0, 2),
        tok_w=f["L0_tok_W"].reshape(KT, 128, D).transpose(1, 0, 2),
        tok_b=f["L0_tok_b"].reshape(1, D),
        cls_pos=np.concatenate([f["cls_tok"].reshape(1, D), f["L0_tok_pos_emb"]]),
        proj_t=f["L0_attn_proj"].T,
        rows=np.stack([f["L0_attn_ln1_g"], f["L0_attn_ln1_b"], f["L0_attn_ln2_g"], f["L0_attn_ln2_b"],
                       f["L0_attn_b2"]]),
        router_w=router, router_b=router_b,
        sw_main=np.concatenate([up_main, chunked(swi[2].transpose(0, 2, 1))], axis=2), sw_rem=up_rem,
        ge_main=np.concatenate([g_main, chunked(g2), gb], axis=2), ge_rem=g_rem,
        a1_main=a1[:D0], a1_rem=a1[D0:],
        a1_col=col.reshape(5, 2 * QK_CHUNKS, 128).transpose(2, 0, 1),
        a1_row=bn[:, 2:].transpose(1, 0, 2),
        moe_b2=f["L1_ffn_b2"],
    )
    return {k: np.ascontiguousarray(a) for k, a in arrays.items()}


def kernel(**inputs):
    import concourse.bacc as bacc
    from concourse.bass_utils import run_bass_kernel_spmd

    nc = bacc.Bacc("TRN2", target_bir_lowering=False, num_devices=1)
    arrays = _launch_arrays(inputs)
    args = {k: nc.dram_tensor(f"in_{k}", a.shape, F32, kind="ExternalInput").ap() for k, a in arrays.items()}
    out = nc.dram_tensor("out", _OUT, F32, kind="ExternalOutput").ap()
    tower_kernel(nc, out=out, **args)
    r = run_bass_kernel_spmd(nc, [{f"in_{k}": a for k, a in arrays.items()}], core_ids=[0])
    return r.results[0]["out"].reshape(IMAGES, TOKENS, D)
```
